# Optimizing a Trainium2 kernel written in Bass

```python
import numpy as np
import jax
import jax.numpy as jnp

def _softmax(x, axis=-1):
    return jax.nn.softmax(x, axis=axis)

def _gelu(x):
    return jax.nn.gelu(x, approximate=True)

def _silu(x):
    return jax.nn.silu(x)

def _sigmoid(x):
    return jax.nn.sigmoid(x)

def _layernorm(x, axis=-1, eps=1e-05):
    m = jnp.mean(x, axis=axis, keepdims=True)
    v = jnp.var(x, axis=axis, keepdims=True)
    return (x - m) / jnp.sqrt(v + eps)

def _scatter_add(tgt, idx, src, axis=0):
    return tgt.at[idx].add(src)

def _segment_sum(src, seg, n):
    return jax.ops.segment_sum(src, seg, n)
kernel_name = 'mk_decoder_preln_d4_seqx_r4_4da3e0'

def setup_inputs(seed: int=0):
    np.random.seed(seed)
    _w = jnp.asarray

    def _rec_inputs():
        import jax
        import jax.numpy as jnp
        _rk = jax.random.key(seed)
        x = -0.0004039 + 1 * jax.random.normal(jax.random.fold_in(_rk, 1), (8, 256, 256), jnp.float32)
        _lenS = 256 - jax.random.randint(jax.random.fold_in(_rk, 7), (8,), 0, max(1, 256 // 4) + 1, jnp.int32)
        _lenS2 = 256 - jax.random.randint(jax.random.fold_in(_rk, 8), (8,), 0, max(1, 256 // 4) + 1, jnp.int32)
        _ctx_768P = jax.random.normal(jax.random.fold_in(_rk, 11), (8, 16, 192), jnp.float32)
        _ctx_768c = jax.random.dirichlet(jax.random.fold_in(_rk, 511), 0.3 * jnp.ones((16,), jnp.float32), (8, 256))
        _ctx_768t = jnp.einsum('bsk,bkd->bsd', _ctx_768c, _ctx_768P)
        _ctx_768t = _ctx_768t * jax.lax.rsqrt(jnp.mean(jnp.square(_ctx_768t)) + 1e-12) * 0.953939
        ctx_768 = -7.55891e-05 + 1.00004 * (_ctx_768t + 0.3 * jax.random.normal(jax.random.fold_in(_rk, 611), (8, 256, 192), jnp.float32))
        return (x, ctx_768)
    x, ctx_768 = _rec_inputs()

    def _L0_attn_setup():
        import jax, jax.numpy as jnp
        import numpy as np
        D_MODEL = 256
        N_HEADS = 16
        N_GROUPS = 4
        CONTEXT_LEN = 128
        D_H = D_MODEL // N_HEADS
        GROUP_SIZE = N_HEADS // N_GROUPS
        B, S = (4, 512)
        key = jax.random.key(seed)
        ks = jax.random.split(key, 9)
        s = 0.02
        return {'x': jax.random.normal(ks[0], (B, S, D_MODEL), dtype=jnp.float32), 'Wq': jax.random.normal(ks[1], (D_MODEL, D_MODEL), dtype=jnp.float32) * s, 'bq': jax.random.normal(ks[2], (D_MODEL,), dtype=jnp.float32) * s, 'Wk': jax.random.normal(ks[3], (D_MODEL, N_GROUPS * D_H), dtype=jnp.float32) * s, 'bk': jax.random.normal(ks[4], (N_GROUPS * D_H,), dtype=jnp.float32) * s, 'Wv': jax.random.normal(ks[5], (D_MODEL, N_GROUPS * D_H), dtype=jnp.float32) * s, 'bv': jax.random.normal(ks[6], (N_GROUPS * D_H,), dtype=jnp.float32) * s, 'Wo': jax.random.normal(ks[7], (D_MODEL, D_MODEL), dtype=jnp.float32) * s, 'bo': jax.random.normal(ks[8], (D_MODEL,), dtype=jnp.float32) * s}
    _L0_attn_all = _L0_attn_setup()
    _L0_attn_in = {k: v for k, v in _L0_attn_all.items() if k in ('Wq', 'bq', 'Wk', 'bk', 'Wv', 'bv', 'Wo', 'bo')}
    del _L0_attn_all

    def _L0_xattn_setup():
        import jax, jax.numpy as jnp
        import numpy as np
        import math
        N_HEADS = 8
        D_EMBED = 256
        D_CROSS = 192
        D_HEAD = D_EMBED // N_HEADS
        key = jax.random.key(seed)
        ks = jax.random.split(key, 10)
        B, S, SKV = (4, 768, 259)
        s_e = 1.0 / math.sqrt(D_EMBED)
        s_c = 1.0 / math.sqrt(D_CROSS)
        return {'x': jax.random.normal(ks[0], (B, S, D_EMBED), jnp.float32), 'y': jax.random.normal(ks[1], (B, SKV, D_CROSS), jnp.float32), 'Wq': jax.random.normal(ks[2], (D_EMBED, D_EMBED), jnp.float32) * s_e, 'bq': jnp.zeros((D_EMBED,), jnp.float32), 'Wk': jax.random.normal(ks[3], (D_EMBED, D_CROSS), jnp.float32) * s_c, 'bk': jnp.zeros((D_EMBED,), jnp.float32), 'Wv': jax.random.normal(ks[4], (D_EMBED, D_CROSS), jnp.float32) * s_c, 'bv': jnp.zeros((D_EMBED,), jnp.float32), 'Wo': jax.random.normal(ks[5], (D_EMBED, D_EMBED), jnp.float32) * s_e, 'bo': jnp.zeros((D_EMBED,), jnp.float32)}
    _L0_xattn_all = _L0_xattn_setup()
    _L0_xattn_in = {k: v for k, v in _L0_xattn_all.items() if k in ('Wq', 'bq', 'Wk', 'bk', 'Wv', 'bv', 'Wo', 'bo')}
    del _L0_xattn_all

    def _L0_ffn_setup():
        import jax, jax.numpy as jnp
        import numpy as np
        DIM = 256

        def _reference_tuple_inner(x, W_r, W_k, W_v, mu_r, mu_k):
            B, T, C = x.shape
            x_prev = jnp.concatenate([jnp.zeros((B, 1, C), x.dtype), x[:, :-1, :]], axis=1)
            xr = mu_r * x + (1.0 - mu_r) * x_prev
            xk = mu_k * x + (1.0 - mu_k) * x_prev
            r = jax.nn.sigmoid(jnp.einsum('btc,dc->btd', xr, W_r))
            k = jnp.einsum('btc,dc->btd', xk, W_k)
            k_act = jnp.square(jax.nn.relu(k))
            out = r * jnp.einsum('btc,dc->btd', k_act, W_v)
            new_state = x[:, -1, :]
            return (out, new_state)
        key = jax.random.key(seed)
        ks = jax.random.split(key, 6)
        B, T, C = (8, 512, DIM)
        x = jax.random.normal(ks[0], (B, T, C), dtype=jnp.float32)
        s = 1.0 / np.sqrt(C)
        W_r = jax.random.uniform(ks[1], (C, C), jnp.float32, -s, s)
        W_k = jax.random.uniform(ks[2], (C, C), jnp.float32, -s, s)
        W_v = jax.random.uniform(ks[3], (C, C), jnp.float32, -s, s)
        mu_r = jax.random.uniform(ks[4], (C,), jnp.float32)
        mu_k = jax.random.uniform(ks[5], (C,), jnp.float32)
        return {'x': x, 'W_r': W_r, 'W_k': W_k, 'W_v': W_v, 'mu_r': mu_r, 'mu_k': mu_k}
    _L0_ffn_all = _L0_ffn_setup()
    _L0_ffn_in = {k: v for k, v in _L0_ffn_all.items() if k in ('W_r', 'W_k', 'W_v', 'mu_r', 'mu_k')}
    del _L0_ffn_all

    def _L1_attn_setup():
        import jax, jax.numpy as jnp
        import numpy as np
        DIM = 256
        NUM_HEADS = 16
        HEAD_DIM = DIM // NUM_HEADS
        EPS_NORM = 1e-12
        EPS_LN = 1e-05
        key = jax.random.key(seed)
        ks = jax.random.split(key, 6)
        x = jax.random.normal(ks[0], (4, 512, DIM), dtype=jnp.float32)
        ln_w = jnp.ones((DIM,), jnp.float32)
        ln_b = jnp.zeros((DIM,), jnp.float32)
        limit = float(np.sqrt(6.0 / (DIM + 3 * DIM)))
        qkv_w = jax.random.uniform(ks[1], (3 * DIM, DIM), jnp.float32, -limit, limit)
        qkv_b = jnp.zeros((3 * DIM,), jnp.float32)
        out_w = 0.02 * jax.random.normal(ks[2], (DIM, DIM), dtype=jnp.float32)
        out_b = jnp.zeros((DIM,), jnp.float32)
        return {'x': x, 'ln_w': ln_w, 'ln_b': ln_b, 'qkv_w': qkv_w, 'qkv_b': qkv_b, 'out_w': out_w, 'out_b': out_b}
    _L1_attn_all = _L1_attn_setup()
    _L1_attn_in = {k: v for k, v in _L1_attn_all.items() if k in ('ln_w', 'ln_b', 'qkv_w', 'qkv_b', 'out_w', 'out_b')}
    del _L1_attn_all

    def _L1_xattn_setup():
        import jax, jax.numpy as jnp
        import numpy as np
        HEADS = 16
        DIM_HEAD = 64
        SCALE = DIM_HEAD ** (-0.5)
        key = jax.random.key(seed)
        ks = jax.random.split(key, 7)
        B, SQ, SKV, QD, CD, ID = (4, 1024, 256, 256, 192, HEADS * DIM_HEAD)
        s = lambda d: 1.0 / np.sqrt(d)
        return {'x': jax.random.normal(ks[0], (B, SQ, QD), jnp.float32), 'context': jax.random.normal(ks[1], (B, SKV, CD), jnp.float32), 'Wq': jax.random.normal(ks[2], (QD, ID), jnp.float32) * s(QD), 'Wk': jax.random.normal(ks[3], (CD, ID), jnp.float32) * s(CD), 'Wv': jax.random.normal(ks[4], (CD, ID), jnp.float32) * s(CD), 'Wo': jax.random.normal(ks[5], (ID, QD), jnp.float32) * s(ID), 'bo': jnp.zeros((QD,), jnp.float32)}
    _L1_xattn_all = _L1_xattn_setup()
    _L1_xattn_in = {k: v for k, v in _L1_xattn_all.items() if k in ('Wq', 'Wk', 'Wv', 'Wo', 'bo')}
    del _L1_xattn_all

    def _L1_ffn_setup():
        import jax, jax.numpy as jnp
        import numpy as np
        CAPACITY_FACTOR = 0.5
        NUM_HEADS = 16
        key = jax.random.key(seed)
        ks = jax.random.split(key, 6)
        B, N, D = (4, 1024, 256)
        s = 1.0 / np.sqrt(D)
        return {'token_inputs': jax.random.normal(ks[0], (B, N, D), jnp.float32), 'Wg': jax.random.normal(ks[1], (D, 1), jnp.float32) * s, 'Wq': jax.random.normal(ks[2], (D, D), jnp.float32) * s, 'Wk': jax.random.normal(ks[3], (D, D), jnp.float32) * s, 'Wv': jax.random.normal(ks[4], (D, D), jnp.float32) * s, 'Wo': jax.random.normal(ks[5], (D, D), jnp.float32) * s}
    _L1_ffn_all = _L1_ffn_setup()
    _L1_ffn_in = {k: v for k, v in _L1_ffn_all.items() if k in ('Wg', 'Wq', 'Wk', 'Wv', 'Wo')}
    del _L1_ffn_all

    def _L2_attn_setup():
        import jax, jax.numpy as jnp
        import numpy as np
        DIM = 256
        NUM_HEADS = 16
        HEAD_DIM = DIM // NUM_HEADS
        key = jax.random.key(seed)
        k1, k2, k3, k4, k5 = jax.random.split(key, 5)
        x = jax.random.normal(k1, (1, 1024, DIM), dtype=jnp.float32)
        scale = 1.0 / np.sqrt(DIM)
        W_qkv = jax.random.normal(k2, (DIM, 3 * DIM), dtype=jnp.float32) * scale
        b_qkv = jnp.zeros((3 * DIM,), dtype=jnp.float32)
        W_proj = jax.random.normal(k3, (DIM, DIM), dtype=jnp.float32) * scale
        b_proj = jnp.zeros((DIM,), dtype=jnp.float32)
        return {'x': x, 'W_qkv': W_qkv, 'b_qkv': b_qkv, 'W_proj': W_proj, 'b_proj': b_proj}
    _L2_attn_all = _L2_attn_setup()
    _L2_attn_in = {k: v for k, v in _L2_attn_all.items() if k in ('W_qkv', 'b_qkv', 'W_proj', 'b_proj')}
    del _L2_attn_all

    def _L2_xattn_setup():
        import jax, jax.numpy as jnp
        import numpy as np
        HEADS = 16
        DIM_HEAD = 64
        SCALE = DIM_HEAD ** (-0.5)
        key = jax.random.key(seed)
        ks = jax.random.split(key, 7)
        B, Nq, Dq = (16, 1024, 256)
        Nc, Dc = (77, 192)
        inner = HEADS * DIM_HEAD
        return {'x': jax.random.normal(ks[0], (B, Nq, Dq), jnp.float32), 'context': jax.random.normal(ks[1], (B, Nc, Dc), jnp.float32), 'Wq': jax.random.normal(ks[2], (Dq, inner), jnp.float32) * Dq ** (-0.5), 'Wk': jax.random.normal(ks[3], (Dc, inner), jnp.float32) * Dc ** (-0.5), 'Wv': jax.random.normal(ks[4], (Dc, inner), jnp.float32) * Dc ** (-0.5), 'Wo': jax.random.normal(ks[5], (inner, Dq), jnp.float32) * inner ** (-0.5), 'bo': jnp.zeros((Dq,), jnp.float32)}
    _L2_xattn_all = _L2_xattn_setup()
    _L2_xattn_in = {k: v for k, v in _L2_xattn_all.items() if k in ('Wq', 'Wk', 'Wv', 'Wo', 'bo')}
    del _L2_xattn_all

    def _L2_ffn_setup():
        import jax, jax.numpy as jnp
        import numpy as np
        NUM_EXPERTS = 8
        TOP_K = 2
        MODEL_DIM = 256
        INTER_DIM = 1024

        def _grouped_matmul(x, w, seg_ids):
            out = jnp.zeros((x.shape[0], w.shape[2]), dtype=x.dtype)
            for e in range(w.shape[0]):
                xe = jnp.where((seg_ids == e)[:, None], x, 0)
                out = out + xe @ w[e]
            return out
        key = jax.random.key(seed)
        k1, k2, k3, k4 = jax.random.split(key, 4)
        hidden_states = jax.random.normal(k1, (4, 128, MODEL_DIM), jnp.float32)
        gate_w = jax.random.normal(k2, (NUM_EXPERTS, MODEL_DIM), jnp.float32) * 0.02
        w_up = jax.random.normal(k3, (NUM_EXPERTS, MODEL_DIM, INTER_DIM), jnp.float32) * 0.02
        w_down = jax.random.normal(k4, (NUM_EXPERTS, INTER_DIM, MODEL_DIM), jnp.float32) * 0.02
        return {'hidden_states': hidden_states, 'gate_w': gate_w, 'w_up': w_up, 'w_down': w_down}
    _L2_ffn_all = _L2_ffn_setup()
    _L2_ffn_in = {k: v for k, v in _L2_ffn_all.items() if k in ('gate_w', 'w_up', 'w_down')}
    del _L2_ffn_all

    def _L3_attn_setup():
        import jax, jax.numpy as jnp
        import numpy as np
        import math
        D_MODEL = 256
        D_K = 64
        D_V = 64
        N_HEADS = 16
        key = jax.random.key(seed)
        ks = jax.random.split(key, 5)
        std = 1.0 / math.sqrt(D_MODEL)
        x = jax.random.normal(ks[0], (2, 512, D_MODEL), dtype=jnp.float32)
        Wq = jax.random.normal(ks[1], (D_MODEL, N_HEADS * D_K), dtype=jnp.float32) * std
        Wk = jax.random.normal(ks[2], (D_MODEL, N_HEADS * D_K), dtype=jnp.float32) * std
        Wv = jax.random.normal(ks[3], (D_MODEL, N_HEADS * D_V), dtype=jnp.float32) * std
        Wo = jax.random.normal(ks[4], (N_HEADS * D_V, D_MODEL), dtype=jnp.float32) * std
        return {'x': x, 'Wq': Wq, 'Wk': Wk, 'Wv': Wv, 'Wo': Wo}
    _L3_attn_all = _L3_attn_setup()
    _L3_attn_in = {k: v for k, v in _L3_attn_all.items() if k in ('Wq', 'Wk', 'Wv', 'Wo')}
    del _L3_attn_all

    def _L3_xattn_setup():
        import jax, jax.numpy as jnp
        import numpy as np
        HEADS = 8
        DIM_HEAD = 64
        QUERY_DIM = 256
        CONTEXT_DIM = 192
        INNER = HEADS * DIM_HEAD
        key = jax.random.key(seed)
        ks = jax.random.split(key, 7)
        B, Sq, Skv = (4, 1024, 256)
        x = jax.random.normal(ks[0], (B, Sq, QUERY_DIM), dtype=jnp.float32)
        context = jax.random.normal(ks[1], (B, Skv, CONTEXT_DIM), dtype=jnp.float32)
        Wq = jax.random.normal(ks[2], (QUERY_DIM, INNER), dtype=jnp.float32) * QUERY_DIM ** (-0.5)
        Wk = jax.random.normal(ks[3], (CONTEXT_DIM, INNER), dtype=jnp.float32) * CONTEXT_DIM ** (-0.5)
        Wv = jax.random.normal(ks[4], (CONTEXT_DIM, INNER), dtype=jnp.float32) * CONTEXT_DIM ** (-0.5)
        Wo = jax.random.normal(ks[5], (INNER, QUERY_DIM), dtype=jnp.float32) * INNER ** (-0.5)
        bo = jax.random.normal(ks[6], (QUERY_DIM,), dtype=jnp.float32) * 0.01
        return {'x': x, 'context': context, 'Wq': Wq, 'Wk': Wk, 'Wv': Wv, 'Wo': Wo, 'bo': bo}
    _L3_xattn_all = _L3_xattn_setup()
    _L3_xattn_in = {k: v for k, v in _L3_xattn_all.items() if k in ('Wq', 'Wk', 'Wv', 'Wo', 'bo')}
    del _L3_xattn_all

    def _L3_ffn_setup():
        import jax, jax.numpy as jnp
        import numpy as np
        TOP_K = 2
        CAPACITY_FACTOR = 1.0
        key = jax.random.key(seed)
        ks = jax.random.split(key, 4)
        sl, bs, hs, ffn, E = (512, 8, 256, 1024, 8)
        x = jax.random.normal(ks[0], (sl, bs, hs), dtype=jnp.float32)
        w_router = jax.random.normal(ks[1], (hs, E), dtype=jnp.float32) * 0.02
        w1 = jax.random.normal(ks[2], (E, hs, ffn), dtype=jnp.float32) * 0.02
        w2 = jax.random.normal(ks[3], (E, ffn, hs), dtype=jnp.float32) * 0.02
        bias = jnp.zeros((1, 1, hs), dtype=jnp.float32)
        return {'x': x, 'w_router': w_router, 'w1': w1, 'w2': w2, 'bias': bias}
    _L3_ffn_all = _L3_ffn_setup()
    _L3_ffn_in = {k: v for k, v in _L3_ffn_all.items() if k in ('w_router', 'w1', 'w2', 'bias')}
    del _L3_ffn_all
    return {'x': x, 'ctx_768': ctx_768, 'L0_attn_Wq': _L0_attn_in['Wq'], 'L0_attn_bq': _L0_attn_in['bq'], 'L0_attn_Wk': _L0_attn_in['Wk'], 'L0_attn_bk': _L0_attn_in['bk'], 'L0_attn_Wv': _L0_attn_in['Wv'], 'L0_attn_bv': _L0_attn_in['bv'], 'L0_attn_Wo': _L0_attn_in['Wo'], 'L0_attn_bo': _L0_attn_in['bo'], 'L0_xattn_Wq': _L0_xattn_in['Wq'], 'L0_xattn_bq': _L0_xattn_in['bq'], 'L0_xattn_Wk': _L0_xattn_in['Wk'], 'L0_xattn_bk': _L0_xattn_in['bk'], 'L0_xattn_Wv': _L0_xattn_in['Wv'], 'L0_xattn_bv': _L0_xattn_in['bv'], 'L0_xattn_Wo': _L0_xattn_in['Wo'], 'L0_xattn_bo': _L0_xattn_in['bo'], 'L0_ffn_W_r': _L0_ffn_in['W_r'], 'L0_ffn_W_k': _L0_ffn_in['W_k'], 'L0_ffn_W_v': _L0_ffn_in['W_v'], 'L0_ffn_mu_r': _L0_ffn_in['mu_r'], 'L0_ffn_mu_k': _L0_ffn_in['mu_k'], 'L1_attn_ln_w': _L1_attn_in['ln_w'], 'L1_attn_ln_b': _L1_attn_in['ln_b'], 'L1_attn_qkv_w': _L1_attn_in['qkv_w'], 'L1_attn_qkv_b': _L1_attn_in['qkv_b'], 'L1_attn_out_w': _L1_attn_in['out_w'], 'L1_attn_out_b': _L1_attn_in['out_b'], 'L1_xattn_Wq': _L1_xattn_in['Wq'], 'L1_xattn_Wk': _L1_xattn_in['Wk'], 'L1_xattn_Wv': _L1_xattn_in['Wv'], 'L1_xattn_Wo': _L1_xattn_in['Wo'], 'L1_xattn_bo': _L1_xattn_in['bo'], 'L1_ffn_Wg': _L1_ffn_in['Wg'], 'L1_ffn_Wq': _L1_ffn_in['Wq'], 'L1_ffn_Wk': _L1_ffn_in['Wk'], 'L1_ffn_Wv': _L1_ffn_in['Wv'], 'L1_ffn_Wo': _L1_ffn_in['Wo'], 'L2_attn_W_qkv': _L2_attn_in['W_qkv'], 'L2_attn_b_qkv': _L2_attn_in['b_qkv'], 'L2_attn_W_proj': _L2_attn_in['W_proj'], 'L2_attn_b_proj': _L2_attn_in['b_proj'], 'L2_xattn_Wq': _L2_xattn_in['Wq'], 'L2_xattn_Wk': _L2_xattn_in['Wk'], 'L2_xattn_Wv': _L2_xattn_in['Wv'], 'L2_xattn_Wo': _L2_xattn_in['Wo'], 'L2_xattn_bo': _L2_xattn_in['bo'], 'L2_ffn_gate_w': _L2_ffn_in['gate_w'], 'L2_ffn_w_up': _L2_ffn_in['w_up'], 'L2_ffn_w_down': _L2_ffn_in['w_down'], 'L3_attn_Wq': _L3_attn_in['Wq'], 'L3_attn_Wk': _L3_attn_in['Wk'], 'L3_attn_Wv': _L3_attn_in['Wv'], 'L3_attn_Wo': _L3_attn_in['Wo'], 'L3_xattn_Wq': _L3_xattn_in['Wq'], 'L3_xattn_Wk': _L3_xattn_in['Wk'], 'L3_xattn_Wv': _L3_xattn_in['Wv'], 'L3_xattn_Wo': _L3_xattn_in['Wo'], 'L3_xattn_bo': _L3_xattn_in['bo'], 'L3_ffn_w_router': _L3_ffn_in['w_router'], 'L3_ffn_w1': _L3_ffn_in['w1'], 'L3_ffn_w2': _L3_ffn_in['w2'], 'L3_ffn_bias': _L3_ffn_in['bias']}

def reference(x, ctx_768, L0_attn_Wq, L0_attn_bq, L0_attn_Wk, L0_attn_bk, L0_attn_Wv, L0_attn_bv, L0_attn_Wo, L0_attn_bo, L0_xattn_Wq, L0_xattn_bq, L0_xattn_Wk, L0_xattn_bk, L0_xattn_Wv, L0_xattn_bv, L0_xattn_Wo, L0_xattn_bo, L0_ffn_W_r, L0_ffn_W_k, L0_ffn_W_v, L0_ffn_mu_r, L0_ffn_mu_k, L1_attn_ln_w, L1_attn_ln_b, L1_attn_qkv_w, L1_attn_qkv_b, L1_attn_out_w, L1_attn_out_b, L1_xattn_Wq, L1_xattn_Wk, L1_xattn_Wv, L1_xattn_Wo, L1_xattn_bo, L1_ffn_Wg, L1_ffn_Wq, L1_ffn_Wk, L1_ffn_Wv, L1_ffn_Wo, L2_attn_W_qkv, L2_attn_b_qkv, L2_attn_W_proj, L2_attn_b_proj, L2_xattn_Wq, L2_xattn_Wk, L2_xattn_Wv, L2_xattn_Wo, L2_xattn_bo, L2_ffn_gate_w, L2_ffn_w_up, L2_ffn_w_down, L3_attn_Wq, L3_attn_Wk, L3_attn_Wv, L3_attn_Wo, L3_xattn_Wq, L3_xattn_Wk, L3_xattn_Wv, L3_xattn_Wo, L3_xattn_bo, L3_ffn_w_router, L3_ffn_w1, L3_ffn_w2, L3_ffn_bias):
    import jax
    import jax.numpy as jnp

    def _L0_attn_ref(x, Wq, bq, Wk, bk, Wv, bv, Wo, bo):
        import jax, jax.numpy as jnp
        import numpy as np
        D_MODEL = 256
        N_HEADS = 16
        N_GROUPS = 4
        CONTEXT_LEN = 128
        D_H = D_MODEL // N_HEADS
        GROUP_SIZE = N_HEADS // N_GROUPS
        B, S = (4, 512)
        b, s = (x.shape[0], x.shape[1])
        q = (x @ Wq + bq).reshape(b, s, N_GROUPS, GROUP_SIZE, D_H)
        q = jnp.transpose(q, (0, 2, 3, 1, 4))
        k = jnp.transpose((x @ Wk + bk).reshape(b, s, N_GROUPS, D_H), (0, 2, 1, 3))
        v = jnp.transpose((x @ Wv + bv).reshape(b, s, N_GROUPS, D_H), (0, 2, 1, 3))
        scores = jnp.einsum('bghqd,bgkd->bghqk', q, k) / jnp.sqrt(jnp.float32(D_H))
        i = jnp.arange(s)
        j = jnp.arange(s)
        upper = (i - CONTEXT_LEN)[:, None] >= j[None, :]
        lower = i[:, None] < j[None, :]
        mask = upper | lower
        scores = jnp.where(mask, jnp.float32(-1000000000.0), scores)
        att = jax.nn.softmax(scores, axis=-1)
        out = jnp.einsum('bghqk,bgkd->bghqd', att, v)
        out = jnp.transpose(out, (0, 3, 1, 2, 4)).reshape(b, s, D_MODEL)
        return out @ Wo + bo

    def _L0_xattn_ref(x, y, Wq, bq, Wk, bk, Wv, bv, Wo, bo):
        import jax, jax.numpy as jnp
        import numpy as np
        import math
        N_HEADS = 8
        D_EMBED = 256
        D_CROSS = 192
        D_HEAD = D_EMBED // N_HEADS
        B, S, _ = x.shape
        SKV = y.shape[1]
        q = x @ Wq.T + bq
        k = y @ Wk.T + bk
        v = y @ Wv.T + bv
        q = q.reshape(B, S, N_HEADS, D_HEAD).transpose(0, 2, 1, 3)
        k = k.reshape(B, SKV, N_HEADS, D_HEAD).transpose(0, 2, 1, 3)
        v = v.reshape(B, SKV, N_HEADS, D_HEAD).transpose(0, 2, 1, 3)
        scores = jnp.einsum('bhqd,bhkd->bhqk', q, k) / math.sqrt(D_HEAD)
        attn = jax.nn.softmax(scores, axis=-1)
        out = jnp.einsum('bhqk,bhkd->bhqd', attn, v)
        out = out.transpose(0, 2, 1, 3).reshape(B, S, D_EMBED)
        return out @ Wo.T + bo

    def _L0_ffn_ref(x, W_r, W_k, W_v, mu_r, mu_k):
        import jax, jax.numpy as jnp
        import numpy as np
        DIM = 256

        def _reference_tuple_inner(x, W_r, W_k, W_v, mu_r, mu_k):
            B, T, C = x.shape
            x_prev = jnp.concatenate([jnp.zeros((B, 1, C), x.dtype), x[:, :-1, :]], axis=1)
            xr = mu_r * x + (1.0 - mu_r) * x_prev
            xk = mu_k * x + (1.0 - mu_k) * x_prev
            r = jax.nn.sigmoid(jnp.einsum('btc,dc->btd', xr, W_r))
            k = jnp.einsum('btc,dc->btd', xk, W_k)
            k_act = jnp.square(jax.nn.relu(k))
            out = r * jnp.einsum('btc,dc->btd', k_act, W_v)
            new_state = x[:, -1, :]
            return (out, new_state)
        return _reference_tuple_inner(x, W_r, W_k, W_v, mu_r, mu_k)[0]

    def _L1_attn_ref(x, ln_w, ln_b, qkv_w, qkv_b, out_w, out_b):
        import jax, jax.numpy as jnp
        import numpy as np
        DIM = 256
        NUM_HEADS = 16
        HEAD_DIM = DIM // NUM_HEADS
        EPS_NORM = 1e-12
        EPS_LN = 1e-05
        B, N, D = x.shape
        mu = jnp.mean(x, axis=-1, keepdims=True)
        var = jnp.mean(jnp.square(x - mu), axis=-1, keepdims=True)
        h = (x - mu) / jnp.sqrt(var + EPS_LN) * ln_w + ln_b
        qkv = h @ qkv_w.T + qkv_b
        qkv = qkv.reshape(B, N, 3, NUM_HEADS, HEAD_DIM)
        q, k, v = (jnp.transpose(qkv[:, :, i], (0, 2, 1, 3)) for i in range(3))
        q = q / jnp.maximum(jnp.linalg.norm(q, axis=-1, keepdims=True), EPS_NORM)
        k = k / jnp.maximum(jnp.linalg.norm(k, axis=-1, keepdims=True), EPS_NORM)
        scale = HEAD_DIM ** 0.5
        attn = jnp.einsum('bhqd,bhkd->bhqk', q, k) * scale
        attn = jax.nn.softmax(attn, axis=-1)
        out = jnp.einsum('bhqk,bhkd->bhqd', attn, v)
        out = jnp.transpose(out, (0, 2, 1, 3)).reshape(B, N, D)
        return x + out @ out_w.T + out_b

    def _L1_xattn_ref(x, context, Wq, Wk, Wv, Wo, bo):
        import jax, jax.numpy as jnp
        import numpy as np
        HEADS = 16
        DIM_HEAD = 64
        SCALE = DIM_HEAD ** (-0.5)
        b, sq, _ = x.shape

        def split_heads(t):
            return t.reshape(b, -1, HEADS, DIM_HEAD).transpose(0, 2, 1, 3)
        q = split_heads(x @ Wq)
        k = split_heads(context @ Wk)
        v = split_heads(context @ Wv)
        sim = jnp.einsum('bhid,bhjd->bhij', q, k) * SCALE
        attn = jax.nn.softmax(sim, axis=-1)
        out = jnp.einsum('bhij,bhjd->bhid', attn, v)
        out = out.transpose(0, 2, 1, 3).reshape(b, sq, HEADS * DIM_HEAD)
        return out @ Wo + bo

    def _L1_ffn_ref(token_inputs, Wg, Wq, Wk, Wv, Wo):
        import jax, jax.numpy as jnp
        import numpy as np
        CAPACITY_FACTOR = 0.5
        NUM_HEADS = 16
        B, N, D = token_inputs.shape
        C = int(N * CAPACITY_FACTOR)
        H = NUM_HEADS
        dh = D // H
        gate = jax.nn.sigmoid((token_inputs @ Wg)[..., 0])
        _, idx = jax.lax.top_k(gate, C)
        attn_in = jnp.take_along_axis(token_inputs, idx[..., None], axis=1)
        q = (attn_in @ Wq).reshape(B, C, H, dh)
        k = (attn_in @ Wk).reshape(B, C, H, dh)
        v = (attn_in @ Wv).reshape(B, C, H, dh)
        scores = jnp.einsum('bqhd,bkhd->bhqk', q, k) / jnp.sqrt(jnp.float32(dh))
        attn = jax.nn.softmax(scores, axis=-1)
        o = jnp.einsum('bhqk,bkhd->bqhd', attn, v).reshape(B, C, D) @ Wo
        gate_sel = jnp.take_along_axis(gate, idx, axis=1)
        out = jnp.zeros_like(token_inputs)
        out = out.at[jnp.arange(B)[:, None], idx].set(o * gate_sel[..., None])
        return out

    def _L2_attn_ref(x, W_qkv, b_qkv, W_proj, b_proj):
        import jax, jax.numpy as jnp
        import numpy as np
        DIM = 256
        NUM_HEADS = 16
        HEAD_DIM = DIM // NUM_HEADS
        B, N, C = x.shape
        H, D = (NUM_HEADS, HEAD_DIM)
        qkv = x @ W_qkv + b_qkv
        qkv = qkv.reshape(B, N, 3, H, D).transpose(2, 0, 3, 1, 4)
        q, k, v = (qkv[0], qkv[1], qkv[2])
        scores = jnp.einsum('bhnd,bhkd->bhnk', q, k) / np.sqrt(D)
        attn = jax.nn.softmax(scores, axis=-1)
        out = jnp.einsum('bhnk,bhkd->bhnd', attn, v)
        out = out.transpose(0, 2, 1, 3).reshape(B, N, C)
        return out @ W_proj + b_proj

    def _L2_xattn_ref(x, context, Wq, Wk, Wv, Wo, bo):
        import jax, jax.numpy as jnp
        import numpy as np
        HEADS = 16
        DIM_HEAD = 64
        SCALE = DIM_HEAD ** (-0.5)
        B, Nq, _ = x.shape
        Nc = context.shape[1]
        q = (x @ Wq).reshape(B, Nq, HEADS, DIM_HEAD).transpose(0, 2, 1, 3)
        k = (context @ Wk).reshape(B, Nc, HEADS, DIM_HEAD).transpose(0, 2, 1, 3)
        v = (context @ Wv).reshape(B, Nc, HEADS, DIM_HEAD).transpose(0, 2, 1, 3)
        sim = jnp.einsum('bhid,bhjd->bhij', q, k) * SCALE
        attn = jax.nn.softmax(sim, axis=-1)
        out = jnp.einsum('bhij,bhjd->bhid', attn, v)
        out = out.transpose(0, 2, 1, 3).reshape(B, Nq, HEADS * DIM_HEAD)
        return out @ Wo + bo

    def _L2_ffn_ref(hidden_states, gate_w, w_up, w_down):
        import jax, jax.numpy as jnp
        import numpy as np
        NUM_EXPERTS = 8
        TOP_K = 2
        MODEL_DIM = 256
        INTER_DIM = 1024

        def _grouped_matmul(x, w, seg_ids):
            out = jnp.zeros((x.shape[0], w.shape[2]), dtype=x.dtype)
            for e in range(w.shape[0]):
                xe = jnp.where((seg_ids == e)[:, None], x, 0)
                out = out + xe @ w[e]
            return out
        orig_shape = hidden_states.shape
        x = hidden_states.reshape(-1, orig_shape[-1])
        T = x.shape[0]
        logits = x @ gate_w.T
        probs = jax.nn.softmax(logits.astype(jnp.float32), axis=-1)
        _, topk_idx = jax.lax.top_k(probs, TOP_K)
        idx_flat = topk_idx.T.reshape(-1)
        order = jnp.argsort(idx_flat)
        seg_ids = idx_flat[order]
        token_ids = order % T
        moe_in = x[token_ids]
        h = _grouped_matmul(moe_in, w_up, seg_ids)
        moe_out = _grouped_matmul(h, w_down, seg_ids)
        out = jnp.zeros_like(x).at[token_ids].add(moe_out)
        return out.reshape(orig_shape)

    def _L3_attn_ref(x, Wq, Wk, Wv, Wo):
        import jax, jax.numpy as jnp
        import numpy as np
        import math
        D_MODEL = 256
        D_K = 64
        D_V = 64
        N_HEADS = 16
        B, S, D = x.shape
        H, dk, dv = (N_HEADS, D_K, D_V)
        q = (x @ Wq).reshape(B, S, H, dk)
        k = (x @ Wk).reshape(B, S, H, dk)
        v = (x @ Wv).reshape(B, S, H, dv)
        scores = jnp.einsum('bqhd,bkhd->bhqk', q / math.sqrt(dk), k)
        causal = jnp.tril(jnp.ones((S, S), dtype=bool))
        scores = scores + jnp.where(causal, 0.0, -jnp.inf).astype(scores.dtype)
        attn = jax.nn.softmax(scores, axis=-1)
        out = jnp.einsum('bhqk,bkhd->bqhd', attn, v).reshape(B, S, H * dv)
        return x + out @ Wo

    def _L3_xattn_ref(x, context, Wq, Wk, Wv, Wo, bo):
        import jax, jax.numpy as jnp
        import numpy as np
        HEADS = 8
        DIM_HEAD = 64
        QUERY_DIM = 256
        CONTEXT_DIM = 192
        INNER = HEADS * DIM_HEAD
        B, Sq, _ = x.shape
        h, d = (HEADS, DIM_HEAD)
        scale = d ** (-0.5)
        q = (x @ Wq).reshape(B, Sq, h, d).transpose(0, 2, 1, 3)
        k = (context @ Wk).reshape(B, -1, h, d).transpose(0, 2, 1, 3)
        v = (context @ Wv).reshape(B, -1, h, d).transpose(0, 2, 1, 3)
        scores = jnp.einsum('bhid,bhjd->bhij', q, k) * scale
        attn = jax.nn.softmax(scores, axis=-1)
        out = jnp.einsum('bhij,bhjd->bhid', attn, v)
        out = out.transpose(0, 2, 1, 3).reshape(B, Sq, h * d)
        return out @ Wo + bo

    def _L3_ffn_ref(x, w_router, w1, w2, bias):
        import jax, jax.numpy as jnp
        import numpy as np
        TOP_K = 2
        CAPACITY_FACTOR = 1.0
        sl, bs, hs = x.shape
        E = w_router.shape[1]
        xf = x.reshape(-1, hs)
        T = xf.shape[0]
        capacity = int(CAPACITY_FACTOR * TOP_K * T / E)
        scores = jax.nn.softmax(xf @ w_router, axis=-1)
        expert_weights, top_experts = jax.lax.top_k(scores, TOP_K)
        flat_e = top_experts.reshape(-1)
        flat_w = expert_weights.reshape(-1)
        N = flat_e.shape[0]
        order = jnp.argsort(flat_e, stable=True)
        bin_ids = flat_e[order]
        tpe = jnp.zeros((E,), jnp.int32).at[flat_e].add(1)
        starts = jnp.cumsum(tpe) - tpe
        offsets = jnp.arange(N) - starts[bin_ids]
        valid = offsets < capacity
        slot = jnp.where(valid, bin_ids * capacity + offsets, E * capacity)
        src = order // TOP_K
        xb = jnp.zeros((E * capacity + 1, hs), x.dtype).at[slot].set(xf[src])
        xb = xb[:-1].reshape(E, capacity, hs)
        h = jax.nn.gelu(jnp.einsum('ech,ehf->ecf', xb, w1))
        y = jnp.einsum('ecf,efh->ech', h, w2).reshape(E * capacity, hs)
        yv = jnp.where(valid[:, None], y[jnp.minimum(slot, E * capacity - 1)], 0.0)
        out = jnp.zeros((T, hs), x.dtype).at[src].add(flat_w[order][:, None] * yv)
        return out.reshape(sl, bs, hs) + bias
    x = x + _L0_attn_ref(_layernorm(x, axis=-1), L0_attn_Wq, L0_attn_bq, L0_attn_Wk, L0_attn_bk, L0_attn_Wv, L0_attn_bv, L0_attn_Wo, L0_attn_bo)
    x = x + _L0_xattn_ref(_layernorm(x, axis=-1), ctx_768, L0_xattn_Wq, L0_xattn_bq, L0_xattn_Wk, L0_xattn_bk, L0_xattn_Wv, L0_xattn_bv, L0_xattn_Wo, L0_xattn_bo)
    x = x + _L0_ffn_ref(_layernorm(x, axis=-1), L0_ffn_W_r, L0_ffn_W_k, L0_ffn_W_v, L0_ffn_mu_r, L0_ffn_mu_k)
    x = x + _L1_attn_ref(_layernorm(x, axis=-1), L1_attn_ln_w, L1_attn_ln_b, L1_attn_qkv_w, L1_attn_qkv_b, L1_attn_out_w, L1_attn_out_b)
    x = x + _L1_xattn_ref(_layernorm(x, axis=-1), ctx_768, L1_xattn_Wq, L1_xattn_Wk, L1_xattn_Wv, L1_xattn_Wo, L1_xattn_bo)
    x = x + _L1_ffn_ref(_layernorm(x, axis=-1), L1_ffn_Wg, L1_ffn_Wq, L1_ffn_Wk, L1_ffn_Wv, L1_ffn_Wo)
    x = x + _L2_attn_ref(_layernorm(x, axis=-1), L2_attn_W_qkv, L2_attn_b_qkv, L2_attn_W_proj, L2_attn_b_proj)
    x = x + _L2_xattn_ref(_layernorm(x, axis=-1), ctx_768, L2_xattn_Wq, L2_xattn_Wk, L2_xattn_Wv, L2_xattn_Wo, L2_xattn_bo)
    x = x + _L2_ffn_ref(_layernorm(x, axis=-1), L2_ffn_gate_w, L2_ffn_w_up, L2_ffn_w_down)
    x = x + _L3_attn_ref(_layernorm(x, axis=-1), L3_attn_Wq, L3_attn_Wk, L3_attn_Wv, L3_attn_Wo)
    x = x + _L3_xattn_ref(_layernorm(x, axis=-1), ctx_768, L3_xattn_Wq, L3_xattn_Wk, L3_xattn_Wv, L3_xattn_Wo, L3_xattn_bo)
    x = x + _L3_ffn_ref(_layernorm(x, axis=-1), L3_ffn_w_router, L3_ffn_w1, L3_ffn_w2, L3_ffn_bias)
    return x

_drawn_inputs = setup_inputs


def setup_inputs(seed=0):
    import zlib

    import numpy as np

    out = dict(_drawn_inputs(seed))
    spreads = {'L0_xattn_bq': (0.0, 0.296),
     'L0_xattn_bk': (0.0, 0.8),
     'L0_xattn_bv': (0.0, 0.1),
     'L0_xattn_bo': (0.0, 0.1),
     'L1_attn_ln_w': (1.0, 0.6),
     'L1_attn_ln_b': (0.0, 0.511),
     'L1_attn_qkv_b': (0.0, 0.363),
     'L1_attn_out_b': (0.0, 0.1),
     'L1_xattn_bo': (0.0, 0.1),
     'L2_attn_b_qkv': (0.0, 0.1),
     'L2_attn_b_proj': (0.0, 0.1),
     'L2_xattn_bo': (0.0, 0.1),
     'L3_ffn_bias': (0.0, 0.3)}
    factors = {'L0_attn_Wq': 8.0,
     'L0_attn_bq': 8.0,
     'L0_attn_Wk': 8.0,
     'L0_attn_bk': 8.0,
     'L0_attn_Wv': 2.803,
     'L0_attn_bv': 4.879,
     'L0_ffn_mu_r': 4.777,
     'L1_ffn_Wq': 2.723,
     'L3_xattn_bo': 8.0,
     'L3_ffn_w_router': 8.0,
     'L3_ffn_w1': 8.0,
     'L3_ffn_w2': 8.0}
    for name, (base, spread) in spreads.items():
        noise = np.random.default_rng([zlib.crc32(name.encode()), seed]).standard_normal(out[name].shape)
        drawn = base * np.exp(spread * noise) if base else spread * noise
        out[name] = jnp.asarray(drawn.astype(out[name].dtype))
    for name, factor in factors.items():
        out[name] = (out[name] * factor).astype(out[name].dtype)
    return out
```

```python
from contextlib import ExitStack

import numpy as np
import concourse.bass as bass
from concourse import mybir

ALU = mybir.AluOpType
ACT = mybir.ActivationFunctionType
AX = mybir.AxisListType
F32 = mybir.dt.float32
BF16 = mybir.dt.bfloat16
I32 = mybir.dt.int32

P = 128
B, S, D = 8, 256, 256
DC = 192
CR = DC // 2
T = B * S
NPAIR = B // 2
TT = 2 * S // P
KD = D // P
BANK = 512
EPS = 1e-5
MASKED = -1.0e30
NE = 8
F = 1024
FC = F // P
CAP = 2 * T // NE
ARENA = 8448


class Attn:

    def __init__(self, name, heads, dh, scale, ctx=False, mask=None, kv_heads=None, qkv_bias=False,
                 out_bias=False, res_h=False, normed=False, selected=False):
        self.name, self.H, self.dh, self.scale, self.ctx, self.mask = name, heads, dh, scale, ctx, mask
        self.qkv_bias, self.out_bias, self.res_h = qkv_bias, out_bias, res_h
        self.normed, self.selected = normed, selected
        self.slot = max(dh, 32)
        self.per = P // self.slot
        self.nch = heads // self.per
        self.kvh = kv_heads or heads
        self.rep = heads // self.kvh
        self.NV = self.kvh * dh
        self.inner = heads * dh
        self.NC = self.inner // P
        self.G = heads // 2
        self.NS = 2 * self.G
        self.TB = P if selected else S
        self.nt = self.TB // P
        self.E = 2 * self.nt
        self.kr = CR if ctx else P
        at = 0
        self.at = {}
        nq = self.nch * P
        for key, n in (("wq", KD * (2 * D if normed else nq)), ("wk", 0 if normed else KD * nq),
                       ("wv", KD * self.NV), ("wo", self.NC * D),
                       ("bq", self.nch if qkv_bias and not normed else 0),
                       ("bk", self.nch if qkv_bias and not normed else 0),
                       ("bqk", 2 * D if normed else 0), ("bv", self.NV if qkv_bias else 0),
                       ("bo", D if out_bias else 0), ("lnw", KD if normed else 0),
                       ("lnb", KD if normed else 0), ("wg", D if selected else 0)):
            self.at[key] = (at, n)
            at += n
        self.width = at
        assert at <= ARENA

    def row(self, h):
        return self.slot * (h % self.per)


ATTN = {
    0: Attn("L0_attn", 16, 16, 0.25, mask="window", kv_heads=4, qkv_bias=True, out_bias=True),
    1: Attn("L0_xattn", 8, 32, float(32.0 ** -0.5), ctx=True, qkv_bias=True, out_bias=True),
    3: Attn("L1_attn", 16, 16, 4.0, qkv_bias=True, out_bias=True, res_h=True, normed=True),
    4: Attn("L1_xattn", 16, 64, 0.125, ctx=True, out_bias=True),
    5: Attn("L1_ffn", 16, 16, 0.25, selected=True),
    6: Attn("L2_attn", 16, 16, 0.25, qkv_bias=True, out_bias=True),
    7: Attn("L2_xattn", 16, 64, 0.125, ctx=True, out_bias=True),
    9: Attn("L3_attn", 16, 64, 0.125, mask="causal", res_h=True),
    10: Attn("L3_xattn", 8, 64, 0.125, ctx=True, out_bias=True),
}
MIX = {"wr": (0, KD * D), "wk": (KD * D, KD * D), "wv": (2 * KD * D, KD * D),
       "mur": (3 * KD * D, KD), "muk": (3 * KD * D + KD, KD)}
MIX_WIDTH = 3 * KD * D + 2 * KD
MOE2 = {"wg": (0, KD * NE), "wc": (KD * NE, NE * KD * D)}
MOE2_WIDTH = KD * NE
MOE3 = {"wr": (0, KD * NE), "bias": (KD * NE, D)}
MOE3_WIDTH = KD * NE + D
LAYERS = 12
WIDTH = {**{n: a.width for n, a in ATTN.items()}, 2: MIX_WIDTH, 8: MOE2_WIDTH, 11: MOE3_WIDTH}


class Core:

    def __init__(self, nc, ctx, dram):
        self.nc, self.dram = nc, dram

        def sb(name, shape, dt=F32):
            return ctx.enter_context(nc.sbuf_tensor(name, shape, dt))

        self.X = sb("X", [P, NPAIR, TT, D])
        self.arena = [sb(f"arena{n}", [P, ARENA]) for n in range(2)]
        self.QT = sb("QT", [P, 8, BANK])
        self.KT = sb("KT", [P, 8, BANK])
        self.V = sb("V", [P, TT, 1024])
        self.O = sb("O", [P, TT, 1024])
        self.Pb = sb("Pb", [P, 2, 4, S])
        self.PT = sb("PT", [P, 2, 2, BANK])
        self.h = sb("h", [P, TT, D])
        self.hT = sb("hT", [P, KD, BANK])
        self.cT = sb("cT", [P, KD, BANK])
        self.res = sb("res", [P, TT, D])
        self.st = sb("st", [P, TT, 6])
        self.mv = sb("mv", [P, TT, 2])
        self.lnv = sb("lnv", [P, TT])
        self.rstd = sb("rstd", [P, TT])
        self.nm = sb("nm", [P, 16, 4])
        self.sums = sb("sums", [P, 16, 4])
        self.rs = sb("rs", [P, 16, 4])
        self.small = sb("small", [P, 24, TT])
        self.ident = sb("ident", [P, P])
        self.identb = sb("identb", [P, P], BF16)
        self.mask = {m: sb(f"mask_{m}", [P, 2, S], BF16) for m in ("causal", "window")}
        self.before = sb("before", [P, 2, S])
        self.iota = sb("iota", [P, P])
        self.eps = sb("eps", [P, 1])
        self.first8 = sb("first8", [P, NE, NE])
        self.upper = sb("upper", [P, P])
        self.ones = sb("ones", [P, P])
        self.starts = sb("starts", [P, NE])
        self.st2 = sb("st2", [P, 5, T // P])
        self.idx = sb("idx", [P, 4, T // P], mybir.dt.uint32)
        self.xb = nc.dram_tensor("xb", (NE * CAP, D), F32, kind="Internal").ap()
        self.yb = nc.dram_tensor("yb", (NE * CAP, D), F32, kind="Internal").ap()
        self.ps = ctx.enter_context(nc.psum_tensor("ps", [P, 8, BANK], F32))
        def sem(name):
            return ctx.enter_context(nc.semaphore(name))

        self.ctx_in = sem("ctx_in")
        self.stats = sem("stats")
        self.rstd_ready = sem("rstd_ready")
        self.h_ready = sem("h_ready")
        self.res_ready = sem("res_ready")
        self.prod_ready = sem("prod_ready")
        self.copied_v = sem("copied_v")
        self.copied_a = sem("copied_a")
        self.scores_ready = sem("scores_ready")
        self.negmax_ready = sem("negmax_ready")
        self.probs_ready = sem("probs_ready")
        self.pT_ready = sem("pT_ready")
        self.pT_copied_v = sem("pT_copied_v")
        self.pT_copied_a = sem("pT_copied_a")
        self.av_ready = sem("av_ready")
        self.rsum_ready = sem("rsum_ready")
        self.av_normed = sem("av_normed")
        self.out_ready = sem("out_ready")
        self.oT_copied = sem("oT_copied")
        self.x_done = sem("x_done")
        self.chain_v = sem("chain_v")
        self.chain_a = sem("chain_a")
        self.sel_ready = sem("sel_ready")
        self.scattered = sem("scattered")
        self.stored = sem("stored")
        self.loop_sems = (self.ctx_in, self.stored)
        self.loop_count = 25
        self.x_in = sem("x_in")
        self.consts = sem("consts")
        self.w_in = [sem(f"w_in{n}") for n in range(LAYERS)]
        self.expert_in = [sem(f"expert_in{n}") for n in range(2 * NE)]
        self.rows_in = [sem(f"rows_in{n}") for n in range(2)]
        self.gathered = [sem(f"gathered{n}") for n in range(T // P)]
        self.zeroed = sem("zeroed")
        self.zero_in = sem("zero_in")
        self.x_out = sem("x_out")

    def clear(self):
        first, last = self.loop_sems[0].num, self.loop_sems[1].num
        assert last - first + 1 == self.loop_count
        self.nc.all_engine_barrier(sems_to_clear=range(first, last + 1))

    def w(self, layer, key, where, rows=P):
        at, n = where[key]
        return self.arena[layer % 2][0:rows, at:at + n]


def constants(k):
    nc = k.nc
    with nc.Block() as block:
        @block.sync
        def _(sp):
            sp.dma_start(k.X[:], k.dram["x"]).then_inc(k.x_in, 16)
            sp.dma_start(k.arena[LIST[0] % 2][:, 0:WIDTH[LIST[0]]],
                         k.dram[f"w{LIST[0]}"]).then_inc(k.w_in[LIST[0]], 16)

        @block.vector
        def _(dve):
            nc.vector.memset(k.eps[:], EPS)
            dve.wait_ge(k.x_in, 16)

        @block.gpsimd
        def _(pool):
            nc.gpsimd.memset(k.ident[:], 0.0).then_inc(k.consts, 1)
            nc.gpsimd.memset(k.mask["causal"][:], 0.0).then_inc(k.consts, 1)
            nc.gpsimd.memset(k.before[:], 1.0).then_inc(k.consts, 1)
            nc.gpsimd.iota(k.iota[:], pattern=[[1, P]], base=0, channel_multiplier=0,
                           allow_small_or_imprecise_dtypes=True).then_inc(k.consts, 1)
            nc.gpsimd.memset(k.first8[:], 1.0).then_inc(k.consts, 1)
            nc.gpsimd.memset(k.ones[:], 1.0).then_inc(k.consts, 1)
            nc.gpsimd.iota(k.starts[:], pattern=[[CAP, NE]], base=0, channel_multiplier=0,
                           allow_small_or_imprecise_dtypes=True).then_inc(k.consts, 1)
            pool.wait_ge(k.consts, 7)
            nc.gpsimd.affine_select(out=k.first8[:], in_=k.first8[:], compare_op=ALU.is_ge, fill=0.0, base=-1,
                                    pattern=[[1, NE], [-1, NE]], channel_multiplier=0).then_inc(k.consts, 1)
            nc.gpsimd.affine_select(out=k.upper[:], in_=k.ones[:], compare_op=ALU.is_ge, fill=0.0, base=-1,
                                    pattern=[[1, P]], channel_multiplier=-1).then_inc(k.consts, 1)
            nc.gpsimd.affine_select(out=k.ident[:], in_=k.ident[:], compare_op=ALU.not_equal, fill=1.0, base=0,
                                    pattern=[[-1, P]], channel_multiplier=1).then_inc(k.consts, 1)
            nc.gpsimd.affine_select(out=k.mask["causal"][:], in_=k.mask["causal"][:], compare_op=ALU.is_ge,
                                    fill=MASKED, base=0, pattern=[[P, 2], [-1, S]],
                                    channel_multiplier=1).then_inc(k.consts, 1)
            nc.gpsimd.affine_select(out=k.before[:], in_=k.before[:], compare_op=ALU.is_ge, fill=0.0, base=-1,
                                    pattern=[[P, 2], [-1, S]], channel_multiplier=1).then_inc(k.consts, 1)
            pool.wait_ge(k.consts, 12)
            nc.gpsimd.tensor_copy(k.identb[:], k.ident[:]).then_inc(k.consts, 1)
            nc.gpsimd.affine_select(out=k.mask["window"][:], in_=k.mask["causal"][:], compare_op=ALU.is_ge,
                                    fill=MASKED, base=P - 1, pattern=[[-P, 2], [1, S]],
                                    channel_multiplier=-1).then_inc(k.consts, 1)
    k.clear()


def weights(k, layer):
    nc = k.nc
    with nc.Block() as block:
        @block.sync
        def _(sp):
            if layer + 1 in LIST:
                sp.dma_start(k.arena[(layer + 1) % 2][:, 0:WIDTH[layer + 1]],
                             k.dram[f"w{layer + 1}"]).then_inc(k.w_in[layer + 1], 16)
            sp.wait_ge(k.w_in[layer], 16)


def norm_stats(k, dve, src):
    nc = k.nc
    for t in range(TT):
        nc.vector.bn_stats(k.st[:, t, :], src(t)).then_inc(k.stats, 1)
    for t in range(TT):
        dve.wait_ge(k.stats, t + 1)
        nc.vector.bn_aggr(k.mv[:, t, :], k.st[:, t, :]).then_inc(k.stats, 1)


def norm_rstd(k, act):
    nc = k.nc
    act.wait_ge(k.stats, 2 * TT)
    nc.scalar.activation(k.lnv[:], k.mv[:, :, 1], ACT.Ln, bias=k.eps[:, 0:1]).then_inc(k.chain_a, 1)
    act.wait_ge(k.chain_a, 1)
    nc.scalar.activation(k.rstd[:], k.lnv[:], ACT.Exp, scale=-0.5).then_inc(k.rstd_ready, 1)


def norm_apply(k, dve, src, dst):
    nc = k.nc
    dve.wait_ge(k.rstd_ready, 1)
    for t in range(TT):
        nc.vector.tensor_scalar(dst[:, t, :], src(t), k.mv[:, t, 0:1], k.rstd[:, t:t + 1],
                                ALU.subtract, ALU.mult).then_inc(k.h_ready, 1)


class Prep:

    def __init__(self, L):
        self.steps = []
        if L.selected:
            self.steps += [("gate", 0, "v"), ("selT", 0, "a"), ("hT", 0, "v"), ("hT", 1, "a")]
        else:
            self.steps += [("hT", 0, "v"), ("hT", 1, "a")]
        if L.normed:
            self.steps += [("qk", t, "v") for t in range(TT)]
            self.steps += [("v", (t, 0, L.NV), "v") for t in range(2 * L.nt)]
            self.steps += [("qkT", c, "a") for c in range(2 * L.nch)]
        else:
            self.steps += [("q", c, "v") for c in range(L.nch)]
            self.steps += [("k", c, "a") for c in range(L.nch)]
            self.steps += [("v", (t, c, min(BANK, L.NV)), "v") for t in range(2 * L.nt)
                           for c in range(0, L.NV, BANK)]

    def copied(self, n, engine):
        return sum(1 for s in self.steps[0:n] if s[2] == engine)

    def where(self, kind, arg=0):
        return next(n for n, s in enumerate(self.steps) if s[0] == kind and s[1] == arg)

    def all(self, kind):
        return max(n for n, s in enumerate(self.steps) if s[0] == kind) + 1


def attention(k, layer):
    nc, L = k.nc, ATTN[layer]
    prep = Prep(L)
    N = len(prep.steps)
    NT = 2 * L.TB
    A = L.at
    wq = k.w(layer, "wq", A).rearrange("p (c n) -> p c n", c=KD)
    wv = k.w(layer, "wv", A, L.kr).rearrange("p (c n) -> p c n", c=KD)
    wo = k.w(layer, "wo", A).rearrange("p (c n) -> p c n", c=L.NC)
    if not L.normed:
        wk = k.w(layer, "wk", A, L.kr).rearrange("p (c n) -> p c n", c=KD)
    kv_in = k.cT if L.ctx else k.hT
    kr = L.kr
    masked = L.mask is not None
    tiles = [(kt, qt) for kt in range(L.nt) for qt in range(L.nt) if not (masked and kt > qt)]
    NB = (L.NC * L.nt * P + BANK - 1) // BANK
    CB = L.NC // NB
    EV = NB + 1
    START = [L.G + 3, L.NS + 3]
    STEPS = START[1] + EV + 1
    Osb = k.V[:, :, L.NV:2 * L.NV] if L.normed else k.O
    qkn = k.O[:].rearrange("p t (j s) -> p t j s", s=32)
    Z, EX, GATE, R1, R2, RANK = (k.small[:, n, :] for n in range(6))
    selT = k.cT[:, 0, :]
    sel = k.cT[:, 1, :]
    scratch = k.res

    with nc.Fori(0, NPAIR) as pair:
        with nc.Block() as block:
            @block.sync
            def _(sp):
                if L.ctx:
                    sp.dma_start(k.cT[0:CR, :, :], k.dram["ctxT"][pair]).then_inc(k.ctx_in, 16)

            @block.gpsimd
            def _(pool):
                src = k.X[:, pair, :, :]
                if L.res_h:
                    pool.wait_ge(k.h_ready, TT)
                    nc.gpsimd.tensor_tensor(k.res[:], src, k.h[:], ALU.add).then_inc(k.res_ready, 1)
                    src = k.res[:]
                if L.out_bias:
                    bo = k.w(layer, "bo", A).unsqueeze(1).to_broadcast([P, TT, D])
                    if L.res_h:
                        pool.wait_ge(k.res_ready, 1)
                    nc.gpsimd.tensor_tensor(k.res[:], src, bo, ALU.add).then_inc(k.res_ready, 1)

            @block.scalar
            def _(act):
                norm_rstd(k, act)
                if L.normed:
                    act.wait_ge(k.stats, 4 * TT)
                    nc.scalar.activation(k.lnv[:], k.mv[:, :, 1], ACT.Ln, bias=k.eps[:, 0:1]).then_inc(k.chain_a, 1)
                    act.wait_ge(k.chain_a, 2)
                    nc.scalar.activation(k.rstd[:], k.lnv[:], ACT.Exp, scale=-0.5).then_inc(k.rstd_ready, 1)
                if L.selected:
                    act.wait_ge(k.chain_v, TT)
                    nc.scalar.activation(EX, Z, ACT.Exp, scale=-1.0).then_inc(k.rstd_ready, 1)
                for n, (kind, c, engine) in enumerate(prep.steps):
                    if engine != "a":
                        continue
                    src = k.ps[:, n % 8, :]
                    if kind == "qkT" and c == 0:
                        for m, buf in enumerate((k.nm, k.sums)):
                            flat = buf[:].rearrange("p a b -> p (a b)")
                            act.wait_ge(k.chain_v, 6 * (m + 1))
                            nc.scalar.activation(flat, flat, ACT.Sqrt).then_inc(k.chain_a, 1)
                    act.wait_ge(k.prod_ready, n + 1)
                    if kind == "hT":
                        if L.normed:
                            i = nc.scalar.activation(k.hT[:, c, :], src, ACT.Identity,
                                                     bias=k.w(layer, "lnb", A)[:, c:c + 1],
                                                     scale=k.w(layer, "lnw", A)[:, c:c + 1])
                        else:
                            i = nc.scalar.activation(k.hT[:, c, 0:NT], src[:, 0:NT], ACT.Copy)
                    elif kind == "selT":
                        i = nc.scalar.activation(selT, src, ACT.Copy)
                    elif kind == "k":
                        if L.qkv_bias:
                            i = nc.scalar.activation(k.KT[:, c, 0:NT], src[:, 0:NT], ACT.Identity,
                                                     bias=k.w(layer, "bk", A)[:, c:c + 1])
                        else:
                            i = nc.scalar.activation(k.KT[:, c, 0:NT], src[:, 0:NT], ACT.Copy)
                    elif kind == "qkT":
                        if c < L.nch:
                            i = nc.scalar.activation(k.QT[:, c, :], src, ACT.Copy, scale=L.scale)
                        else:
                            i = nc.scalar.activation(k.KT[:, c - L.nch, :], src, ACT.Copy)
                    i.then_inc(k.copied_a, 1)
                done = 0
                for s in range(STEPS):
                    if s < L.NS:
                        if L.normed:
                            act.wait_ge(k.scores_ready, 2 * s + 2)
                        if s >= 2:
                            act.wait_ge(k.pT_ready, 2 * (s - 1))
                        for j in range(2):
                            if not L.normed:
                                act.wait_ge(k.negmax_ready, 2 * s + j + 1)
                            for q in range(L.nt):
                                keys = P * (q + 1) if masked else L.TB
                                m = 2 * j + q
                                nc.scalar.activation(
                                    k.Pb[:, s % 2, m, 0:keys], k.ps[:, 2 * (s % 2) + j, q * S:q * S + keys],
                                    ACT.Exp, bias=0.0 if L.normed else k.nm[:, s, m:m + 1],
                                    accum_out=k.sums[:, s, m:m + 1]).then_inc(k.probs_ready, 1)
                    u = s - 1
                    if 0 <= u < L.NS:
                        act.wait_ge(k.pT_ready, 2 * u + 2)
                        if u >= 2:
                            act.wait_ge(k.av_ready, u - 1)
                        nc.scalar.activation(k.PT[:, u % 2, 1, 0:len(tiles) * P], k.ps[:, 5, 0:len(tiles) * P],
                                             ACT.Copy).then_inc(k.pT_copied_a, 1)
                    for a in range(2):
                        e = s - START[a]
                        if 0 <= e < NB:
                            act.wait_ge(k.out_ready, a * EV + e + 1)
                            w = L.nt * P
                            nc.scalar.activation(
                                k.QT[:, e * CB:(e + 1) * CB, a * L.TB:a * L.TB + w],
                                k.ps[:, 7, 0:CB * w].rearrange("p (c n) -> p c n", c=CB), ACT.Copy
                            ).then_inc(k.oT_copied, 1)

            @block.tensor
            def _(pe):
                for n, (kind, c, engine) in enumerate(prep.steps):
                    out = k.ps[:, n % 8, :]
                    if n >= 8:
                        pe.wait_ge(k.copied_v if prep.steps[n - 8][2] == "v" else k.copied_a,
                                   prep.copied(n - 7, prep.steps[n - 8][2]))
                    if kind == "hT" and not L.selected:
                        if c == 0:
                            pe.wait_ge(k.h_ready, 2 * TT if L.normed else TT)
                        hs = k.res if L.normed else k.h
                        if L.normed:
                            hs = k.KT[:, 6:8, :].rearrange("p c (t d) -> p (c t) d", d=D)
                        for t in range(TT):
                            i = nc.tensor.transpose(out[:, t * P:(t + 1) * P], hs[:, t, c * P:(c + 1) * P], k.ident[:])
                    elif kind == "gate":
                        pe.wait_ge(k.sel_ready, TT)
                        for t in range(TT):
                            i = nc.tensor.transpose(out[:, t * P:(t + 1) * P], k.O[:, t, 0:P], k.ident[:])
                    elif kind == "selT":
                        pe.wait_ge(k.sel_ready, 2 * TT)
                        for t in range(TT):
                            i = nc.tensor.transpose(out[:, t * P:(t + 1) * P], sel[:, t * P:(t + 1) * P], k.ident[:])
                    elif kind == "hT":
                        for a in range(2):
                            for q in range(2):
                                t = 2 * a + q
                                i = nc.tensor.matmul(out[:, a * P:(a + 1) * P], k.h[:, t, c * P:(c + 1) * P],
                                                     sel[:, t * P:(t + 1) * P], start=q == 0, stop=q == 1)
                    elif kind == "qkT":
                        if c == 0:
                            pe.wait_ge(k.sel_ready, 1 + TT)
                        j = 4 * c * 32
                        for t in range(TT):
                            i = nc.tensor.transpose(out[:, t * P:(t + 1) * P], k.O[:, t, j:j + P], k.ident[:])
                    else:
                        if kind in ("q", "qk") and c == 0:
                            pe.wait_ge(k.copied_v, prep.copied(prep.all("hT"), "v"))
                            pe.wait_ge(k.copied_a, prep.copied(prep.all("hT"), "a"))
                        if kind == "k" and c == 0 and L.ctx:
                            pe.wait_ge(k.ctx_in, 16)
                        for m in range(KD):
                            if kind == "q":
                                i = nc.tensor.matmul(out[:, 0:NT], wq[:, m, c * P:(c + 1) * P], k.hT[:, m, 0:NT],
                                                     start=m == 0, stop=m == KD - 1)
                            elif kind == "k":
                                i = nc.tensor.matmul(out[:, 0:NT], wk[:, m, c * P:(c + 1) * P], kv_in[0:kr, m, 0:NT],
                                                     start=m == 0, stop=m == KD - 1)
                            elif kind == "qk":
                                i = nc.tensor.matmul(out, k.hT[:, m, c * P:(c + 1) * P], wq[:, m, :],
                                                     start=m == 0, stop=m == KD - 1)
                            else:
                                t, c0, w = c
                                i = nc.tensor.matmul(out[:, 0:w], kv_in[0:kr, m, t * P:(t + 1) * P],
                                                     wv[:, m, c0:c0 + w], start=m == 0, stop=m == KD - 1)
                    i.then_inc(k.prod_ready, 1)
                pe.wait_ge(k.copied_v, prep.copied(N, "v"))
                pe.wait_ge(k.copied_a, prep.copied(N, "a"))
                for s in range(STEPS):
                    if s < L.NS:
                        a, g = divmod(s, L.G)
                        if s >= 2:
                            pe.wait_ge(k.probs_ready, L.E * (s - 1))
                        for j in range(2):
                            h = 2 * g + j
                            r, c = L.row(h), h // L.per
                            bank = k.ps[:, 2 * (s % 2) + j, :]
                            if masked:
                                nc.tensor.matmul(bank, k.identb[:], k.mask[L.mask][:].rearrange("p q n -> p (q n)"),
                                                 start=True, stop=False, skip_group_check=True)
                            for q in range(L.nt):
                                keys = P * (q + 1) if masked else L.TB
                                i = nc.tensor.matmul(
                                    bank[:, q * S:q * S + keys],
                                    k.QT[r:r + L.dh, c, a * L.TB + q * P:a * L.TB + (q + 1) * P],
                                    k.KT[r:r + L.dh, c, a * L.TB:a * L.TB + keys],
                                    start=not masked, stop=True, skip_group_check=masked)
                            i.then_inc(k.scores_ready, 1)
                    u = s - 1
                    if 0 <= u < L.NS:
                        for j in range(2):
                            pe.wait_ge(k.probs_ready, L.E * u + (j + 1) * L.nt)
                            if u >= 1:
                                pe.wait_ge(k.pT_copied_a if j else k.pT_copied_v, u)
                            for n, (kt, qt) in enumerate(tiles):
                                i = nc.tensor.transpose(k.ps[:, 4 + j, n * P:(n + 1) * P],
                                                        k.Pb[:, u % 2, 2 * j + qt, kt * P:(kt + 1) * P], k.ident[:])
                            i.then_inc(k.pT_ready, 1)
                    u = s - 2
                    if 0 <= u < L.NS:
                        a, g = divmod(u, L.G)
                        pe.wait_ge(k.pT_copied_v, u + 1)
                        pe.wait_ge(k.pT_copied_a, u + 1)
                        if u >= 1:
                            pe.wait_ge(k.av_normed, u)
                        for j in range(2):
                            v0 = (2 * g + j) // L.rep * L.dh
                            for qt in range(L.nt):
                                o = (2 * j + qt) * L.dh
                                mine = [(n, kt) for n, (kt, q) in enumerate(tiles) if q == qt]
                                for n, kt in mine:
                                    i = nc.tensor.matmul(k.ps[:, 6, o:o + L.dh], k.PT[:, u % 2, j, n * P:(n + 1) * P],
                                                         k.V[:, a * L.nt + kt, v0:v0 + L.dh],
                                                         start=(n, kt) == mine[0], stop=(n, kt) == mine[-1])
                        i.then_inc(k.av_ready, 1)
                    for a in range(2):
                        e = s - START[a]
                        if 0 <= e < NB:
                            if e == 0:
                                pe.wait_ge(k.av_normed, (a + 1) * L.G)
                                if a:
                                    pe.wait_ge(k.x_done, 1)
                            else:
                                pe.wait_ge(k.oT_copied, a * NB + e)
                            for c in range(CB):
                                for q in range(L.nt):
                                    o = (c * L.nt + q) * P
                                    ch = (e * CB + c) * P
                                    i = nc.tensor.transpose(k.ps[:, 7, o:o + P], Osb[:, a * L.nt + q, ch:ch + P],
                                                            k.ident[:])
                            i.then_inc(k.out_ready, 1)
                        if e == NB:
                            pe.wait_ge(k.oT_copied, (a + 1) * NB)
                            for q in range(L.nt):
                                for c in range(L.NC):
                                    o = a * L.TB + q * P
                                    i = nc.tensor.matmul(k.ps[:, 7, q * D:(q + 1) * D], k.QT[:, c, o:o + P], wo[:, c, :],
                                                         start=c == 0, stop=c == L.NC - 1)
                            i.then_inc(k.out_ready, 1)
                            if L.selected:
                                pe.wait_ge(k.sel_ready, 2 * TT + a + 1)
                                for q in range(2):
                                    t = 2 * a + q
                                    i = nc.tensor.matmul(k.ps[:, 7, q * D:(q + 1) * D], selT[:, t * P:(t + 1) * P],
                                                         k.O[:, 2 + a, 0:D], start=True, stop=True)
                                i.then_inc(k.res_ready, 1)

            @block.vector
            def _(dve):
                norm_stats(k, dve, lambda t: k.X[:, pair, t, :])
                norm_apply(k, dve, lambda t: k.X[:, pair, t, :], k.h)
                if L.normed:
                    h2 = k.KT[:, 6:8, :].rearrange("p c (t d) -> p (c t) d", d=D)
                    for t in range(TT):
                        dve.wait_ge(k.h_ready, t + 1)
                        nc.vector.bn_stats(k.st[:, t, :], k.h[:, t, :]).then_inc(k.stats, 1)
                    dve.wait_ge(k.h_ready, TT)
                    for t in range(TT):
                        dve.wait_ge(k.stats, 2 * TT + t + 1)
                        nc.vector.bn_aggr(k.mv[:, t, :], k.st[:, t, :]).then_inc(k.stats, 1)
                    dve.wait_ge(k.rstd_ready, 2)
                    for t in range(TT):
                        nc.vector.tensor_scalar(h2[:, t, :], k.h[:, t, :], k.mv[:, t, 0:1], k.rstd[:, t:t + 1],
                                                ALU.subtract, ALU.mult).then_inc(k.h_ready, 1)
                    nc.vector.memset(k.O[:], 0.0).then_inc(k.sel_ready, 1)
                if L.selected:
                    for t in range(TT):
                        dve.wait_ge(k.h_ready, t + 1)
                        nc.vector.tensor_tensor_reduce(scratch[:, t, :], k.h[:, t, :], k.w(layer, "wg", A), 1.0, 0.0,
                                                       ALU.mult, ALU.add, Z[:, t:t + 1]).then_inc(k.chain_v, 1)
                    dve.wait_ge(k.rstd_ready, 2)
                    nc.vector.tensor_scalar(R1, EX, 1.0, None, ALU.add).then_inc(k.chain_v, 1)
                    dve.wait_ge(k.chain_v, TT + 1)
                    nc.vector.reciprocal(GATE, R1).then_inc(k.chain_v, 1)
                    dve.wait_ge(k.chain_v, TT + 2)
                    for t in range(TT):
                        nc.vector.tensor_copy(k.O[:, t, 0:P], GATE[:, t:t + 1].to_broadcast([P, P])).then_inc(k.sel_ready, 1)
                for n, (kind, c, engine) in enumerate(prep.steps):
                    if engine != "v":
                        continue
                    src = k.ps[:, n % 8, :]
                    dve.wait_ge(k.prod_ready, n + 1)
                    if kind == "gate":
                        for t in range(TT):
                            G = src[:, (t // 2) * S:(t // 2 + 1) * S]
                            nc.vector.tensor_scalar(k.O[:, t, 256:512], G, GATE[:, t:t + 1], None, ALU.is_gt, ALU.add,
                                                    accum_out=R1[:, t:t + 1]).then_inc(k.chain_v, 1)
                            nc.vector.scalar_tensor_tensor(out=k.O[:, t, 512:768], in0=G, scalar=GATE[:, t:t + 1],
                                                           in1=k.before[:, t % 2, :], op0=ALU.is_equal, op1=ALU.mult,
                                                           accum_out=R2[:, t:t + 1]).then_inc(k.chain_v, 1)
                        dve.wait_ge(k.chain_v, 3 * TT + 2)
                        nc.vector.tensor_tensor(RANK, R1, R2, ALU.add).then_inc(k.chain_v, 1)
                        dve.wait_ge(k.chain_v, 3 * TT + 3)
                        for t in range(TT):
                            i = nc.vector.tensor_scalar(sel[:, t * P:(t + 1) * P], k.iota[:], RANK[:, t:t + 1], None,
                                                        ALU.is_equal)
                            i.then_inc(k.sel_ready, 1)
                        nc.vector.tensor_copy(k.small[:, 6, 0:1], src[:, 0:1]).then_inc(k.copied_v, 1)
                        continue
                    if kind == "hT":
                        if L.normed:
                            i = nc.vector.tensor_scalar(k.hT[:, c, :], src, k.w(layer, "lnw", A)[:, c:c + 1],
                                                        k.w(layer, "lnb", A)[:, c:c + 1], ALU.mult, ALU.add)
                        else:
                            i = nc.vector.tensor_copy(k.hT[:, c, 0:NT], src[:, 0:NT])
                    elif kind == "q":
                        if L.qkv_bias:
                            i = nc.vector.tensor_scalar(k.QT[:, c, 0:NT], src[:, 0:NT], k.w(layer, "bq", A)[:, c:c + 1],
                                                        L.scale, ALU.add, ALU.mult)
                        else:
                            i = nc.vector.tensor_scalar(k.QT[:, c, 0:NT], src[:, 0:NT], L.scale, None, ALU.mult)
                    elif kind == "v":
                        t, c0, w = c
                        if L.qkv_bias:
                            i = nc.vector.tensor_tensor(k.V[:, t, c0:c0 + w], src[:, 0:w],
                                                        k.w(layer, "bv", A)[:, c0:c0 + w], ALU.add)
                        else:
                            i = nc.vector.tensor_copy(k.V[:, t, c0:c0 + w], src[:, 0:w])
                    elif kind == "qk":
                        i = nc.vector.tensor_tensor(k.PT[:, c // 2, c % 2, :], src, k.w(layer, "bqk", A), ALU.add)
                    i.then_inc(k.copied_v, 1)
                    if kind == "qk":
                        qk, sq = k.PT[:, c // 2, c % 2, :], k.Pb[:, c // 2, 2 * (c % 2):2 * (c % 2) + 2, :]
                        dve.wait_ge(k.copied_v, prep.copied(n + 1, "v"))
                        nc.vector.tensor_tensor(sq, qk.rearrange("p (a b) -> p a b", a=2),
                                                qk.rearrange("p (a b) -> p a b", a=2), ALU.mult).then_inc(k.chain_v, 1)
                        dve.wait_ge(k.chain_v, 3 * c + 1)
                        ss = k.nm[:, 8 * (c % 2):8 * (c % 2) + 8, :].rearrange("p a b -> p (a b)")
                        if c >= 2:
                            ss = k.sums[:, 8 * (c % 2):8 * (c % 2) + 8, :].rearrange("p a b -> p (a b)")
                        nc.vector.tensor_reduce(ss, sq.rearrange("p a (j d) -> p (a j) d", d=L.dh), AX.X,
                                                ALU.add).then_inc(k.chain_v, 1)
                        dve.wait_ge(k.chain_v, 3 * c + 2)
                        nc.vector.tensor_scalar(ss, ss, 1e-24, None, ALU.max).then_inc(k.chain_v, 1)
                    if kind == "v" and L.normed and c[0] == TT - 1:
                        for m, buf in enumerate((k.nm, k.sums)):
                            dve.wait_ge(k.chain_a, 3 + m)
                            flat = buf[:].rearrange("p a b -> p (a b)")
                            nc.vector.reciprocal(flat, flat).then_inc(k.chain_v, 1)
                            dve.wait_ge(k.chain_v, 3 * TT + m + 1)
                            if m == 0:
                                dve.wait_ge(k.sel_ready, 1)
                            for t in range(2 * m, 2 * m + 2):
                                qk = k.PT[:, t // 2, t % 2, :].rearrange("p (j d) -> p j d", d=L.dh)
                                rn = buf[:, 8 * (t % 2):8 * (t % 2) + 8, :].rearrange("p a b -> p (a b)")
                                nc.vector.tensor_tensor(qkn[:, t, :, 0:L.dh], qk,
                                                        rn.unsqueeze(2).to_broadcast([P, 2 * L.H, L.dh]),
                                                        ALU.mult).then_inc(k.sel_ready, 1)
                for s in range(STEPS):
                    if s < L.NS and not L.normed:
                        for j in range(2):
                            dve.wait_ge(k.scores_ready, 2 * s + j + 1)
                            src = k.ps[:, 2 * (s % 2) + j, 0:L.nt * L.TB].rearrange("p (q n) -> p q n", q=L.nt)
                            nc.vector.tensor_reduce(k.nm[:, s, 2 * j:2 * j + L.nt], src, AX.X, ALU.max,
                                                    negate=True).then_inc(k.negmax_ready, 1)
                    u = s - 1
                    if 0 <= u < L.NS:
                        dve.wait_ge(k.pT_ready, 2 * u + 1)
                        if u >= 2:
                            dve.wait_ge(k.av_ready, u - 1)
                        nc.vector.tensor_copy(k.PT[:, u % 2, 0, 0:len(tiles) * P],
                                              k.ps[:, 4, 0:len(tiles) * P]).then_inc(k.pT_copied_v, 1)
                    u = s - 2
                    if 0 <= u < L.NS:
                        a, g = divmod(u, L.G)
                        dve.wait_ge(k.probs_ready, L.E * (u + 1))
                        sm = k.sums[:, u, :].rearrange("p (j q) -> p j q", j=2)[:, :, 0:L.nt]
                        rv = k.rs[:, u, :].rearrange("p (j q) -> p j q", j=2)[:, :, 0:L.nt]
                        nc.vector.reciprocal(rv, sm).then_inc(k.rsum_ready, 1)
                        dve.wait_ge(k.rsum_ready, u + 1)
                        dve.wait_ge(k.av_ready, u + 1)
                        for q in range(L.nt):
                            o = Osb[:, a * L.nt + q, 2 * g * L.dh:(2 * g + 2) * L.dh].rearrange("p (j d) -> p j d", j=2)
                            av = k.ps[:, 6, 0:4 * L.dh].rearrange(
                                "p (j q d) -> p j q d", j=2, q=2)[:, :, q, :]
                            i = nc.vector.tensor_tensor(o, av, rv[:, :, q].unsqueeze(2).to_broadcast([P, 2, L.dh]),
                                                        ALU.mult)
                        i.then_inc(k.av_normed, 1)
                    for a in range(2):
                        if s - START[a] == NB:
                            dve.wait_ge(k.out_ready, (a + 1) * EV)
                            if L.selected:
                                nc.vector.tensor_copy(k.O[:, 2 + a, 0:D], k.ps[:, 7, 0:D]).then_inc(k.sel_ready, 1)
                                dve.wait_ge(k.res_ready, a + 1)
                                for q in range(2):
                                    t = 2 * a + q
                                    i = nc.vector.scalar_tensor_tensor(
                                        out=k.X[:, pair, t, :], in0=k.ps[:, 7, q * D:(q + 1) * D],
                                        scalar=GATE[:, t:t + 1], in1=k.X[:, pair, t, :], op0=ALU.mult, op1=ALU.add)
                            else:
                                dve.wait_ge(k.res_ready, L.res_h + L.out_bias)
                                i = nc.vector.tensor_tensor(
                                    k.X[:, pair, 2 * a:2 * a + 2, :], k.ps[:, 7, :].rearrange("p (q d) -> p q d", q=2),
                                    k.res[:, 2 * a:2 * a + 2, :], ALU.add)
                            i.then_inc(k.x_done, 1)
        k.clear()


def mixer(k, layer):
    nc = k.nc
    wr, wk, wv = (k.w(layer, n, MIX).rearrange("p (c n) -> p c n", c=KD) for n in ("wr", "wk", "wv"))
    mur, muk = k.w(layer, "mur", MIX), k.w(layer, "muk", MIX)
    XR, XK = k.QT[:, 0:KD, :], k.KT[:, 0:KD, :]
    relu = k.QT[:, KD:2 * KD, :]
    kact = k.KT[:, KD:2 * KD, :]
    ez = k.O[:, :, 0:D]
    r = k.O[:, :, D:2 * D]
    prod = k.O[:, :, 2 * D:3 * D]
    omr, omk = k.small[:, 0, 0:KD], k.small[:, 1, 0:KD]

    def tok(bank):
        return k.ps[:, bank, :].rearrange("p (q d) -> p q d", q=2)

    with nc.Fori(0, NPAIR) as pair:
        with nc.Block() as block:
            @block.scalar
            def _(act):
                norm_rstd(k, act)
                act.wait_ge(k.prod_ready, 2)
                nc.scalar.activation(k.hT[:, 1, :], k.ps[:, 1, :], ACT.Copy).then_inc(k.copied_a, 1)
                for c in range(KD):
                    act.wait_ge(k.prod_ready, 3 + c)
                    nc.scalar.activation(relu[:, c, :], k.ps[:, 2 + c, :], ACT.Relu).then_inc(k.chain_a, 1)
                    act.wait_ge(k.chain_a, 2 + c)
                    nc.scalar.activation(kact[:, c, :], relu[:, c, :], ACT.Square).then_inc(k.copied_a, 1)
                for b in range(2):
                    act.wait_ge(k.prod_ready, 5 + b)
                    nc.scalar.activation(ez[:, 2 * b:2 * b + 2, :], tok(4 + b), ACT.Exp,
                                         scale=-1.0).then_inc(k.copied_a, 1)

            @block.tensor
            def _(pe):
                for c in range(KD):
                    if c == 0:
                        pe.wait_ge(k.h_ready, TT)
                    for t in range(TT):
                        i = nc.tensor.transpose(k.ps[:, c, t * P:(t + 1) * P], k.h[:, t, c * P:(c + 1) * P], k.ident[:])
                    i.then_inc(k.prod_ready, 1)
                pe.wait_ge(k.sel_ready, 2)
                for c in range(KD):
                    for m in range(KD):
                        i = nc.tensor.matmul(k.ps[:, 2 + c, :], wk[:, m, c * P:(c + 1) * P], XK[:, m, :],
                                             start=m == 0, stop=m == KD - 1)
                    i.then_inc(k.prod_ready, 1)
                pe.wait_ge(k.sel_ready, 4)
                for t in range(TT):
                    for m in range(KD):
                        i = nc.tensor.matmul(tok(4 + t // 2)[:, t % 2, :], XR[:, m, t * P:(t + 1) * P], wr[:, m, :],
                                             start=m == 0, stop=m == KD - 1)
                    if t % 2:
                        i.then_inc(k.prod_ready, 1)
                pe.wait_ge(k.copied_a, 3)
                for t in range(TT):
                    for m in range(KD):
                        i = nc.tensor.matmul(tok(6 + t // 2)[:, t % 2, :], kact[:, m, t * P:(t + 1) * P], wv[:, m, :],
                                             start=m == 0, stop=m == KD - 1)
                    if t % 2:
                        i.then_inc(k.prod_ready, 1)

            @block.vector
            def _(dve):
                nc.vector.tensor_scalar(omr, mur, -1.0, 1.0, ALU.mult, ALU.add).then_inc(k.chain_v, 1)
                nc.vector.tensor_scalar(omk, muk, -1.0, 1.0, ALU.mult, ALU.add).then_inc(k.chain_v, 1)
                norm_stats(k, dve, lambda t: k.X[:, pair, t, :])
                norm_apply(k, dve, lambda t: k.X[:, pair, t, :], k.h)
                dve.wait_ge(k.prod_ready, 1)
                nc.vector.tensor_copy(k.hT[:, 0, :], k.ps[:, 0, :]).then_inc(k.copied_v, 1)
                dve.wait_ge(k.copied_v, 1)
                dve.wait_ge(k.copied_a, 1)
                n = 2
                for to, mu, om in ((XK, muk, omk), (XR, mur, omr)):
                    for c in range(KD):
                        nc.vector.tensor_scalar(to[:, c, :], k.hT[:, c, :], mu[:, c:c + 1], None,
                                                ALU.mult).then_inc(k.chain_v, 1)
                    for c in range(KD):
                        n += 1
                        dve.wait_ge(k.chain_v, n)
                        x = to[:, c, :].rearrange("p (b s) -> p b s", b=2)[:, :, 1:S]
                        before = k.hT[:, c, :].rearrange("p (b s) -> p b s", b=2)[:, :, 0:S - 1]
                        nc.vector.scalar_tensor_tensor(out=x, in0=before, scalar=om[:, c:c + 1], in1=x, op0=ALU.mult,
                                                       op1=ALU.add).then_inc(k.sel_ready, 1)
                for b in range(2):
                    two = slice(2 * b, 2 * b + 2)
                    dve.wait_ge(k.copied_a, 4 + b)
                    nc.vector.tensor_scalar(ez[:, two, :], ez[:, two, :], 1.0, None, ALU.add).then_inc(k.chain_v, 1)
                    dve.wait_ge(k.chain_v, 7 + 3 * b)
                    nc.vector.reciprocal(r[:, two, :], ez[:, two, :]).then_inc(k.chain_v, 1)
                    dve.wait_ge(k.chain_v, 8 + 3 * b)
                    dve.wait_ge(k.prod_ready, 7 + b)
                    nc.vector.tensor_tensor(prod[:, two, :], tok(6 + b), r[:, two, :], ALU.mult).then_inc(k.chain_v, 1)
                    dve.wait_ge(k.chain_v, 9 + 3 * b)
                    nc.vector.tensor_tensor(k.X[:, pair, two, :], k.X[:, pair, two, :], prod[:, two, :],
                                            ALU.add).then_inc(k.x_done, 1)
        k.clear()


class Route:

    def __init__(self, k):
        self.lg, self.e, self.pr = (k.small[:, 8 * n:8 * n + 8, :].rearrange("p a b -> p (a b)").rearrange(
            "p (t e) -> p t e", e=NE) for n in range(3))
        self.mx, self.sm, self.ri = (k.rs[:, n, :] for n in range(3))
        self.rank = k.nm[:, 0:8, :].rearrange("p a b -> p (a b)").rearrange("p (t e) -> p t e", e=NE)
        self.G = k.Pb[:, 0, 0, :].rearrange("p (t e j) -> p t e j", t=TT, e=NE)
        self.Q = k.Pb[:, 0, 1, :].rearrange("p (t e j) -> p t e j", t=TT, e=NE)

    def vector(self, k, dve, logits, pr):
        nc = k.nc
        spread = [P, TT, NE]
        nc.vector.tensor_reduce(self.mx, logits, AX.X, ALU.max, negate=True).then_inc(k.chain_v, 1)
        dve.wait_ge(k.chain_v, 1)
        nc.vector.tensor_tensor(self.lg, logits, self.mx.unsqueeze(2).to_broadcast(spread), ALU.add).then_inc(k.chain_v, 1)
        dve.wait_ge(k.chain_a, 2)
        nc.vector.tensor_reduce(self.sm, self.e, AX.X, ALU.add).then_inc(k.chain_v, 1)
        dve.wait_ge(k.chain_v, 3)
        nc.vector.reciprocal(self.ri, self.sm).then_inc(k.chain_v, 1)
        dve.wait_ge(k.chain_v, 4)
        nc.vector.tensor_tensor(pr, self.e, self.ri.unsqueeze(2).to_broadcast(spread), ALU.mult).then_inc(k.chain_v, 1)
        dve.wait_ge(k.chain_v, 5)
        for t in range(TT):
            other = pr[:, t, :].unsqueeze(1).to_broadcast([P, NE, NE])
            own = pr[:, t, :].unsqueeze(2).to_broadcast([P, NE, NE])
            nc.vector.tensor_tensor(self.G[:, t], other, own, ALU.is_gt)
            nc.vector.tensor_tensor(self.Q[:, t], other, own, ALU.is_equal).then_inc(k.chain_v, 1)
        dve.wait_ge(k.chain_v, 9)
        q = self.Q.rearrange("p t e j -> p t (e j)")
        nc.vector.tensor_tensor(q, q, k.first8[:].rearrange("p e j -> p (e j)").unsqueeze(1).to_broadcast([P, TT, NE * NE]),
                                ALU.mult).then_inc(k.chain_v, 1)
        dve.wait_ge(k.chain_v, 10)
        g = self.G.rearrange("p t e j -> p t (e j)")
        nc.vector.tensor_tensor(g, g, q, ALU.add).then_inc(k.chain_v, 1)
        dve.wait_ge(k.chain_v, 11)
        nc.vector.tensor_reduce(self.rank.rearrange("p t e -> p (t e)"),
                                self.G.rearrange("p t e j -> p (t e) j"), AX.X, ALU.add).then_inc(k.chain_v, 1)
        dve.wait_ge(k.chain_v, 12)

    def scalar(self, k, act):
        act.wait_ge(k.chain_v, 2)
        k.nc.scalar.activation(self.e, self.lg, ACT.Exp).then_inc(k.chain_a, 1)


def composed(k, layer):
    nc = k.nc
    at, n = MOE2["wc"]
    wc = k.arena[layer % 2][:, at:at + n].rearrange("p (m n) -> p m n", m=KD)
    wg = k.w(layer, "wg", MOE2).rearrange("p (m e) -> p m e", m=KD)
    slots = [k.QT[:].rearrange("p c n -> p (c n)"), k.KT[:].rearrange("p c n -> p (c n)"),
             k.V[:].rearrange("p c n -> p (c n)"), k.O[:].rearrange("p c n -> p (c n)")]
    NSLOT = len(slots)
    with nc.Block() as block:
        @block.sync
        def _(sp):
            for e in range(NE):
                if e >= NSLOT:
                    sp.wait_ge(k.prod_ready, KD * (e - NSLOT + 1))
                sp.dma_start(slots[e % NSLOT], k.dram["moe2"][e]).then_inc(k.expert_in[e], 16)

        @block.tensor
        def _(pe):
            for e in range(NE):
                pe.wait_ge(k.expert_in[e], 16)
                up = slots[e % NSLOT][:, 0:FC * D].rearrange("p (f d) -> p f d", f=FC)
                down = slots[e % NSLOT][:, FC * D:].rearrange("p (f d) -> p f d", f=FC)
                for m in range(KD):
                    if e >= 4:
                        pe.wait_ge(k.copied_a if m else k.copied_v, e - 3)
                    for f in range(FC):
                        i = nc.tensor.matmul(k.ps[:, (KD * e + m) % 8, 0:D], up[:, f, m * P:(m + 1) * P], down[:, f, :],
                                             start=f == 0, stop=f == FC - 1)
                    i.then_inc(k.prod_ready, 1)

        @block.vector
        def _(dve):
            for e in range(NE):
                dve.wait_ge(k.prod_ready, KD * e + 1)
                nc.vector.tensor_copy(wc[:, 0, e * D:(e + 1) * D], k.ps[:, KD * e % 8, 0:D]).then_inc(k.copied_v, 1)

        @block.scalar
        def _(act):
            for e in range(NE):
                act.wait_ge(k.prod_ready, KD * e + 2)
                nc.scalar.activation(wc[:, 1, e * D:(e + 1) * D], k.ps[:, (KD * e + 1) % 8, 0:D],
                                     ACT.Copy).then_inc(k.copied_a, 1)
    k.clear()

    route = Route(k)
    mask = k.sums[:, 0:8, :].rearrange("p a b -> p (a b)").rearrange("p (t e) -> p t e", e=NE)
    with nc.Fori(0, NPAIR) as pair:
        with nc.Block() as block:
            @block.scalar
            def _(act):
                norm_rstd(k, act)
                act.wait_ge(k.prod_ready, 2)
                nc.scalar.activation(k.hT[:, 1, :], k.ps[:, 1, :], ACT.Copy).then_inc(k.copied_a, 1)
                route.scalar(k, act)

            @block.tensor
            def _(pe):
                for c in range(KD):
                    if c == 0:
                        pe.wait_ge(k.h_ready, TT)
                    for t in range(TT):
                        i = nc.tensor.transpose(k.ps[:, c, t * P:(t + 1) * P], k.h[:, t, c * P:(c + 1) * P], k.ident[:])
                    i.then_inc(k.prod_ready, 1)
                pe.wait_ge(k.copied_v, 1)
                pe.wait_ge(k.copied_a, 1)
                for t in range(TT):
                    for m in range(KD):
                        i = nc.tensor.matmul(k.ps[:, 2, t * NE:(t + 1) * NE], k.hT[:, m, t * P:(t + 1) * P], wg[:, m, :],
                                             start=m == 0, stop=m == KD - 1)
                i.then_inc(k.prod_ready, 1)
                n = 0
                for e in range(0, NE, 2):
                    for t in range(TT):
                        if n >= 5:
                            pe.wait_ge(k.x_done, 2 * (n - 4))
                        for m in range(KD):
                            i = nc.tensor.matmul(k.ps[:, 3 + n % 5, :], k.hT[:, m, t * P:(t + 1) * P],
                                                 wc[:, m, e * D:(e + 2) * D], start=m == 0, stop=m == KD - 1)
                        i.then_inc(k.out_ready, 1)
                        n += 1

            @block.vector
            def _(dve):
                norm_stats(k, dve, lambda t: k.X[:, pair, t, :])
                norm_apply(k, dve, lambda t: k.X[:, pair, t, :], k.h)
                dve.wait_ge(k.prod_ready, 1)
                nc.vector.tensor_copy(k.hT[:, 0, :], k.ps[:, 0, :]).then_inc(k.copied_v, 1)
                dve.wait_ge(k.prod_ready, 3)
                route.vector(k, dve, k.ps[:, 2, 0:TT * NE].rearrange("p (t e) -> p t e", e=NE), route.pr)
                nc.vector.tensor_scalar(mask, route.rank, 1.5, None, ALU.is_lt).then_inc(k.chain_v, 1)
                dve.wait_ge(k.chain_v, 13)
                n = 0
                for e in range(0, NE, 2):
                    for t in range(TT):
                        dve.wait_ge(k.out_ready, n + 1)
                        for i in range(2):
                            done = 2 * n - 7 if i == 0 else 2 * n + 1
                            if done > 0:
                                dve.wait_ge(k.x_done, done)
                            nc.vector.scalar_tensor_tensor(
                                out=k.X[:, pair, t, :], in0=k.ps[:, 3 + n % 5, i * D:(i + 1) * D],
                                scalar=mask[:, t, e + i:e + i + 1], in1=k.X[:, pair, t, :], op0=ALU.mult,
                                op1=ALU.add).then_inc(k.x_done, 1)
                        n += 1
        k.clear()


def capacity(k, layer):
    nc = k.nc
    U32 = mybir.dt.uint32
    NTT = T // P
    xb, yb = k.xb, k.yb
    wr = k.w(layer, "wr", MOE3).rearrange("p (m e) -> p m e", m=KD)
    bias = k.w(layer, "bias", MOE3)
    HB = k.KT[:].rearrange("p c n -> p (c n)").rearrange("p (t d) -> p t d", d=D)
    HP = HB.rearrange("p (g t) d -> p g t d", t=TT)
    flat = k.res[:].rearrange("p t d -> p (t d)")

    def part(n):
        return flat[:, n * NTT * NE:(n + 1) * NTT * NE].rearrange("p (t e) -> p t e", e=NE)

    PR, M1, M2, ALLM, POS, SLOT, TMP, BASE = (part(n) for n in range(8))
    sk = [k.st2[:, n, :] for n in range(2)]
    wk = [k.st2[:, 2 + n, :] for n in range(2)]
    tmp = k.st2[:, 4, :]
    idx = [k.idx[:, n, :] for n in range(4)]
    A0, A1 = k.arena[(layer + 1) % 2], k.arena[layer % 2]
    first = MOE3_WIDTH
    slots = [A0[:, 0:2 * FC * D], A0[:, 2 * FC * D:4 * FC * D], A1[:, first:first + 2 * FC * D],
             k.QT[:].rearrange("p c n -> p (c n)"), k.O[:].rearrange("p c n -> p (c n)")]
    NSLOT = len(slots)
    zero = k.V[:].rearrange("p c n -> p (c n)")

    with nc.Block() as block:
        @block.vector
        def _(dve):
            nc.vector.memset(zero, 0.0).then_inc(k.zeroed, 1)

        @block.sync
        def _(sp):
            sp.wait_ge(k.zeroed, 1)
            for n in range(2):
                sp.dma_start(xb.rearrange("(p c) d -> p (c d)", p=P)[:, n * 4096:(n + 1) * 4096],
                             zero).then_inc(k.zero_in, 16)
            for e in range(NSLOT):
                sp.dma_start(slots[e], k.dram["moe3"][e]).then_inc(k.expert_in[NE + e], 16)

    route = Route(k)
    with nc.Fori(0, NPAIR) as pair:
        with nc.Block() as block:
            pp = [x.rearrange("p (g t) e -> p g t e", t=TT)[:, pair, :, :] for x in (PR, M1, M2)]

            @block.scalar
            def _(act):
                norm_rstd(k, act)
                act.wait_ge(k.prod_ready, 2)
                nc.scalar.activation(k.hT[:, 1, :], k.ps[:, 1, :], ACT.Copy).then_inc(k.copied_a, 1)
                route.scalar(k, act)

            @block.gpsimd
            def _(pool):
                pool.wait_ge(k.h_ready, TT)
                nc.gpsimd.tensor_copy(HP[:, pair, :, :], k.h[:]).then_inc(k.res_ready, 1)
                nc.gpsimd.tensor_tensor(k.X[:, pair, :, :], k.X[:, pair, :, :],
                                        bias.unsqueeze(1).to_broadcast([P, TT, D]), ALU.add).then_inc(k.x_done, 1)

            @block.tensor
            def _(pe):
                for c in range(KD):
                    if c == 0:
                        pe.wait_ge(k.h_ready, TT)
                    for t in range(TT):
                        i = nc.tensor.transpose(k.ps[:, c, t * P:(t + 1) * P], k.h[:, t, c * P:(c + 1) * P], k.ident[:])
                    i.then_inc(k.prod_ready, 1)
                pe.wait_ge(k.copied_v, 1)
                pe.wait_ge(k.copied_a, 1)
                for t in range(TT):
                    for m in range(KD):
                        i = nc.tensor.matmul(k.ps[:, 2, t * NE:(t + 1) * NE], k.hT[:, m, t * P:(t + 1) * P], wr[:, m, :],
                                             start=m == 0, stop=m == KD - 1)
                i.then_inc(k.prod_ready, 1)

            @block.vector
            def _(dve):
                norm_stats(k, dve, lambda t: k.X[:, pair, t, :])
                norm_apply(k, dve, lambda t: k.X[:, pair, t, :], k.h)
                dve.wait_ge(k.prod_ready, 1)
                nc.vector.tensor_copy(k.hT[:, 0, :], k.ps[:, 0, :]).then_inc(k.copied_v, 1)
                dve.wait_ge(k.prod_ready, 3)
                route.vector(k, dve, k.ps[:, 2, 0:TT * NE].rearrange("p (t e) -> p t e", e=NE), route.pr)
                nc.vector.tensor_copy(pp[0], route.pr).then_inc(k.chain_v, 1)
                nc.vector.tensor_scalar(pp[1], route.rank, 0.0, None, ALU.is_equal).then_inc(k.chain_v, 1)
                nc.vector.tensor_scalar(pp[2], route.rank, 1.0, None, ALU.is_equal).then_inc(k.chain_v, 1)
        k.clear()

    def one(x):
        return x.rearrange("p t e -> p (t e)")

    with nc.Block() as block:
        @block.tensor
        def _(pe):
            pe.wait_ge(k.chain_v, 1)
            nc.tensor.matmul(k.ps[:, 0, 0:P], k.upper[:], one(ALLM), start=True, stop=True)
            nc.tensor.matmul(k.ps[:, 1, 0:P], k.ones[:], one(ALLM), start=True, stop=True).then_inc(k.prod_ready, 1)

        @block.vector
        def _(dve):
            n = [0]

            def then(i):
                n[0] += 1
                i.then_inc(k.chain_v, 1)
                dve.wait_ge(k.chain_v, n[0])

            then(nc.vector.tensor_tensor(ALLM, M1, M2, ALU.add))
            then(nc.vector.memset(BASE[:, 0, :], 0.0))
            dve.wait_ge(k.prod_ready, 1)
            tot = k.ps[:, 1, 0:P].rearrange("p (t e) -> p t e", e=NE)
            for t in range(1, NTT):
                then(nc.vector.tensor_tensor(BASE[:, t, :], BASE[:, t - 1, :], tot[:, t - 1, :], ALU.add))
            then(nc.vector.tensor_tensor(one(POS), k.ps[:, 0, 0:P], one(BASE), ALU.add))
            then(nc.vector.tensor_scalar(TMP, POS, float(CAP), 4.0 * NE * CAP, ALU.is_ge, ALU.mult))
            then(nc.vector.tensor_tensor(SLOT, POS, TMP, ALU.add))
            then(nc.vector.tensor_tensor(SLOT, SLOT, k.starts[:].unsqueeze(1).to_broadcast([P, NTT, NE]), ALU.add))
            for c, M in enumerate((M1, M2)):
                then(nc.vector.tensor_tensor(TMP, M, SLOT, ALU.mult))
                then(nc.vector.tensor_reduce(sk[c], TMP, AX.X, ALU.add))
                then(nc.vector.tensor_copy(idx[c], sk[c]))
                then(nc.vector.tensor_scalar(tmp, sk[c], NE * CAP - 1.0, None, ALU.min))
                then(nc.vector.tensor_copy(idx[2 + c], tmp))
                then(nc.vector.tensor_tensor(TMP, M, PR, ALU.mult))
                then(nc.vector.tensor_reduce(wk[c], TMP, AX.X, ALU.add))
                then(nc.vector.tensor_scalar(tmp, sk[c], float(NE * CAP), None, ALU.is_lt))
                then(nc.vector.tensor_tensor(wk[c], wk[c], tmp, ALU.mult))
    k.clear()

    xe = [k.Pb[:, n, :, :] for n in range(2)]
    xeT = [k.PT[:, n, :, :] for n in range(2)]
    gT = [k.KT, k.V[:].rearrange("p t (a n) -> p (t a) n", a=2)]
    ysb = [k.h[:], k.cT[:].rearrange("p c (t d) -> p (c t) d", d=D)]
    back = A0[:, 0:2 * NTT * D].rearrange("p (n d) -> p n d", d=D)
    with nc.Block() as block:
        @block.gpsimd
        def _(pool):
            pool.wait_ge(k.zero_in, 32)
            for t in range(NTT):
                for c in range(2):
                    nc.gpsimd.indirect_dma_start(
                        out=xb, out_offset=bass.IndirectOffsetOnAxis(ap=idx[c][:, t:t + 1], axis=0), in_=HB[:, t, :],
                        in_offset=None, bounds_check=NE * CAP - 1, oob_is_err=False).then_inc(k.scattered, 16)
            pool.wait_ge(k.stored, 16 * NE)
            for t in range(NTT):
                for c in range(2):
                    nc.gpsimd.indirect_dma_start(
                        out=back[:, 2 * t + c, :], out_offset=None, in_=yb,
                        in_offset=bass.IndirectOffsetOnAxis(ap=idx[2 + c][:, t:t + 1], axis=0),
                        bounds_check=NE * CAP - 1, oob_is_err=False).then_inc(k.gathered[t], 16)

        @block.sync
        def _(sp):
            sp.wait_ge(k.scattered, 16 * 2 * NTT)
            for e in range(NE):
                if e >= 2:
                    sp.wait_ge(k.prod_ready, KD * (e - 1))
                sp.dma_start(xe[e % 2], xb[e * CAP:(e + 1) * CAP, :].rearrange("(t p) d -> p t d", p=P)
                             ).then_inc(k.rows_in[e % 2], 16)
                if NSLOT <= e + 2 < NE:
                    sp.wait_ge(k.out_ready, 2 * (e + 3 - NSLOT))
                    sp.dma_start(slots[(e + 2) % NSLOT], k.dram["moe3"][e + 2]).then_inc(k.expert_in[NE + e + 2], 16)
                if e >= 1:
                    sp.wait_ge(k.chain_v, 2 * e)
                    sp.dma_start(yb[(e - 1) * CAP:e * CAP, :].rearrange("(t p) d -> p t d", p=P),
                                 ysb[(e - 1) % 2]).then_inc(k.stored, 16)
            sp.wait_ge(k.chain_v, 2 * NE)
            sp.dma_start(yb[(NE - 1) * CAP:NE * CAP, :].rearrange("(t p) d -> p t d", p=P),
                         ysb[(NE - 1) % 2]).then_inc(k.stored, 16)

        @block.tensor
        def _(pe):
            for e in range(NE):
                w = slots[e % NSLOT]
                w1 = w[:, 0:KD * F].rearrange("p (m f) -> p m f", m=KD)
                w2 = w[:, KD * F:].rearrange("p (f d) -> p f d", f=FC)
                pe.wait_ge(k.rows_in[e % 2], 16 * (e // 2 + 1))
                if e >= 1:
                    pe.wait_ge(k.copied_v, KD * e)
                for c in range(KD):
                    for t in range(TT):
                        i = nc.tensor.transpose(k.ps[:, c, t * P:(t + 1) * P], xe[e % 2][:, t, c * P:(c + 1) * P],
                                                k.ident[:])
                    i.then_inc(k.prod_ready, 1)
                pe.wait_ge(k.copied_v, KD * (e + 1))
                pe.wait_ge(k.expert_in[NE + e], 16)
                for f in range(FC):
                    n = e * FC + f
                    if n >= 4:
                        pe.wait_ge(k.copied_a, n - 3)
                    for m in range(KD):
                        i = nc.tensor.matmul(k.ps[:, 2 + n % 4, :], w1[:, m, f * P:(f + 1) * P], xeT[e % 2][:, m, :],
                                             start=m == 0, stop=m == KD - 1)
                    i.then_inc(k.scores_ready, 1)
                pe.wait_ge(k.copied_a, FC * (e + 1))
                for b in range(2):
                    if e >= 1:
                        pe.wait_ge(k.chain_v, 2 * e + b - 1)
                    for q in range(2):
                        t = 2 * b + q
                        for f in range(FC):
                            i = nc.tensor.matmul(k.ps[:, 6 + b, q * D:(q + 1) * D], gT[e % 2][:, f, t * P:(t + 1) * P],
                                                 w2[:, f, :], start=f == 0, stop=f == FC - 1)
                    i.then_inc(k.out_ready, 1)

        @block.scalar
        def _(act):
            for e in range(NE):
                if e >= 2:
                    act.wait_ge(k.out_ready, 2 * (e - 1))
                for f in range(FC):
                    n = e * FC + f
                    act.wait_ge(k.scores_ready, n + 1)
                    nc.scalar.activation(gT[e % 2][:, f, :], k.ps[:, 2 + n % 4, :], ACT.Gelu_apprx_tanh
                                         ).then_inc(k.copied_a, 1)

        @block.vector
        def _(dve):
            for e in range(NE):
                for c in range(KD):
                    dve.wait_ge(k.prod_ready, KD * e + c + 1)
                    nc.vector.tensor_copy(xeT[e % 2][:, c, :], k.ps[:, c, :]).then_inc(k.copied_v, 1)
                if e >= 2:
                    dve.wait_ge(k.stored, 16 * (e - 1))
                for b in range(2):
                    dve.wait_ge(k.out_ready, 2 * e + b + 1)
                    nc.vector.tensor_copy(ysb[e % 2][:, 2 * b:2 * b + 2, :],
                                          k.ps[:, 6 + b, :].rearrange("p (q d) -> p q d", q=2)).then_inc(k.chain_v, 1)
            X = k.X[:].rearrange("p g t d -> p (g t) d")
            for t in range(NTT):
                dve.wait_ge(k.gathered[t], 32)
                for c in range(2):
                    if c:
                        dve.wait_ge(k.x_done, 2 * t + 1)
                    nc.vector.scalar_tensor_tensor(out=X[:, t, :], in0=back[:, 2 * t + c, :], scalar=wk[c][:, t:t + 1],
                                                   in1=X[:, t, :], op0=ALU.mult, op1=ALU.add).then_inc(k.x_done, 1)
    k.clear()


def finish(k, out):
    nc = k.nc
    with nc.Block() as block:
        @block.sync
        def _(sp):
            sp.dma_start(out, k.X[:]).then_inc(k.x_out, 16)
            sp.wait_ge(k.x_out, 16)


LIST = list(range(12))


def program(nc, dram, out):
    with ExitStack() as ctx:
        k = Core(nc, ctx, dram)
        constants(k)
        for n in LIST:
            weights(k, n)
            if n in ATTN:
                attention(k, n)
            else:
                {2: mixer, 8: composed, 11: capacity}[n](k, n)
        finish(k, out)


def _rows(w, r=P):
    c = w.shape[0] // r
    w = w.reshape(c, r, -1).transpose(1, 0, 2).reshape(r, -1)
    full = np.zeros((P, w.shape[1]), np.float32)
    full[0:r] = w
    return full


def _slots(w, heads, dh, slot, rep=1):
    w = w.reshape(-1, heads, 1, dh)
    full = np.zeros((w.shape[0], heads, rep, slot), np.float32)
    full[..., 0:dh] = w
    return full.reshape(w.shape[0], -1)


def _cols(b):
    return np.ascontiguousarray(b.reshape(-1, P).T)


def _spread(b):
    return np.broadcast_to(b.reshape(1, -1), (P, b.size))


def _pack_attn(L, a):
    n = L.name + "_"
    parts = []
    if L.normed:
        w, b = a[n + "qkv_w"].T, a[n + "qkv_b"]
        parts = [_rows(w[:, 0:2 * D]), _rows(w[:, 2 * D:]), _rows(a[n + "out_w"].T), _spread(b[0:2 * D]),
                 _spread(b[2 * D:]), _spread(a[n + "out_b"]), _cols(a[n + "ln_w"]), _cols(a[n + "ln_b"])]
        return np.concatenate(parts, axis=1)
    if L.name == "L2_attn":
        w, b = a["L2_attn_W_qkv"], a["L2_attn_b_qkv"]
        wq, wk, wv, wo = w[:, 0:D], w[:, D:2 * D], w[:, 2 * D:], a["L2_attn_W_proj"]
        bq, bk, bv, bo = b[0:D], b[D:2 * D], b[2 * D:], a["L2_attn_b_proj"]
    else:
        wq, wk, wv, wo = (a[n + x] for x in ("Wq", "Wk", "Wv", "Wo"))
        if L.name == "L0_xattn":
            wq, wk, wv, wo = wq.T, wk.T, wv.T, wo.T
        if L.qkv_bias:
            bq, bk, bv = (a[n + x] for x in ("bq", "bk", "bv"))
        if L.out_bias:
            bo = a[n + "bo"]
    parts = [_rows(_slots(wq, L.H, L.dh, L.slot)), _rows(_slots(wk, L.kvh, L.dh, L.slot, L.rep), L.kr),
             _rows(wv, L.kr), _rows(wo)]
    if L.qkv_bias:
        parts += [_cols(_slots(bq, L.H, L.dh, L.slot)), _cols(_slots(bk, L.kvh, L.dh, L.slot, L.rep)), _spread(bv)]
    if L.out_bias:
        parts += [_spread(bo)]
    if L.selected:
        parts += [_spread(a[n + "Wg"])]
    return np.concatenate(parts, axis=1)


def _layout(a):
    out = {"x": a["x"].reshape(NPAIR, TT, P, D).transpose(2, 0, 1, 3),
           "ctxT": a["ctx_768"].reshape(NPAIR, 2 * S, KD, CR).transpose(0, 3, 2, 1)}
    for n, L in ATTN.items():
        out[f"w{n}"] = _pack_attn(L, a)
    out["w2"] = np.concatenate([_rows(a["L0_ffn_W_r"].T), _rows(a["L0_ffn_W_k"].T), _rows(a["L0_ffn_W_v"].T),
                                _cols(a["L0_ffn_mu_r"]), _cols(a["L0_ffn_mu_k"])], axis=1)
    out["w8"] = _rows(a["L2_ffn_gate_w"].T)
    out["moe2"] = np.stack([np.concatenate([_rows(a["L2_ffn_w_up"][e].T), _rows(a["L2_ffn_w_down"][e])], axis=1)
                            for e in range(NE)])
    out["w11"] = np.concatenate([_rows(a["L3_ffn_w_router"]), _spread(a["L3_ffn_bias"])], axis=1)
    out["moe3"] = np.stack([np.concatenate([_rows(a["L3_ffn_w1"][e]), _rows(a["L3_ffn_w2"][e])], axis=1)
                            for e in range(NE)])
    return {n: np.ascontiguousarray(v) for n, v in out.items()}


def kernel(**inputs):
    import concourse.bacc as bacc
    from concourse.bass_utils import run_bass_kernel_spmd

    arrays = _layout({n: np.asarray(v) for n, v in inputs.items()})
    nc = bacc.Bacc("TRN2", target_bir_lowering=False, num_devices=1)
    dram = {n: nc.dram_tensor(n, v.shape, mybir.dt.from_np(v.dtype), kind="ExternalInput").ap()
            for n, v in arrays.items()}
    out = nc.dram_tensor("out", (P, NPAIR, TT, D), F32, kind="ExternalOutput").ap()
    program(nc, dram, out)
    r = run_bass_kernel_spmd(nc, [arrays], core_ids=[0])
    return np.ascontiguousarray(r.results[0]["out"].transpose(1, 2, 0, 3)).reshape(B, S, D)
```

```python
from contextlib import ExitStack

import numpy as np
import concourse.bass as bass
from concourse import mybir

ALU = mybir.AluOpType
ACT = mybir.ActivationFunctionType
AX = mybir.AxisListType
F32 = mybir.dt.float32
BF16 = mybir.dt.bfloat16
I32 = mybir.dt.int32

P = 128
B, S, D = 8, 256, 256
DC = 192
CR = DC // 2
T = B * S
NPAIR = B // 2
TT = 2 * S // P
KD = D // P
BANK = 512
EPS = 1e-5
MASKED = -1.0e30
NE = 8
F = 1024
FC = F // P
CAP = 2 * T // NE
ARENA = 8448


class Attn:

    def __init__(self, name, heads, dh, scale, ctx=False, mask=None, kv_heads=None, qkv_bias=False,
                 out_bias=False, res_h=False, normed=False, selected=False):
        self.name, self.H, self.dh, self.scale, self.ctx, self.mask = name, heads, dh, scale, ctx, mask
        self.qkv_bias, self.out_bias, self.res_h = qkv_bias, out_bias, res_h
        self.normed, self.selected = normed, selected
        self.per = P // dh
        self.nch = heads // self.per
        self.kvh = kv_heads or heads
        self.rep = heads // self.kvh
        self.NV = self.kvh * dh
        self.inner = heads * dh
        self.NC = self.inner // P
        self.CS = self.per // 2
        self.wide = dh == 16
        self.G = heads // 2
        self.NS = 2 * self.G
        self.TB = P if selected else S
        self.nt = self.TB // P
        self.E = 2 * self.nt
        self.kr = CR if ctx else P
        at = 0
        self.at = {}
        nq = self.nch * P
        for key, n in (("wq", KD * (2 * D if normed else nq)), ("wk", 0 if normed else KD * nq),
                       ("wv", KD * self.NV), ("wo", self.NC * D),
                       ("bq", self.nch if qkv_bias and not normed else 0),
                       ("bk", self.nch if qkv_bias and not normed else 0),
                       ("bqk", 2 * D if normed else 0), ("bv", self.NV if qkv_bias else 0),
                       ("bo", D if out_bias else 0), ("lnw", KD if normed else 0),
                       ("lnb", KD if normed else 0), ("wg", D if selected else 0)):
            self.at[key] = (at, n)
            at += n
        self.width = at
        assert at <= ARENA


ATTN = {
    0: Attn("L0_attn", 16, 16, 0.25, mask="window", kv_heads=4, qkv_bias=True, out_bias=True),
    1: Attn("L0_xattn", 8, 32, float(32.0 ** -0.5), ctx=True, qkv_bias=True, out_bias=True),
    3: Attn("L1_attn", 16, 16, 4.0, qkv_bias=True, out_bias=True, res_h=True, normed=True),
    4: Attn("L1_xattn", 16, 64, 0.125, ctx=True, out_bias=True),
    5: Attn("L1_ffn", 16, 16, 0.25, selected=True),
    6: Attn("L2_attn", 16, 16, 0.25, qkv_bias=True, out_bias=True),
    7: Attn("L2_xattn", 16, 64, 0.125, ctx=True, out_bias=True),
    9: Attn("L3_attn", 16, 64, 0.125, mask="causal", res_h=True),
    10: Attn("L3_xattn", 8, 64, 0.125, ctx=True, out_bias=True),
}
MIX = {"wr": (0, KD * D), "wk": (KD * D, KD * D), "wv": (2 * KD * D, KD * D),
       "mur": (3 * KD * D, KD), "muk": (3 * KD * D + KD, KD)}
MIX_WIDTH = 3 * KD * D + 2 * KD
MOE2 = {"wg": (0, KD * NE), "wc": (KD * NE, NE * KD * D)}
MOE2_WIDTH = KD * NE
MOE3 = {"wr": (0, KD * NE), "bias": (KD * NE, D)}
MOE3_WIDTH = KD * NE + D
LAYERS = 12
WIDTH = {**{n: a.width for n, a in ATTN.items()}, 2: MIX_WIDTH, 8: MOE2_WIDTH, 11: MOE3_WIDTH}


class Core:

    def __init__(self, nc, ctx, dram):
        self.nc, self.dram = nc, dram

        def sb(name, shape, dt=F32):
            return ctx.enter_context(nc.sbuf_tensor(name, shape, dt))

        self.X = sb("X", [P, NPAIR, TT, D])
        self.arena = [sb(f"arena{n}", [P, ARENA]) for n in range(2)]
        self.W = sb("work", [P, 5 * 4096])
        W = self.W
        self.QT = W[:, 0:8192].rearrange("p (c n) -> p c n", n=BANK)
        self.KT = W[:, 8192:12288].rearrange("p (c n) -> p c n", n=BANK)
        self.V = W[:, 12288:16384].rearrange("p (t n) -> p t n", t=TT)
        self.O = W[:, 16384:20480].rearrange("p (t n) -> p t n", t=TT)
        self.ob = sb("ob", [P, 2, S])
        self.rexp = sb("rexp", [P, 2, 2, P])
        self.hm = sb("hm", [P, 8])
        self.bqm = sb("bqm", [P, 16])
        self.ind = {d: sb(f"ind{d}", [P, P // d]) for d in (16, 32, 64)}
        self.Pb = sb("Pb", [P, 2, 4, S])
        self.PT = sb("PT", [P, 2, 2, BANK])
        self.h = sb("h", [P, TT, D])
        self.hT = sb("hT", [P, KD, BANK])
        self.cT = sb("cT", [P, KD, BANK])
        self.res = sb("res", [P, TT, D])
        self.st = sb("st", [P, TT, 6])
        self.mv = sb("mv", [P, TT, 2])
        self.lnv = sb("lnv", [P, TT])
        self.rstd = sb("rstd", [P, TT])
        self.rt = sb("rt", [P, 64])
        self.nm = sb("nm", [P, 16, 4])
        self.sums = sb("sums", [P, 16, 4])
        self.rs = sb("rs", [P, 16, 4])
        self.small = sb("small", [P, 24, TT])
        self.ident = sb("ident", [P, P])
        self.identb = sb("identb", [P, P], BF16)
        self.mask = {m: sb(f"mask_{m}", [P, 2, S], BF16) for m in ("causal", "window")}
        self.before = sb("before", [P, 2, S])
        self.iota = sb("iota", [P, P])
        self.first8 = sb("first8", [P, NE, NE])
        self.upper = sb("upper", [P, P])
        self.ones = sb("ones", [P, P])
        self.starts = sb("starts", [P, NE])
        self.st2 = sb("st2", [P, 5, T // P])
        self.idx = sb("idx", [P, 4, T // P], mybir.dt.uint32)
        self.xb = nc.dram_tensor("xb", (NE * CAP, D), F32, kind="Internal").ap()
        self.yb = nc.dram_tensor("yb", (NE * CAP, D), F32, kind="Internal").ap()
        self.ps = ctx.enter_context(nc.psum_tensor("ps", [P, 8, BANK], F32))
        def sem(name):
            return ctx.enter_context(nc.semaphore(name))

        self.ctx_in = sem("ctx_in")
        self.stats = sem("stats")
        self.root_step = sem("root_step")
        self.gate_exp = sem("gate_exp")
        self.h_ready = sem("h_ready")
        self.res_ready = sem("res_ready")
        self.prod_ready = sem("prod_ready")
        self.copied_v = sem("copied_v")
        self.copied_a = sem("copied_a")
        self.scores_ready = sem("scores_ready")
        self.negmax_ready = sem("negmax_ready")
        self.probs_ready = sem("probs_ready")
        self.pT_ready = sem("pT_ready")
        self.pT_copied_v = sem("pT_copied_v")
        self.pT_copied_a = sem("pT_copied_a")
        self.av_ready = sem("av_ready")
        self.rsum_ready = sem("rsum_ready")
        self.av_normed = sem("av_normed")
        self.out_ready = sem("out_ready")
        self.o_copied = sem("o_copied")
        self.rexp_ready = sem("rexp_ready")
        self.r_ready = sem("r_ready")
        self.x_done = sem("x_done")
        self.chain_v = sem("chain_v")
        self.chain_a = sem("chain_a")
        self.sel_ready = sem("sel_ready")
        self.scattered = sem("scattered")
        self.stored = sem("stored")
        self.loop_sems = (self.ctx_in, self.stored)
        self.loop_count = 28
        self.x_in = sem("x_in")
        self.consts = sem("consts")
        self.w_in = [sem(f"w_in{n}") for n in range(LAYERS)]
        self.expert_in = [sem(f"expert_in{n}") for n in range(2 * NE)]
        self.rows_in = [sem(f"rows_in{n}") for n in range(2)]
        self.gathered = [sem(f"gathered{n}") for n in range(T // P)]
        self.zeroed = sem("zeroed")
        self.zero_in = sem("zero_in")
        self.x_out = sem("x_out")

    def clear(self):
        first, last = self.loop_sems[0].num, self.loop_sems[1].num
        assert last - first + 1 == self.loop_count
        self.nc.all_engine_barrier(sems_to_clear=range(first, last + 1))

    def w(self, layer, key, where, rows=P):
        at, n = where[key]
        return self.arena[layer % 2][0:rows, at:at + n]


def constants(k):
    nc = k.nc
    with nc.Block() as block:
        @block.sync
        def _(sp):
            sp.dma_start(k.X[:], k.dram["x"]).then_inc(k.x_in, 16)
            sp.dma_start(k.arena[LIST[0] % 2][:, 0:WIDTH[LIST[0]]],
                         k.dram[f"w{LIST[0]}"]).then_inc(k.w_in[LIST[0]], 16)

        @block.vector
        def _(dve):
            dve.wait_ge(k.x_in, 16)
            for part in range(5):
                norm_ahead(k, dve, lambda t: k.X[:, 0, t, :], part)

        @block.gpsimd
        def _(pool):
            nc.gpsimd.memset(k.ident[:], 0.0).then_inc(k.consts, 1)
            nc.gpsimd.memset(k.mask["causal"][:], 0.0).then_inc(k.consts, 1)
            nc.gpsimd.memset(k.before[:], 1.0).then_inc(k.consts, 1)
            nc.gpsimd.iota(k.iota[:], pattern=[[1, P]], base=0, channel_multiplier=0,
                           allow_small_or_imprecise_dtypes=True).then_inc(k.consts, 1)
            nc.gpsimd.memset(k.first8[:], 1.0).then_inc(k.consts, 1)
            nc.gpsimd.memset(k.ones[:], 1.0).then_inc(k.consts, 1)
            nc.gpsimd.iota(k.starts[:], pattern=[[CAP, NE]], base=0, channel_multiplier=0,
                           allow_small_or_imprecise_dtypes=True).then_inc(k.consts, 1)
            nc.gpsimd.memset(k.ind[16][:], 1.0).then_inc(k.consts, 1)
            nc.gpsimd.memset(k.ind[32][:], 1.0).then_inc(k.consts, 1)
            nc.gpsimd.memset(k.ind[64][:], 1.0).then_inc(k.consts, 1)
            pool.wait_ge(k.consts, 10)
            for n, (d, ind) in enumerate(k.ind.items()):
                nc.gpsimd.affine_select(out=ind[:], in_=ind[:], compare_op=ALU.is_ge, fill=0.0, base=0,
                                        pattern=[[-d, P // d]], channel_multiplier=1).then_inc(k.consts, 1)
                pool.wait_ge(k.consts, 11 + 2 * n)
                nc.gpsimd.affine_select(out=ind[:], in_=ind[:], compare_op=ALU.is_ge, fill=0.0, base=d - 1,
                                        pattern=[[d, P // d]], channel_multiplier=-1).then_inc(k.consts, 1)
            nc.gpsimd.affine_select(out=k.first8[:], in_=k.first8[:], compare_op=ALU.is_ge, fill=0.0, base=-1,
                                    pattern=[[1, NE], [-1, NE]], channel_multiplier=0).then_inc(k.consts, 1)
            nc.gpsimd.affine_select(out=k.upper[:], in_=k.ones[:], compare_op=ALU.is_ge, fill=0.0, base=-1,
                                    pattern=[[1, P]], channel_multiplier=-1).then_inc(k.consts, 1)
            nc.gpsimd.affine_select(out=k.ident[:], in_=k.ident[:], compare_op=ALU.not_equal, fill=1.0, base=0,
                                    pattern=[[-1, P]], channel_multiplier=1).then_inc(k.consts, 1)
            nc.gpsimd.affine_select(out=k.mask["causal"][:], in_=k.mask["causal"][:], compare_op=ALU.is_ge,
                                    fill=MASKED, base=0, pattern=[[P, 2], [-1, S]],
                                    channel_multiplier=1).then_inc(k.consts, 1)
            nc.gpsimd.affine_select(out=k.before[:], in_=k.before[:], compare_op=ALU.is_ge, fill=0.0, base=-1,
                                    pattern=[[P, 2], [-1, S]], channel_multiplier=1).then_inc(k.consts, 1)
            pool.wait_ge(k.consts, 21)
            nc.gpsimd.tensor_copy(k.identb[:], k.ident[:]).then_inc(k.consts, 1)
            nc.gpsimd.affine_select(out=k.mask["window"][:], in_=k.mask["causal"][:], compare_op=ALU.is_ge,
                                    fill=MASKED, base=P - 1, pattern=[[-P, 2], [1, S]],
                                    channel_multiplier=-1).then_inc(k.consts, 1)
    k.clear()


def weights(k, layer):
    nc = k.nc
    with nc.Block() as block:
        @block.sync
        def _(sp):
            if layer + 1 in LIST:
                sp.dma_start(k.arena[(layer + 1) % 2][:, 0:WIDTH[layer + 1]],
                             k.dram[f"w{layer + 1}"]).then_inc(k.w_in[layer + 1], 16)
            sp.wait_ge(k.w_in[layer], 16)


MAGIC = float(0x5F3759DF)


def inverse_root(k, dve, v, y, t, done=0):
    nc = k.nc
    bits = mybir.dt.uint32
    nc.vector.tensor_scalar(t.bitcast(bits), v.bitcast(bits), 1, None, ALU.logical_shift_right).then_inc(k.root_step, 1)
    dve.wait_ge(k.root_step, done + 1)
    nc.vector.tensor_scalar(y.bitcast(bits), t.bitcast(bits), -1.0, MAGIC, ALU.mult, ALU.add).then_inc(k.root_step, 1)
    for n in range(3):
        dve.wait_ge(k.root_step, done + 3 * n + 2)
        nc.vector.tensor_tensor(t, y, y, ALU.mult).then_inc(k.root_step, 1)
        dve.wait_ge(k.root_step, done + 3 * n + 3)
        nc.vector.scalar_tensor_tensor(out=t, in0=t, scalar=-0.5, in1=v, op0=ALU.mult, op1=ALU.mult
                                       ).then_inc(k.root_step, 1)
        dve.wait_ge(k.root_step, done + 3 * n + 4)
        nc.vector.scalar_tensor_tensor(out=y, in0=t, scalar=1.5, in1=y, op0=ALU.add, op1=ALU.mult
                                       ).then_inc(k.root_step, 1)
    dve.wait_ge(k.root_step, done + 11)


ROOT = 11


def norm_stats(k, dve, src, t, done=0):
    k.nc.vector.bn_stats(k.st[:, t, :], src).then_inc(k.stats, 1)


def norm_root(k, dve, done=0, roots=0):
    nc = k.nc
    for t in range(TT):
        dve.wait_ge(k.stats, done + t + 1)
        nc.vector.bn_aggr(k.mv[:, t, :], k.st[:, t, :]).then_inc(k.stats, 1)
    dve.wait_ge(k.stats, done + 2 * TT)
    nc.vector.tensor_scalar(k.lnv[:], k.mv[:, :, 1], EPS, None, ALU.add).then_inc(k.stats, 1)
    dve.wait_ge(k.stats, done + 2 * TT + 1)
    inverse_root(k, dve, k.lnv[:], k.rstd[:], k.rt[:, 0:TT], roots)


def norm_apply(k, dve, src, dst, t):
    k.nc.vector.tensor_scalar(dst[:, t, :], src, k.mv[:, t, 0:1], k.rstd[:, t:t + 1],
                              ALU.subtract, ALU.mult).then_inc(k.h_ready, 1)


def norm_ahead(k, dve, src, part, done=0, roots=0):
    if part < 2:
        for t in (2 * part, 2 * part + 1):
            norm_stats(k, dve, src(t), t)
    elif part == 2:
        norm_root(k, dve, done, roots)
    elif part < 5:
        for t in (2 * part - 6, 2 * part - 5):
            norm_apply(k, dve, src(t), k.h, t)


class Prep:

    def __init__(self, L):
        self.steps = []
        if L.selected:
            self.steps += [("gate", 0, "v"), ("selT", 0, "a"), ("hT", 0, "v"), ("hT", 1, "a")]
        else:
            self.steps += [("hT", 0, "v"), ("hT", 1, "a")]
        if L.normed:
            self.steps += [("qk", t, "v") for t in range(TT)]
            self.steps += [("v", (t, 0, L.NV), "v") for t in range(2 * L.nt)]
            self.steps += [("qkT", c, "av"[c % 2]) for c in range(2 * L.nch)]
        else:
            self.steps += [("q", c, "va"[c % 2]) for c in range(L.nch)]
            self.steps += [("k", c, "a") for c in range(L.nch)]
            self.steps += [("v", (t, c, min(BANK, L.NV)), "v") for t in range(2 * L.nt)
                           for c in range(0, L.NV, BANK)]

    def copied(self, n, engine):
        return sum(1 for s in self.steps[0:n] if s[2] == engine)

    def where(self, kind, arg=0):
        return next(n for n, s in enumerate(self.steps) if s[0] == kind and s[1] == arg)

    def all(self, kind):
        return max(n for n, s in enumerate(self.steps) if s[0] == kind) + 1


def attention(k, layer):
    nc, L = k.nc, ATTN[layer]
    prep = Prep(L)
    N = len(prep.steps)
    NT = 2 * L.TB
    A = L.at
    wq = k.w(layer, "wq", A).rearrange("p (c n) -> p c n", c=KD)
    wv = k.w(layer, "wv", A, L.kr).rearrange("p (c n) -> p c n", c=KD)
    wo = k.w(layer, "wo", A).rearrange("p (c n) -> p c n", c=L.NC)
    if not L.normed:
        wk = k.w(layer, "wk", A, L.kr).rearrange("p (c n) -> p c n", c=KD)
    kv_in = k.cT if L.ctx else k.hT
    kr = L.kr
    masked = L.mask is not None
    tiles = [(kt, qt) for kt in range(L.nt) for qt in range(L.nt) if not (masked and kt > qt)]
    START = [(a + 1) * L.G + 3 for a in range(2)]
    STEPS = START[1] + 1
    W = k.W

    def seen(x):
        return x[:, 0:len(tiles) * P]

    if L.wide:
        KT = W[:, 8192:9216].rearrange("p (c n) -> p c n", n=BANK)
        V0 = 9216
        Vm = W[:, V0:V0 + 2 * L.nt * L.H * P]
        OT = W[:, 17408 if L.nt == 2 else 13312:][:, 0:L.NC * NT].rearrange("p (c n) -> p c n", n=NT)
    else:
        KT = k.KT
        OT = k.O.rearrange("p t n -> p (t n)")[:, 0:L.NC * NT].rearrange("p (c n) -> p c n", n=NT)
    h2 = W[:, 18432:19456].rearrange("p (t d) -> p t d", d=D)
    qkn = W[:, 18432:20480].rearrange("p (t n) -> p t n", t=TT)
    Z, EX, GATE, R1, R2, RANK = (k.small[:, n, :] for n in range(6))
    selT = k.cT[:, 0, :]
    sel = k.cT[:, 1, :]
    scratch = k.res

    with nc.Block() as block:
        @block.vector
        def _(dve):
            ind = k.ind[L.dh]
            nc.vector.tensor_scalar(k.hm[:, 0:L.per], ind[:], L.scale, None, ALU.mult).then_inc(k.chain_v, 1)
            dve.wait_ge(k.chain_v, 1)
            if L.qkv_bias and not L.normed:
                for c in range(L.nch):
                    nc.vector.tensor_scalar(k.bqm[:, c * L.per:(c + 1) * L.per], k.hm[:, 0:L.per],
                                            k.w(layer, "bq", A)[:, c:c + 1], None, ALU.mult)

        @block.gpsimd
        def _(pool):
            if L.wide:
                nc.gpsimd.memset(Vm, 0.0)
    k.clear()

    with nc.Fori(0, NPAIR) as pair:
        with nc.Block() as block:
            @block.sync
            def _(sp):
                if L.ctx:
                    sp.dma_start(k.cT[0:CR, :, :], k.dram["ctxT"][pair]).then_inc(k.ctx_in, 16)

            @block.gpsimd
            def _(pool):
                src = k.X[:, pair, :, :]
                if L.res_h:
                    nc.gpsimd.tensor_tensor(k.res[:], src, k.h[:], ALU.add).then_inc(k.res_ready, 1)
                    src = k.res[:]
                if L.out_bias:
                    bo = k.w(layer, "bo", A).unsqueeze(1).to_broadcast([P, TT, D])
                    if L.res_h:
                        pool.wait_ge(k.res_ready, 1)
                    nc.gpsimd.tensor_tensor(k.res[:], src, bo, ALU.add).then_inc(k.res_ready, 1)
                for n in range(L.NS // L.CS):
                    pool.wait_ge(k.rsum_ready, n + 1)
                    if n >= 2:
                        pool.wait_ge(k.r_ready, n - 1)
                    for q in range(L.nt):
                        rs = k.rs[:, n * L.CS:(n + 1) * L.CS, :].rearrange("p s (j q) -> p (s j) q", j=2)[:, :, q]
                        nc.gpsimd.tensor_copy(
                            k.rexp[:, n % 2, q, :].rearrange("p (h d) -> p h d", d=L.dh),
                            rs.unsqueeze(2).to_broadcast([P, L.per, L.dh])).then_inc(k.rexp_ready, 1)

            @block.scalar
            def _(act):
                if L.selected:
                    act.wait_ge(k.chain_v, TT)
                    nc.scalar.activation(EX, Z, ACT.Exp, scale=-1.0).then_inc(k.gate_exp, 1)
                for n, (kind, c, engine) in enumerate(prep.steps):
                    if engine != "a":
                        continue
                    src = k.ps[:, n % 8, :]
                    act.wait_ge(k.prod_ready, n + 1)
                    if kind == "hT":
                        if L.normed:
                            i = nc.scalar.activation(k.hT[:, c, :], src, ACT.Identity,
                                                     bias=k.w(layer, "lnb", A)[:, c:c + 1],
                                                     scale=k.w(layer, "lnw", A)[:, c:c + 1])
                        else:
                            i = nc.scalar.activation(k.hT[:, c, 0:NT], src[:, 0:NT], ACT.Copy)
                    elif kind == "selT":
                        i = nc.scalar.activation(selT, src, ACT.Copy)
                    elif kind == "k":
                        if L.qkv_bias:
                            i = nc.scalar.activation(KT[:, c, 0:NT], src[:, 0:NT], ACT.Identity,
                                                     bias=k.w(layer, "bk", A)[:, c:c + 1])
                        else:
                            i = nc.scalar.activation(KT[:, c, 0:NT], src[:, 0:NT], ACT.Copy)
                    elif kind == "qkT" and c >= L.nch:
                        i = nc.scalar.activation(KT[:, c - L.nch, :], src, ACT.Copy)
                    elif kind in ("q", "qkT"):
                        for j in range(L.per):
                            h = c * L.per + j
                            if kind == "q" and L.qkv_bias:
                                i = nc.scalar.activation(k.QT[:, h, 0:NT], src[:, 0:NT], ACT.Identity,
                                                         bias=k.bqm[:, h:h + 1], scale=k.hm[:, j:j + 1])
                            else:
                                i = nc.scalar.activation(k.QT[:, h, 0:NT], src[:, 0:NT], ACT.Copy,
                                                         scale=k.hm[:, j:j + 1])
                    i.then_inc(k.copied_a, 1)
                for s in range(STEPS):
                    if s < L.NS:
                        if L.normed:
                            act.wait_ge(k.scores_ready, 2 * s + 2)
                        if s >= 2:
                            act.wait_ge(k.pT_ready, 2 * (s - 1))
                        for j in range(2):
                            if not L.normed:
                                act.wait_ge(k.negmax_ready, 2 * s + j + 1)
                            for q in range(L.nt):
                                keys = P * (q + 1) if masked else L.TB
                                m = 2 * j + q
                                nc.scalar.activation(
                                    k.Pb[:, s % 2, m, 0:keys], k.ps[:, 2 * (s % 2) + j, q * S:q * S + keys],
                                    ACT.Exp, bias=0.0 if L.normed else k.nm[:, s, m:m + 1],
                                    accum_out=k.sums[:, s, m:m + 1]).then_inc(k.probs_ready, 1)
                    u = s - 1
                    if 0 <= u < L.NS:
                        act.wait_ge(k.pT_ready, 2 * u + 2)
                        if u >= 2:
                            act.wait_ge(k.av_ready, u - 1)
                        nc.scalar.activation(seen(k.PT[:, u % 2, 1, :]), seen(k.ps[:, 5, :]),
                                             ACT.Copy).then_inc(k.pT_copied_a, 1)
                    u = s - 2
                    if 0 <= u < L.NS and u % L.CS == L.CS - 1:
                        n = u // L.CS
                        act.wait_ge(k.av_ready, u + 1)
                        if n >= 2:
                            act.wait_ge(k.av_normed, n - 1)
                        nc.scalar.activation(k.ob[:, n % 2, 0:L.TB], k.ps[:, 6, 0:L.TB], ACT.Copy).then_inc(k.o_copied, 1)

            @block.tensor
            def _(pe):
                for n, (kind, c, engine) in enumerate(prep.steps):
                    out = k.ps[:, n % 8, :]
                    if n >= 8:
                        pe.wait_ge(k.copied_v if prep.steps[n - 8][2] == "v" else k.copied_a,
                                   prep.copied(n - 7, prep.steps[n - 8][2]))
                    if kind == "hT" and not L.selected:
                        if c == 0 and L.normed:
                            pe.wait_ge(k.h_ready, TT)
                        hs = h2 if L.normed else k.h
                        for t in range(TT):
                            i = nc.tensor.transpose(out[:, t * P:(t + 1) * P], hs[:, t, c * P:(c + 1) * P], k.ident[:])
                    elif kind == "gate":
                        pe.wait_ge(k.sel_ready, TT)
                        for t in range(TT):
                            i = nc.tensor.transpose(out[:, t * P:(t + 1) * P], k.O[:, t, 0:P], k.ident[:])
                    elif kind == "selT":
                        pe.wait_ge(k.sel_ready, 2 * TT)
                        for t in range(TT):
                            i = nc.tensor.transpose(out[:, t * P:(t + 1) * P], sel[:, t * P:(t + 1) * P], k.ident[:])
                    elif kind == "hT":
                        for a in range(2):
                            for q in range(2):
                                t = 2 * a + q
                                i = nc.tensor.matmul(out[:, a * P:(a + 1) * P], k.h[:, t, c * P:(c + 1) * P],
                                                     sel[:, t * P:(t + 1) * P], start=q == 0, stop=q == 1)
                    elif kind == "qkT":
                        if c == 0:
                            pe.wait_ge(k.sel_ready, TT)
                        for t in range(TT):
                            i = nc.tensor.transpose(out[:, t * P:(t + 1) * P], qkn[:, t, c * P:(c + 1) * P], k.ident[:])
                    else:
                        if kind in ("q", "qk") and c == 0:
                            pe.wait_ge(k.copied_v, prep.copied(prep.all("hT"), "v"))
                            pe.wait_ge(k.copied_a, prep.copied(prep.all("hT"), "a"))
                        if kind == "k" and c == 0 and L.ctx:
                            pe.wait_ge(k.ctx_in, 16)
                        for m in range(KD):
                            if kind == "q":
                                i = nc.tensor.matmul(out[:, 0:NT], wq[:, m, c * P:(c + 1) * P], k.hT[:, m, 0:NT],
                                                     start=m == 0, stop=m == KD - 1)
                            elif kind == "k":
                                i = nc.tensor.matmul(out[:, 0:NT], wk[:, m, c * P:(c + 1) * P], kv_in[0:kr, m, 0:NT],
                                                     start=m == 0, stop=m == KD - 1)
                            elif kind == "qk":
                                i = nc.tensor.matmul(out, k.hT[:, m, c * P:(c + 1) * P], wq[:, m, :],
                                                     start=m == 0, stop=m == KD - 1)
                            else:
                                t, c0, w = c
                                i = nc.tensor.matmul(out[:, 0:w], kv_in[0:kr, m, t * P:(t + 1) * P],
                                                     wv[:, m, c0:c0 + w], start=m == 0, stop=m == KD - 1)
                    i.then_inc(k.prod_ready, 1)
                pe.wait_ge(k.copied_v, prep.copied(N, "v"))
                pe.wait_ge(k.copied_a, prep.copied(N, "a"))
                used = None
                for s in range(STEPS):
                    if s < L.NS:
                        a, g = divmod(s, L.G)
                        if s >= 2:
                            pe.wait_ge(k.probs_ready, L.E * (s - 1))
                        for j in range(2):
                            h = 2 * g + j
                            c = h // L.per
                            bank = k.ps[:, 2 * (s % 2) + j, :]
                            if masked:
                                nc.tensor.matmul(bank, k.identb[:], k.mask[L.mask][:].rearrange("p q n -> p (q n)"),
                                                 start=True, stop=False, skip_group_check=True)
                            for q in range(L.nt):
                                keys = P * (q + 1) if masked else L.TB
                                i = nc.tensor.matmul(
                                    bank[:, q * S:q * S + keys],
                                    k.QT[:, h, a * L.TB + q * P:a * L.TB + (q + 1) * P],
                                    KT[:, c, a * L.TB:a * L.TB + keys],
                                    start=not masked, stop=True, skip_group_check=masked)
                            i.then_inc(k.scores_ready, 1)
                    u = s - 1
                    if 0 <= u < L.NS:
                        for j in range(2):
                            pe.wait_ge(k.probs_ready, L.E * u + (j + 1) * L.nt)
                            if u >= 1:
                                pe.wait_ge(k.pT_copied_a if j else k.pT_copied_v, u)
                            for kt, qt in tiles:
                                o = kt * L.TB + qt * P - (P * kt if masked else 0)
                                i = nc.tensor.transpose(k.ps[:, 4 + j, o:o + P],
                                                        k.Pb[:, u % 2, 2 * j + qt, kt * P:(kt + 1) * P], k.ident[:])
                            i.then_inc(k.pT_ready, 1)
                    for a in range(2):
                        if s == START[a]:
                            pe.wait_ge(*used)
                            for q in range(L.nt):
                                for c in range(L.NC):
                                    o = a * L.TB + q * P
                                    i = nc.tensor.matmul(k.ps[:, 7, q * D:(q + 1) * D], OT[:, c, o:o + P], wo[:, c, :],
                                                         start=c == 0, stop=c == L.NC - 1)
                            i.then_inc(k.out_ready, 1)
                            if L.selected:
                                pe.wait_ge(k.sel_ready, 2 * TT + a + 1)
                                for q in range(2):
                                    t = 2 * a + q
                                    i = nc.tensor.matmul(k.ps[:, 7, q * D:(q + 1) * D], selT[:, t * P:(t + 1) * P],
                                                         k.O[:, 2 + a, 0:D], start=True, stop=True)
                                i.then_inc(k.res_ready, 1)
                            used = (k.x_done, a + 1)
                    u = s - 2
                    if 0 <= u < L.NS:
                        a, g = divmod(u, L.G)
                        n, first, last = u // L.CS, u % L.CS == 0, u % L.CS == L.CS - 1
                        if first and n:
                            pe.wait_ge(k.o_copied, n)
                        for j in range(2):
                            h = 2 * g + j
                            pe.wait_ge(k.pT_copied_a if j else k.pT_copied_v, u + 1)
                            for kt in range(L.nt):
                                q0 = P * kt if masked else 0
                                if L.wide:
                                    v = Vm[:, ((a * L.nt + kt) * L.H + h) * P:][:, 0:P]
                                    out = k.ps[:, 6, q0:L.TB]
                                    start, stop = first and j == 0 and kt == 0, last and j == 1 and kt == L.nt - 1
                                else:
                                    v = k.V[:, a * L.nt + kt, h // L.rep * L.dh:(h // L.rep + 1) * L.dh]
                                    r = h % L.per * L.dh
                                    out = k.ps[r:r + L.dh, 6, q0:L.TB]
                                    start, stop = kt == 0, kt == L.nt - 1
                                i = nc.tensor.matmul(out, v, k.PT[:, u % 2, j, kt * L.TB:(kt + 1) * L.TB - q0],
                                                     start=start, stop=stop, skip_group_check=True)
                        i.then_inc(k.av_ready, 1)
                        if last:
                            if used:
                                pe.wait_ge(*used)
                            pe.wait_ge(k.rexp_ready, L.nt * (n + 1))
                            for q in range(L.nt):
                                i = nc.tensor.transpose(k.ps[:, 7, q * P:(q + 1) * P], k.rexp[:, n % 2, q, :], k.ident[:])
                            i.then_inc(k.r_ready, 1)
                            used = (k.av_normed, n + 1)

            @block.vector
            def _(dve):
                if L.normed:
                    for t in range(TT):
                        norm_stats(k, dve, k.h[:, t, :], t)
                    norm_root(k, dve)
                    for t in range(TT):
                        norm_apply(k, dve, k.h[:, t, :], h2, t)
                if L.selected:
                    for t in range(TT):
                        nc.vector.tensor_tensor_reduce(scratch[:, t, :], k.h[:, t, :], k.w(layer, "wg", A), 1.0, 0.0,
                                                       ALU.mult, ALU.add, Z[:, t:t + 1]).then_inc(k.chain_v, 1)
                    dve.wait_ge(k.gate_exp, 1)
                    nc.vector.tensor_scalar(R1, EX, 1.0, None, ALU.add).then_inc(k.chain_v, 1)
                    dve.wait_ge(k.chain_v, TT + 1)
                    nc.vector.reciprocal(GATE, R1).then_inc(k.chain_v, 1)
                    dve.wait_ge(k.chain_v, TT + 2)
                    for t in range(TT):
                        nc.vector.tensor_copy(k.O[:, t, 0:P], GATE[:, t:t + 1].to_broadcast([P, P])).then_inc(k.sel_ready, 1)
                for n, (kind, c, engine) in enumerate(prep.steps):
                    if engine != "v":
                        continue
                    src = k.ps[:, n % 8, :]
                    dve.wait_ge(k.prod_ready, n + 1)
                    if kind == "gate":
                        for t in range(TT):
                            G = src[:, (t // 2) * S:(t // 2 + 1) * S]
                            nc.vector.tensor_scalar(k.O[:, t, 256:512], G, GATE[:, t:t + 1], None, ALU.is_gt, ALU.add,
                                                    accum_out=R1[:, t:t + 1]).then_inc(k.chain_v, 1)
                            nc.vector.scalar_tensor_tensor(out=k.O[:, t, 512:768], in0=G, scalar=GATE[:, t:t + 1],
                                                           in1=k.before[:, t % 2, :], op0=ALU.is_equal, op1=ALU.mult,
                                                           accum_out=R2[:, t:t + 1]).then_inc(k.chain_v, 1)
                        dve.wait_ge(k.chain_v, 3 * TT + 2)
                        nc.vector.tensor_tensor(RANK, R1, R2, ALU.add).then_inc(k.chain_v, 1)
                        dve.wait_ge(k.chain_v, 3 * TT + 3)
                        for t in range(TT):
                            i = nc.vector.tensor_scalar(sel[:, t * P:(t + 1) * P], k.iota[:], RANK[:, t:t + 1], None,
                                                        ALU.is_equal)
                            i.then_inc(k.sel_ready, 1)
                        nc.vector.tensor_copy(k.small[:, 6, 0:1], src[:, 0:1]).then_inc(k.copied_v, 1)
                        continue
                    if kind == "hT":
                        if L.normed:
                            i = nc.vector.tensor_scalar(k.hT[:, c, :], src, k.w(layer, "lnw", A)[:, c:c + 1],
                                                        k.w(layer, "lnb", A)[:, c:c + 1], ALU.mult, ALU.add)
                        else:
                            i = nc.vector.tensor_copy(k.hT[:, c, 0:NT], src[:, 0:NT])
                    elif kind == "qkT" and c >= L.nch:
                        i = nc.vector.tensor_copy(KT[:, c - L.nch, :], src)
                    elif kind in ("q", "qkT"):
                        for j in range(L.per):
                            h = c * L.per + j
                            if kind == "q" and L.qkv_bias:
                                i = nc.vector.tensor_scalar(k.QT[:, h, 0:NT], src[:, 0:NT], k.hm[:, j:j + 1],
                                                            k.bqm[:, h:h + 1], ALU.mult, ALU.add)
                            else:
                                i = nc.vector.tensor_scalar(k.QT[:, h, 0:NT], src[:, 0:NT], k.hm[:, j:j + 1], None,
                                                            ALU.mult)
                    elif kind == "v" and L.wide:
                        t, c0, w = c
                        for m in range(L.nch):
                            o = V0 + (t * L.H + m * L.per) * P
                            to = W[:, o:o + L.per * (P + L.dh)].rearrange("p (i x) -> p i x", x=P + L.dh)[:, :, 0:L.dh]
                            kh = L.per // L.rep
                            to = to.rearrange("p (v r) d -> p v r d", v=kh)
                            wide = [P, kh, L.rep, L.dh]
                            cut = slice(m * kh * L.dh, (m + 1) * kh * L.dh)
                            mine = src[:, cut].rearrange("p (v d) -> p v d", d=L.dh).unsqueeze(2).to_broadcast(wide)
                            if L.qkv_bias:
                                bv = k.w(layer, "bv", A)[:, cut].rearrange("p (v d) -> p v d", d=L.dh)
                                i = nc.vector.tensor_tensor(to, mine, bv.unsqueeze(2).to_broadcast(wide), ALU.add)
                            else:
                                i = nc.vector.tensor_copy(to, mine)
                    elif kind == "v":
                        t, c0, w = c
                        if L.qkv_bias:
                            i = nc.vector.tensor_tensor(k.V[:, t, c0:c0 + w], src[:, 0:w],
                                                        k.w(layer, "bv", A)[:, c0:c0 + w], ALU.add)
                        else:
                            i = nc.vector.tensor_copy(k.V[:, t, c0:c0 + w], src[:, 0:w])
                    elif kind == "qk":
                        i = nc.vector.tensor_tensor(k.PT[:, c // 2, c % 2, :], src, k.w(layer, "bqk", A), ALU.add)
                    i.then_inc(k.copied_v, 1)
                    if kind == "qk":
                        qk, sq = k.PT[:, c // 2, c % 2, :], k.Pb[:, c // 2, 2 * (c % 2):2 * (c % 2) + 2, :]
                        dve.wait_ge(k.copied_v, prep.copied(n + 1, "v"))
                        nc.vector.tensor_tensor(sq, qk.rearrange("p (a b) -> p a b", a=2),
                                                qk.rearrange("p (a b) -> p a b", a=2), ALU.mult).then_inc(k.chain_v, 1)
                        dve.wait_ge(k.chain_v, 3 * c + 1)
                        ss = k.nm[:, 8 * (c % 2):8 * (c % 2) + 8, :].rearrange("p a b -> p (a b)")
                        if c >= 2:
                            ss = k.sums[:, 8 * (c % 2):8 * (c % 2) + 8, :].rearrange("p a b -> p (a b)")
                        nc.vector.tensor_reduce(ss, sq.rearrange("p a (j d) -> p (a j) d", d=L.dh), AX.X,
                                                ALU.add).then_inc(k.chain_v, 1)
                        dve.wait_ge(k.chain_v, 3 * c + 2)
                        nc.vector.tensor_scalar(ss, ss, 1e-24, None, ALU.max).then_inc(k.chain_v, 1)
                    if kind == "v" and L.normed and c[0] == TT - 1:
                        for m, buf in enumerate((k.nm, k.sums)):
                            flat = buf[:].rearrange("p a b -> p (a b)")
                            inv = k.rs[:].rearrange("p a b -> p (a b)")
                            dve.wait_ge(k.chain_v, 6 * (m + 1))
                            if m:
                                dve.wait_ge(k.sel_ready, 2)
                            inverse_root(k, dve, flat, inv, k.rt[:], ROOT * (m + 1))
                            for t in range(2 * m, 2 * m + 2):
                                qk = k.PT[:, t // 2, t % 2, :].rearrange("p (j d) -> p j d", d=L.dh)
                                rn = k.rs[:, 8 * (t % 2):8 * (t % 2) + 8, :].rearrange("p a b -> p (a b)")
                                nc.vector.tensor_tensor(qkn[:, t, :].rearrange("p (j d) -> p j d", d=L.dh), qk,
                                                        rn.unsqueeze(2).to_broadcast([P, 2 * L.H, L.dh]),
                                                        ALU.mult).then_inc(k.sel_ready, 1)
                ahead = TT + TT + 1 if L.normed else 0
                roots = 3 * ROOT if L.normed else 0
                for s in range(STEPS):
                    if L.NS - 7 <= s < L.NS - 2:
                        if s == L.NS - 4 and L.res_h:
                            dve.wait_ge(k.res_ready, 1)
                        norm_ahead(k, dve, lambda t: k.X[:, (pair + 1) % NPAIR, t, :], s - L.NS + 7, ahead, roots)
                    if s < L.NS and not L.normed:
                        for j in range(2):
                            dve.wait_ge(k.scores_ready, 2 * s + j + 1)
                            src = k.ps[:, 2 * (s % 2) + j, 0:L.nt * L.TB].rearrange("p (q n) -> p q n", q=L.nt)
                            nc.vector.tensor_reduce(k.nm[:, s, 2 * j:2 * j + L.nt], src, AX.X, ALU.max,
                                                    negate=True).then_inc(k.negmax_ready, 1)
                    u = s - 1
                    if 0 <= u < L.NS:
                        dve.wait_ge(k.pT_ready, 2 * u + 1)
                        if u >= 2:
                            dve.wait_ge(k.av_ready, u - 1)
                        nc.vector.tensor_copy(seen(k.PT[:, u % 2, 0, :]), seen(k.ps[:, 4, :])).then_inc(k.pT_copied_v, 1)
                    if 0 <= u < L.NS and u % L.CS == L.CS - 1:
                        n = u // L.CS
                        dve.wait_ge(k.probs_ready, L.E * (u + 1))
                        rv, sm = (x[:, n * L.CS:(n + 1) * L.CS, :].rearrange("p s (j q) -> p (s j) q", j=2)[:, :, 0:L.nt]
                                  for x in (k.rs, k.sums))
                        nc.vector.reciprocal(rv, sm).then_inc(k.rsum_ready, 1)
                    for a in range(2):
                        if s == START[a]:
                            dve.wait_ge(k.out_ready, a + 1)
                            if L.selected:
                                nc.vector.tensor_copy(k.O[:, 2 + a, 0:D], k.ps[:, 7, 0:D]).then_inc(k.sel_ready, 1)
                                dve.wait_ge(k.res_ready, a + 1)
                                for q in range(2):
                                    t = 2 * a + q
                                    i = nc.vector.scalar_tensor_tensor(
                                        out=k.X[:, pair, t, :], in0=k.ps[:, 7, q * D:(q + 1) * D],
                                        scalar=GATE[:, t:t + 1], in1=k.X[:, pair, t, :], op0=ALU.mult, op1=ALU.add)
                            else:
                                dve.wait_ge(k.res_ready, L.res_h + L.out_bias)
                                i = nc.vector.tensor_tensor(
                                    k.X[:, pair, 2 * a:2 * a + 2, :], k.ps[:, 7, :].rearrange("p (q d) -> p q d", q=2),
                                    k.res[:, 2 * a:2 * a + 2, :], ALU.add)
                            i.then_inc(k.x_done, 1)
                    u = s - 2
                    if 0 <= u < L.NS and u % L.CS == L.CS - 1:
                        n = u // L.CS
                        a, c = divmod(n, L.NC)
                        dve.wait_ge(k.o_copied, n + 1)
                        dve.wait_ge(k.r_ready, n + 1)
                        nc.vector.tensor_tensor(OT[:, c, a * L.TB:(a + 1) * L.TB], k.ob[:, n % 2, 0:L.TB],
                                                k.ps[:, 7, 0:L.TB], ALU.mult).then_inc(k.av_normed, 1)
        k.clear()


def mixer(k, layer):
    nc = k.nc
    wr, wk, wv = (k.w(layer, n, MIX).rearrange("p (c n) -> p c n", c=KD) for n in ("wr", "wk", "wv"))
    mur, muk = k.w(layer, "mur", MIX), k.w(layer, "muk", MIX)
    XR, XK = k.QT[:, 0:KD, :], k.KT[:, 0:KD, :]
    relu = k.QT[:, KD:2 * KD, :]
    kact = k.KT[:, KD:2 * KD, :]
    ez = k.O[:, :, 0:D]
    r = k.O[:, :, D:2 * D]
    prod = k.O[:, :, 2 * D:3 * D]
    omr, omk = k.small[:, 0, 0:KD], k.small[:, 1, 0:KD]

    def tok(bank):
        return k.ps[:, bank, :].rearrange("p (q d) -> p q d", q=2)

    with nc.Fori(0, NPAIR) as pair:
        with nc.Block() as block:
            @block.scalar
            def _(act):
                act.wait_ge(k.prod_ready, 2)
                nc.scalar.activation(k.hT[:, 1, :], k.ps[:, 1, :], ACT.Copy).then_inc(k.copied_a, 1)
                for c in range(KD):
                    act.wait_ge(k.prod_ready, 3 + c)
                    nc.scalar.activation(relu[:, c, :], k.ps[:, 2 + c, :], ACT.Relu).then_inc(k.chain_a, 1)
                    act.wait_ge(k.chain_a, 1 + c)
                    nc.scalar.activation(kact[:, c, :], relu[:, c, :], ACT.Square).then_inc(k.copied_a, 1)
                for b in range(2):
                    act.wait_ge(k.prod_ready, 5 + b)
                    nc.scalar.activation(ez[:, 2 * b:2 * b + 2, :], tok(4 + b), ACT.Exp,
                                         scale=-1.0).then_inc(k.copied_a, 1)

            @block.tensor
            def _(pe):
                for c in range(KD):
                    for t in range(TT):
                        i = nc.tensor.transpose(k.ps[:, c, t * P:(t + 1) * P], k.h[:, t, c * P:(c + 1) * P], k.ident[:])
                    i.then_inc(k.prod_ready, 1)
                pe.wait_ge(k.sel_ready, 2)
                for c in range(KD):
                    for m in range(KD):
                        i = nc.tensor.matmul(k.ps[:, 2 + c, :], wk[:, m, c * P:(c + 1) * P], XK[:, m, :],
                                             start=m == 0, stop=m == KD - 1)
                    i.then_inc(k.prod_ready, 1)
                pe.wait_ge(k.sel_ready, 4)
                for t in range(TT):
                    for m in range(KD):
                        i = nc.tensor.matmul(tok(4 + t // 2)[:, t % 2, :], XR[:, m, t * P:(t + 1) * P], wr[:, m, :],
                                             start=m == 0, stop=m == KD - 1)
                    if t % 2:
                        i.then_inc(k.prod_ready, 1)
                pe.wait_ge(k.copied_a, 3)
                for t in range(TT):
                    for m in range(KD):
                        i = nc.tensor.matmul(tok(6 + t // 2)[:, t % 2, :], kact[:, m, t * P:(t + 1) * P], wv[:, m, :],
                                             start=m == 0, stop=m == KD - 1)
                    if t % 2:
                        i.then_inc(k.prod_ready, 1)

            @block.vector
            def _(dve):
                nc.vector.tensor_scalar(omr, mur, -1.0, 1.0, ALU.mult, ALU.add).then_inc(k.chain_v, 1)
                nc.vector.tensor_scalar(omk, muk, -1.0, 1.0, ALU.mult, ALU.add).then_inc(k.chain_v, 1)
                dve.wait_ge(k.prod_ready, 1)
                nc.vector.tensor_copy(k.hT[:, 0, :], k.ps[:, 0, :]).then_inc(k.copied_v, 1)
                dve.wait_ge(k.copied_v, 1)
                dve.wait_ge(k.copied_a, 1)
                n = 2
                for to, mu, om in ((XK, muk, omk), (XR, mur, omr)):
                    for c in range(KD):
                        nc.vector.tensor_scalar(to[:, c, :], k.hT[:, c, :], mu[:, c:c + 1], None,
                                                ALU.mult).then_inc(k.chain_v, 1)
                    for c in range(KD):
                        n += 1
                        dve.wait_ge(k.chain_v, n)
                        x = to[:, c, :].rearrange("p (b s) -> p b s", b=2)[:, :, 1:S]
                        before = k.hT[:, c, :].rearrange("p (b s) -> p b s", b=2)[:, :, 0:S - 1]
                        nc.vector.scalar_tensor_tensor(out=x, in0=before, scalar=om[:, c:c + 1], in1=x, op0=ALU.mult,
                                                       op1=ALU.add).then_inc(k.sel_ready, 1)
                for part in range(5):
                    if part == 3:
                        dve.wait_ge(k.prod_ready, 2)
                    norm_ahead(k, dve, lambda t: k.X[:, (pair + 1) % NPAIR, t, :], part)
                for b in range(2):
                    two = slice(2 * b, 2 * b + 2)
                    dve.wait_ge(k.copied_a, 4 + b)
                    nc.vector.tensor_scalar(ez[:, two, :], ez[:, two, :], 1.0, None, ALU.add).then_inc(k.chain_v, 1)
                    dve.wait_ge(k.chain_v, 7 + 3 * b)
                    nc.vector.reciprocal(r[:, two, :], ez[:, two, :]).then_inc(k.chain_v, 1)
                    dve.wait_ge(k.chain_v, 8 + 3 * b)
                    dve.wait_ge(k.prod_ready, 7 + b)
                    nc.vector.tensor_tensor(prod[:, two, :], tok(6 + b), r[:, two, :], ALU.mult).then_inc(k.chain_v, 1)
                    dve.wait_ge(k.chain_v, 9 + 3 * b)
                    nc.vector.tensor_tensor(k.X[:, pair, two, :], k.X[:, pair, two, :], prod[:, two, :],
                                            ALU.add).then_inc(k.x_done, 1)
        k.clear()


class Route:

    def __init__(self, k):
        self.lg, self.e, self.pr = (k.small[:, 8 * n:8 * n + 8, :].rearrange("p a b -> p (a b)").rearrange(
            "p (t e) -> p t e", e=NE) for n in range(3))
        self.mx, self.sm, self.ri = (k.rs[:, n, :] for n in range(3))
        self.rank = k.nm[:, 0:8, :].rearrange("p a b -> p (a b)").rearrange("p (t e) -> p t e", e=NE)
        self.G = k.Pb[:, 0, 0, :].rearrange("p (t e j) -> p t e j", t=TT, e=NE)
        self.Q = k.Pb[:, 0, 1, :].rearrange("p (t e j) -> p t e j", t=TT, e=NE)

    def vector(self, k, dve, logits, pr):
        nc = k.nc
        spread = [P, TT, NE]
        nc.vector.tensor_reduce(self.mx, logits, AX.X, ALU.max, negate=True).then_inc(k.chain_v, 1)
        dve.wait_ge(k.chain_v, 1)
        nc.vector.tensor_tensor(self.lg, logits, self.mx.unsqueeze(2).to_broadcast(spread), ALU.add).then_inc(k.chain_v, 1)
        dve.wait_ge(k.chain_a, 1)
        nc.vector.tensor_reduce(self.sm, self.e, AX.X, ALU.add).then_inc(k.chain_v, 1)
        dve.wait_ge(k.chain_v, 3)
        nc.vector.reciprocal(self.ri, self.sm).then_inc(k.chain_v, 1)
        dve.wait_ge(k.chain_v, 4)
        nc.vector.tensor_tensor(pr, self.e, self.ri.unsqueeze(2).to_broadcast(spread), ALU.mult).then_inc(k.chain_v, 1)
        dve.wait_ge(k.chain_v, 5)
        for t in range(TT):
            other = pr[:, t, :].unsqueeze(1).to_broadcast([P, NE, NE])
            own = pr[:, t, :].unsqueeze(2).to_broadcast([P, NE, NE])
            nc.vector.tensor_tensor(self.G[:, t], other, own, ALU.is_gt)
            nc.vector.tensor_tensor(self.Q[:, t], other, own, ALU.is_equal).then_inc(k.chain_v, 1)
        dve.wait_ge(k.chain_v, 9)
        q = self.Q.rearrange("p t e j -> p t (e j)")
        nc.vector.tensor_tensor(q, q, k.first8[:].rearrange("p e j -> p (e j)").unsqueeze(1).to_broadcast([P, TT, NE * NE]),
                                ALU.mult).then_inc(k.chain_v, 1)
        dve.wait_ge(k.chain_v, 10)
        g = self.G.rearrange("p t e j -> p t (e j)")
        nc.vector.tensor_tensor(g, g, q, ALU.add).then_inc(k.chain_v, 1)
        dve.wait_ge(k.chain_v, 11)
        nc.vector.tensor_reduce(self.rank.rearrange("p t e -> p (t e)"),
                                self.G.rearrange("p t e j -> p (t e) j"), AX.X, ALU.add).then_inc(k.chain_v, 1)
        dve.wait_ge(k.chain_v, 12)

    def scalar(self, k, act):
        act.wait_ge(k.chain_v, 2)
        k.nc.scalar.activation(self.e, self.lg, ACT.Exp).then_inc(k.chain_a, 1)


def composed(k, layer):
    nc = k.nc
    at, n = MOE2["wc"]
    wc = k.arena[layer % 2][:, at:at + n].rearrange("p (m n) -> p m n", m=KD)
    wg = k.w(layer, "wg", MOE2).rearrange("p (m e) -> p m e", m=KD)
    slots = [k.W[:, n * 4096:(n + 1) * 4096] for n in range(5)]
    NSLOT = len(slots)
    with nc.Block() as block:
        @block.sync
        def _(sp):
            for e in range(NE):
                if e >= NSLOT:
                    sp.wait_ge(k.prod_ready, KD * (e - NSLOT + 1))
                sp.dma_start(slots[e % NSLOT], k.dram["moe2"][e]).then_inc(k.expert_in[e], 16)

        @block.tensor
        def _(pe):
            for e in range(NE):
                pe.wait_ge(k.expert_in[e], 16)
                up = slots[e % NSLOT][:, 0:FC * D].rearrange("p (f d) -> p f d", f=FC)
                down = slots[e % NSLOT][:, FC * D:].rearrange("p (f d) -> p f d", f=FC)
                for m in range(KD):
                    if e >= 4:
                        pe.wait_ge(k.copied_a if m else k.copied_v, e - 3)
                    for f in range(FC):
                        i = nc.tensor.matmul(k.ps[:, (KD * e + m) % 8, 0:D], up[:, f, m * P:(m + 1) * P], down[:, f, :],
                                             start=f == 0, stop=f == FC - 1)
                    i.then_inc(k.prod_ready, 1)

        @block.vector
        def _(dve):
            for e in range(NE):
                dve.wait_ge(k.prod_ready, KD * e + 1)
                nc.vector.tensor_copy(wc[:, 0, e * D:(e + 1) * D], k.ps[:, KD * e % 8, 0:D]).then_inc(k.copied_v, 1)

        @block.scalar
        def _(act):
            for e in range(NE):
                act.wait_ge(k.prod_ready, KD * e + 2)
                nc.scalar.activation(wc[:, 1, e * D:(e + 1) * D], k.ps[:, (KD * e + 1) % 8, 0:D],
                                     ACT.Copy).then_inc(k.copied_a, 1)
    k.clear()

    route = Route(k)
    mask = k.sums[:, 0:8, :].rearrange("p a b -> p (a b)").rearrange("p (t e) -> p t e", e=NE)
    with nc.Fori(0, NPAIR) as pair:
        with nc.Block() as block:
            @block.scalar
            def _(act):
                act.wait_ge(k.prod_ready, 2)
                nc.scalar.activation(k.hT[:, 1, :], k.ps[:, 1, :], ACT.Copy).then_inc(k.copied_a, 1)
                route.scalar(k, act)

            @block.tensor
            def _(pe):
                for c in range(KD):
                    for t in range(TT):
                        i = nc.tensor.transpose(k.ps[:, c, t * P:(t + 1) * P], k.h[:, t, c * P:(c + 1) * P], k.ident[:])
                    i.then_inc(k.prod_ready, 1)
                pe.wait_ge(k.copied_v, 1)
                pe.wait_ge(k.copied_a, 1)
                for t in range(TT):
                    for m in range(KD):
                        i = nc.tensor.matmul(k.ps[:, 2, t * NE:(t + 1) * NE], k.hT[:, m, t * P:(t + 1) * P], wg[:, m, :],
                                             start=m == 0, stop=m == KD - 1)
                i.then_inc(k.prod_ready, 1)
                n = 0
                for e in range(0, NE, 2):
                    for t in range(TT):
                        if n >= 5:
                            pe.wait_ge(k.x_done, 2 * (n - 4))
                        for m in range(KD):
                            i = nc.tensor.matmul(k.ps[:, 3 + n % 5, :], k.hT[:, m, t * P:(t + 1) * P],
                                                 wc[:, m, e * D:(e + 2) * D], start=m == 0, stop=m == KD - 1)
                        i.then_inc(k.out_ready, 1)
                        n += 1

            @block.vector
            def _(dve):
                dve.wait_ge(k.prod_ready, 1)
                nc.vector.tensor_copy(k.hT[:, 0, :], k.ps[:, 0, :]).then_inc(k.copied_v, 1)
                dve.wait_ge(k.prod_ready, 3)
                route.vector(k, dve, k.ps[:, 2, 0:TT * NE].rearrange("p (t e) -> p t e", e=NE), route.pr)
                nc.vector.tensor_scalar(mask, route.rank, 1.5, None, ALU.is_lt).then_inc(k.chain_v, 1)
                for part in range(5):
                    norm_ahead(k, dve, lambda t: k.X[:, (pair + 1) % NPAIR, t, :], part)
                dve.wait_ge(k.chain_v, 13)
                n = 0
                for e in range(0, NE, 2):
                    for t in range(TT):
                        dve.wait_ge(k.out_ready, n + 1)
                        for i in range(2):
                            done = 2 * n - 7 if i == 0 else 2 * n + 1
                            if done > 0:
                                dve.wait_ge(k.x_done, done)
                            nc.vector.scalar_tensor_tensor(
                                out=k.X[:, pair, t, :], in0=k.ps[:, 3 + n % 5, i * D:(i + 1) * D],
                                scalar=mask[:, t, e + i:e + i + 1], in1=k.X[:, pair, t, :], op0=ALU.mult,
                                op1=ALU.add).then_inc(k.x_done, 1)
                        n += 1
        k.clear()


def capacity(k, layer):
    nc = k.nc
    U32 = mybir.dt.uint32
    NTT = T // P
    xb, yb = k.xb, k.yb
    wr = k.w(layer, "wr", MOE3).rearrange("p (m e) -> p m e", m=KD)
    bias = k.w(layer, "bias", MOE3)
    HB = k.KT[:].rearrange("p c n -> p (c n)").rearrange("p (t d) -> p t d", d=D)
    HP = HB.rearrange("p (g t) d -> p g t d", t=TT)
    flat = k.res[:].rearrange("p t d -> p (t d)")

    def part(n):
        return flat[:, n * NTT * NE:(n + 1) * NTT * NE].rearrange("p (t e) -> p t e", e=NE)

    PR, M1, M2, ALLM, POS, SLOT, TMP, BASE = (part(n) for n in range(8))
    sk = [k.st2[:, n, :] for n in range(2)]
    wk = [k.st2[:, 2 + n, :] for n in range(2)]
    tmp = k.st2[:, 4, :]
    idx = [k.idx[:, n, :] for n in range(4)]
    A0, A1 = k.arena[(layer + 1) % 2], k.arena[layer % 2]
    first = MOE3_WIDTH
    slots = [A0[:, 0:2 * FC * D], A0[:, 2 * FC * D:4 * FC * D], A1[:, first:first + 2 * FC * D],
             k.W[:, 0:4096], k.W[:, 4096:8192], k.W[:, 16384:20480]]
    NSLOT = len(slots)
    zero = k.V[:].rearrange("p c n -> p (c n)")

    with nc.Block() as block:
        @block.vector
        def _(dve):
            nc.vector.memset(zero, 0.0).then_inc(k.zeroed, 1)

        @block.sync
        def _(sp):
            sp.wait_ge(k.zeroed, 1)
            for n in range(2):
                sp.dma_start(xb.rearrange("(p c) d -> p (c d)", p=P)[:, n * 4096:(n + 1) * 4096],
                             zero).then_inc(k.zero_in, 16)
            for e in range(NSLOT):
                sp.dma_start(slots[e], k.dram["moe3"][e]).then_inc(k.expert_in[NE + e], 16)

    route = Route(k)
    with nc.Fori(0, NPAIR) as pair:
        with nc.Block() as block:
            pp = [x.rearrange("p (g t) e -> p g t e", t=TT)[:, pair, :, :] for x in (PR, M1, M2)]

            @block.scalar
            def _(act):
                act.wait_ge(k.prod_ready, 2)
                nc.scalar.activation(k.hT[:, 1, :], k.ps[:, 1, :], ACT.Copy).then_inc(k.copied_a, 1)
                route.scalar(k, act)

            @block.gpsimd
            def _(pool):
                nc.gpsimd.tensor_copy(HP[:, pair, :, :], k.h[:]).then_inc(k.res_ready, 1)
                nc.gpsimd.tensor_tensor(k.X[:, pair, :, :], k.X[:, pair, :, :],
                                        bias.unsqueeze(1).to_broadcast([P, TT, D]), ALU.add).then_inc(k.x_done, 1)

            @block.tensor
            def _(pe):
                for c in range(KD):
                    for t in range(TT):
                        i = nc.tensor.transpose(k.ps[:, c, t * P:(t + 1) * P], k.h[:, t, c * P:(c + 1) * P], k.ident[:])
                    i.then_inc(k.prod_ready, 1)
                pe.wait_ge(k.copied_v, 1)
                pe.wait_ge(k.copied_a, 1)
                for t in range(TT):
                    for m in range(KD):
                        i = nc.tensor.matmul(k.ps[:, 2, t * NE:(t + 1) * NE], k.hT[:, m, t * P:(t + 1) * P], wr[:, m, :],
                                             start=m == 0, stop=m == KD - 1)
                i.then_inc(k.prod_ready, 1)

            @block.vector
            def _(dve):
                dve.wait_ge(k.prod_ready, 1)
                nc.vector.tensor_copy(k.hT[:, 0, :], k.ps[:, 0, :]).then_inc(k.copied_v, 1)
                dve.wait_ge(k.prod_ready, 3)
                route.vector(k, dve, k.ps[:, 2, 0:TT * NE].rearrange("p (t e) -> p t e", e=NE), route.pr)
                nc.vector.tensor_copy(pp[0], route.pr).then_inc(k.chain_v, 1)
                nc.vector.tensor_scalar(pp[1], route.rank, 0.0, None, ALU.is_equal).then_inc(k.chain_v, 1)
                nc.vector.tensor_scalar(pp[2], route.rank, 1.0, None, ALU.is_equal).then_inc(k.chain_v, 1)
                dve.wait_ge(k.res_ready, 1)
                for part in range(5):
                    norm_ahead(k, dve, lambda t: k.X[:, (pair + 1) % NPAIR, t, :], part)
        k.clear()

    def one(x):
        return x.rearrange("p t e -> p (t e)")

    with nc.Block() as block:
        @block.tensor
        def _(pe):
            pe.wait_ge(k.chain_v, 1)
            nc.tensor.matmul(k.ps[:, 0, 0:P], k.upper[:], one(ALLM), start=True, stop=True)
            nc.tensor.matmul(k.ps[:, 1, 0:P], k.ones[:], one(ALLM), start=True, stop=True).then_inc(k.prod_ready, 1)

        @block.vector
        def _(dve):
            n = [0]

            def then(i):
                n[0] += 1
                i.then_inc(k.chain_v, 1)
                dve.wait_ge(k.chain_v, n[0])

            then(nc.vector.tensor_tensor(ALLM, M1, M2, ALU.add))
            then(nc.vector.memset(BASE[:, 0, :], 0.0))
            dve.wait_ge(k.prod_ready, 1)
            tot = k.ps[:, 1, 0:P].rearrange("p (t e) -> p t e", e=NE)
            for t in range(1, NTT):
                then(nc.vector.tensor_tensor(BASE[:, t, :], BASE[:, t - 1, :], tot[:, t - 1, :], ALU.add))
            then(nc.vector.tensor_tensor(one(POS), k.ps[:, 0, 0:P], one(BASE), ALU.add))
            then(nc.vector.tensor_scalar(TMP, POS, float(CAP), 4.0 * NE * CAP, ALU.is_ge, ALU.mult))
            then(nc.vector.tensor_tensor(SLOT, POS, TMP, ALU.add))
            then(nc.vector.tensor_tensor(SLOT, SLOT, k.starts[:].unsqueeze(1).to_broadcast([P, NTT, NE]), ALU.add))
            for c, M in enumerate((M1, M2)):
                then(nc.vector.tensor_tensor(TMP, M, SLOT, ALU.mult))
                then(nc.vector.tensor_reduce(sk[c], TMP, AX.X, ALU.add))
                then(nc.vector.tensor_copy(idx[c], sk[c]))
                then(nc.vector.tensor_scalar(tmp, sk[c], NE * CAP - 1.0, None, ALU.min))
                then(nc.vector.tensor_copy(idx[2 + c], tmp))
                then(nc.vector.tensor_tensor(TMP, M, PR, ALU.mult))
                then(nc.vector.tensor_reduce(wk[c], TMP, AX.X, ALU.add))
                then(nc.vector.tensor_scalar(tmp, sk[c], float(NE * CAP), None, ALU.is_lt))
                then(nc.vector.tensor_tensor(wk[c], wk[c], tmp, ALU.mult))
    k.clear()

    xe = [k.Pb[:, n, :, :] for n in range(2)]
    xeT = [k.PT[:, n, :, :] for n in range(2)]
    gT = [k.KT, k.V[:].rearrange("p t (a n) -> p (t a) n", a=2)]
    ysb = [k.h[:], k.cT[:].rearrange("p c (t d) -> p (c t) d", d=D)]
    back = A0[:, 0:2 * NTT * D].rearrange("p (n d) -> p n d", d=D)
    with nc.Block() as block:
        @block.gpsimd
        def _(pool):
            pool.wait_ge(k.zero_in, 32)
            for t in range(NTT):
                for c in range(2):
                    nc.gpsimd.indirect_dma_start(
                        out=xb, out_offset=bass.IndirectOffsetOnAxis(ap=idx[c][:, t:t + 1], axis=0), in_=HB[:, t, :],
                        in_offset=None, bounds_check=NE * CAP - 1, oob_is_err=False).then_inc(k.scattered, 16)
            pool.wait_ge(k.stored, 16 * NE)
            for t in range(NTT):
                for c in range(2):
                    nc.gpsimd.indirect_dma_start(
                        out=back[:, 2 * t + c, :], out_offset=None, in_=yb,
                        in_offset=bass.IndirectOffsetOnAxis(ap=idx[2 + c][:, t:t + 1], axis=0),
                        bounds_check=NE * CAP - 1, oob_is_err=False).then_inc(k.gathered[t], 16)

        @block.sync
        def _(sp):
            sp.wait_ge(k.scattered, 16 * 2 * NTT)
            for e in range(NE):
                if e >= 2:
                    sp.wait_ge(k.prod_ready, KD * (e - 1))
                sp.dma_start(xe[e % 2], xb[e * CAP:(e + 1) * CAP, :].rearrange("(t p) d -> p t d", p=P)
                             ).then_inc(k.rows_in[e % 2], 16)
                if NSLOT <= e + 2 < NE:
                    sp.wait_ge(k.out_ready, 2 * (e + 3 - NSLOT))
                    sp.dma_start(slots[(e + 2) % NSLOT], k.dram["moe3"][e + 2]).then_inc(k.expert_in[NE + e + 2], 16)
                if e >= 1:
                    sp.wait_ge(k.chain_v, 2 * e)
                    sp.dma_start(yb[(e - 1) * CAP:e * CAP, :].rearrange("(t p) d -> p t d", p=P),
                                 ysb[(e - 1) % 2]).then_inc(k.stored, 16)
            sp.wait_ge(k.chain_v, 2 * NE)
            sp.dma_start(yb[(NE - 1) * CAP:NE * CAP, :].rearrange("(t p) d -> p t d", p=P),
                         ysb[(NE - 1) % 2]).then_inc(k.stored, 16)

        @block.tensor
        def _(pe):
            for e in range(NE):
                w = slots[e % NSLOT]
                w1 = w[:, 0:KD * F].rearrange("p (m f) -> p m f", m=KD)
                w2 = w[:, KD * F:].rearrange("p (f d) -> p f d", f=FC)
                pe.wait_ge(k.rows_in[e % 2], 16 * (e // 2 + 1))
                if e >= 1:
                    pe.wait_ge(k.copied_v, KD * e)
                for c in range(KD):
                    for t in range(TT):
                        i = nc.tensor.transpose(k.ps[:, c, t * P:(t + 1) * P], xe[e % 2][:, t, c * P:(c + 1) * P],
                                                k.ident[:])
                    i.then_inc(k.prod_ready, 1)
                pe.wait_ge(k.copied_v, KD * (e + 1))
                pe.wait_ge(k.expert_in[NE + e], 16)
                for f in range(FC):
                    n = e * FC + f
                    if n >= 4:
                        pe.wait_ge(k.copied_a, n - 3)
                    for m in range(KD):
                        i = nc.tensor.matmul(k.ps[:, 2 + n % 4, :], w1[:, m, f * P:(f + 1) * P], xeT[e % 2][:, m, :],
                                             start=m == 0, stop=m == KD - 1)
                    i.then_inc(k.scores_ready, 1)
                pe.wait_ge(k.copied_a, FC * (e + 1))
                for b in range(2):
                    if e >= 1:
                        pe.wait_ge(k.chain_v, 2 * e + b - 1)
                    for q in range(2):
                        t = 2 * b + q
                        for f in range(FC):
                            i = nc.tensor.matmul(k.ps[:, 6 + b, q * D:(q + 1) * D], gT[e % 2][:, f, t * P:(t + 1) * P],
                                                 w2[:, f, :], start=f == 0, stop=f == FC - 1)
                    i.then_inc(k.out_ready, 1)

        @block.scalar
        def _(act):
            for e in range(NE):
                if e >= 2:
                    act.wait_ge(k.out_ready, 2 * (e - 1))
                for f in range(FC):
                    n = e * FC + f
                    act.wait_ge(k.scores_ready, n + 1)
                    nc.scalar.activation(gT[e % 2][:, f, :], k.ps[:, 2 + n % 4, :], ACT.Gelu_apprx_tanh
                                         ).then_inc(k.copied_a, 1)

        @block.vector
        def _(dve):
            for e in range(NE):
                for c in range(KD):
                    dve.wait_ge(k.prod_ready, KD * e + c + 1)
                    nc.vector.tensor_copy(xeT[e % 2][:, c, :], k.ps[:, c, :]).then_inc(k.copied_v, 1)
                if e >= 2:
                    dve.wait_ge(k.stored, 16 * (e - 1))
                for b in range(2):
                    dve.wait_ge(k.out_ready, 2 * e + b + 1)
                    nc.vector.tensor_copy(ysb[e % 2][:, 2 * b:2 * b + 2, :],
                                          k.ps[:, 6 + b, :].rearrange("p (q d) -> p q d", q=2)).then_inc(k.chain_v, 1)
            X = k.X[:].rearrange("p g t d -> p (g t) d")
            for t in range(NTT):
                dve.wait_ge(k.gathered[t], 32)
                for c in range(2):
                    if c:
                        dve.wait_ge(k.x_done, 2 * t + 1)
                    nc.vector.scalar_tensor_tensor(out=X[:, t, :], in0=back[:, 2 * t + c, :], scalar=wk[c][:, t:t + 1],
                                                   in1=X[:, t, :], op0=ALU.mult, op1=ALU.add).then_inc(k.x_done, 1)
    k.clear()


def finish(k, out):
    nc = k.nc
    with nc.Block() as block:
        @block.sync
        def _(sp):
            sp.dma_start(out, k.X[:]).then_inc(k.x_out, 16)
            sp.wait_ge(k.x_out, 16)


LIST = list(range(12))


def program(nc, dram, out):
    with ExitStack() as ctx:
        k = Core(nc, ctx, dram)
        constants(k)
        for n in LIST:
            weights(k, n)
            if n in ATTN:
                attention(k, n)
            else:
                {2: mixer, 8: composed, 11: capacity}[n](k, n)
        finish(k, out)


def _rows(w, r=P):
    c = w.shape[0] // r
    w = w.reshape(c, r, -1).transpose(1, 0, 2).reshape(r, -1)
    full = np.zeros((P, w.shape[1]), np.float32)
    full[0:r] = w
    return full


def _copies(w, L):
    w = w.reshape(-1, L.kvh, 1, L.dh)
    return np.broadcast_to(w, (w.shape[0], L.kvh, L.rep, L.dh)).reshape(w.shape[0], L.inner)


def _cols(b):
    return np.ascontiguousarray(b.reshape(-1, P).T)


def _spread(b):
    return np.broadcast_to(b.reshape(1, -1), (P, b.size))


def _pack_attn(L, a):
    n = L.name + "_"
    parts = []
    if L.normed:
        w, b = a[n + "qkv_w"].T, a[n + "qkv_b"]
        parts = [_rows(w[:, 0:2 * D]), _rows(w[:, 2 * D:]), _rows(a[n + "out_w"].T), _spread(b[0:2 * D]),
                 _spread(b[2 * D:]), _spread(a[n + "out_b"]), _cols(a[n + "ln_w"]), _cols(a[n + "ln_b"])]
        return np.concatenate(parts, axis=1)
    if L.name == "L2_attn":
        w, b = a["L2_attn_W_qkv"], a["L2_attn_b_qkv"]
        wq, wk, wv, wo = w[:, 0:D], w[:, D:2 * D], w[:, 2 * D:], a["L2_attn_W_proj"]
        bq, bk, bv, bo = b[0:D], b[D:2 * D], b[2 * D:], a["L2_attn_b_proj"]
    else:
        wq, wk, wv, wo = (a[n + x] for x in ("Wq", "Wk", "Wv", "Wo"))
        if L.name == "L0_xattn":
            wq, wk, wv, wo = wq.T, wk.T, wv.T, wo.T
        if L.qkv_bias:
            bq, bk, bv = (a[n + x] for x in ("bq", "bk", "bv"))
        if L.out_bias:
            bo = a[n + "bo"]
    parts = [_rows(wq), _rows(_copies(wk, L), L.kr),
             _rows(wv, L.kr), _rows(wo)]
    if L.qkv_bias:
        parts += [_cols(bq), _cols(_copies(bk, L)), _spread(bv)]
    if L.out_bias:
        parts += [_spread(bo)]
    if L.selected:
        parts += [_spread(a[n + "Wg"])]
    return np.concatenate(parts, axis=1)


def _layout(a):
    out = {"x": a["x"].reshape(NPAIR, TT, P, D).transpose(2, 0, 1, 3),
           "ctxT": a["ctx_768"].reshape(NPAIR, 2 * S, KD, CR).transpose(0, 3, 2, 1)}
    for n, L in ATTN.items():
        out[f"w{n}"] = _pack_attn(L, a)
    out["w2"] = np.concatenate([_rows(a["L0_ffn_W_r"].T), _rows(a["L0_ffn_W_k"].T), _rows(a["L0_ffn_W_v"].T),
                                _cols(a["L0_ffn_mu_r"]), _cols(a["L0_ffn_mu_k"])], axis=1)
    out["w8"] = _rows(a["L2_ffn_gate_w"].T)
    out["moe2"] = np.stack([np.concatenate([_rows(a["L2_ffn_w_up"][e].T), _rows(a["L2_ffn_w_down"][e])], axis=1)
                            for e in range(NE)])
    out["w11"] = np.concatenate([_rows(a["L3_ffn_w_router"]), _spread(a["L3_ffn_bias"])], axis=1)
    out["moe3"] = np.stack([np.concatenate([_rows(a["L3_ffn_w1"][e]), _rows(a["L3_ffn_w2"][e])], axis=1)
                            for e in range(NE)])
    return {n: np.ascontiguousarray(v) for n, v in out.items()}


def kernel(**inputs):
    import concourse.bacc as bacc
    from concourse.bass_utils import run_bass_kernel_spmd

    arrays = _layout({n: np.asarray(v) for n, v in inputs.items()})
    nc = bacc.Bacc("TRN2", target_bir_lowering=False, num_devices=1)
    dram = {n: nc.dram_tensor(n, v.shape, mybir.dt.from_np(v.dtype), kind="ExternalInput").ap()
            for n, v in arrays.items()}
    out = nc.dram_tensor("out", (P, NPAIR, TT, D), F32, kind="ExternalOutput").ap()
    program(nc, dram, out)
    r = run_bass_kernel_spmd(nc, [arrays], core_ids=[0])
    return np.ascontiguousarray(r.results[0]["out"].transpose(1, 2, 0, 3)).reshape(B, S, D)
```

```python
from contextlib import ExitStack

import numpy as np
import concourse.bass as bass
from concourse import mybir

ALU = mybir.AluOpType
ACT = mybir.ActivationFunctionType
AX = mybir.AxisListType
F32 = mybir.dt.float32
BF16 = mybir.dt.bfloat16
I32 = mybir.dt.int32

P = 128
B, S, D = 8, 256, 256
DC = 192
CR = DC // 2
T = B * S
NPAIR = B // 2
TT = 2 * S // P
KD = D // P
BANK = 512
EPS = 1e-5
MASKED = -1.0e30
NE = 8
F = 1024
FC = F // P
CAP = 2 * T // NE
ARENA = 8448


class Attn:

    def __init__(self, name, heads, dh, scale, ctx=False, mask=None, kv_heads=None, qkv_bias=False,
                 out_bias=False, res_h=False, normed=False, selected=False):
        self.name, self.H, self.dh, self.scale, self.ctx, self.mask = name, heads, dh, scale, ctx, mask
        self.qkv_bias, self.out_bias, self.res_h = qkv_bias, out_bias, res_h
        self.normed, self.selected = normed, selected
        self.per = P // dh
        self.nch = heads // self.per
        self.kvh = kv_heads or heads
        self.rep = heads // self.kvh
        self.NV = self.kvh * dh
        self.inner = heads * dh
        self.NC = self.inner // P
        self.CS = self.per // 2
        self.wide = dh == 16 and not normed
        self.G = heads // 2
        self.NS = 2 * self.G
        self.TB = P if selected else S
        self.nt = self.TB // P
        self.E = 2 * self.nt
        self.kr = CR if ctx else P
        at = 0
        self.at = {}
        nq = self.nch * P
        for key, n in (("wq", KD * (2 * D if normed else nq)), ("wk", 0 if normed else KD * nq),
                       ("wv", KD * self.NV), ("wo", self.NC * D),
                       ("bq", self.nch if qkv_bias and not normed else 0),
                       ("bk", self.nch if qkv_bias and not normed else 0),
                       ("bqk", 2 * D if normed else 0), ("bv", self.NV if qkv_bias else 0),
                       ("bo", D if out_bias else 0), ("lnw", KD if normed else 0),
                       ("lnb", KD if normed else 0), ("wg", D if selected else 0)):
            self.at[key] = (at, n)
            at += n
        self.width = at
        assert at <= ARENA


ATTN = {
    0: Attn("L0_attn", 16, 16, 0.25, mask="window", kv_heads=4, qkv_bias=True, out_bias=True),
    1: Attn("L0_xattn", 8, 32, float(32.0 ** -0.5), ctx=True, qkv_bias=True, out_bias=True),
    3: Attn("L1_attn", 16, 16, 4.0, qkv_bias=True, out_bias=True, res_h=True, normed=True),
    4: Attn("L1_xattn", 16, 64, 0.125, ctx=True, out_bias=True),
    5: Attn("L1_ffn", 16, 16, 0.25, selected=True),
    6: Attn("L2_attn", 16, 16, 0.25, qkv_bias=True, out_bias=True),
    7: Attn("L2_xattn", 16, 64, 0.125, ctx=True, out_bias=True),
    9: Attn("L3_attn", 16, 64, 0.125, mask="causal", res_h=True),
    10: Attn("L3_xattn", 8, 64, 0.125, ctx=True, out_bias=True),
}
MIX = {"wr": (0, KD * D), "wk": (KD * D, KD * D), "wv": (2 * KD * D, KD * D),
       "mur": (3 * KD * D, KD), "muk": (3 * KD * D + KD, KD)}
MIX_WIDTH = 3 * KD * D + 2 * KD
MOE2 = {"wg": (0, KD * NE), "wc": (KD * NE, NE * KD * D)}
MOE2_WIDTH = KD * NE
MOE3 = {"wr": (0, KD * NE), "bias": (KD * NE, D)}
MOE3_WIDTH = KD * NE + D
LAYERS = 12
WIDTH = {**{n: a.width for n, a in ATTN.items()}, 2: MIX_WIDTH, 8: MOE2_WIDTH, 11: MOE3_WIDTH}


class Core:

    def __init__(self, nc, ctx, dram):
        self.nc, self.dram = nc, dram

        def sb(name, shape, dt=F32):
            return ctx.enter_context(nc.sbuf_tensor(name, shape, dt))

        self.X = sb("X", [P, NPAIR, TT, D])
        self.arena = [sb(f"arena{n}", [P, ARENA]) for n in range(2)]
        self.W = sb("work", [P, 5 * 4096])
        W = self.W
        self.QT = W[:, 0:8192].rearrange("p (c n) -> p c n", n=BANK)
        self.KT = W[:, 8192:12288].rearrange("p (c n) -> p c n", n=BANK)
        self.V = W[:, 12288:16384].rearrange("p (t n) -> p t n", t=TT)
        self.O = W[:, 16384:20480].rearrange("p (t n) -> p t n", t=TT)
        self.ob = sb("ob", [P, 2, S])
        self.rexp = sb("rexp", [P, 2, 2, P])
        self.hm = sb("hm", [P, 8])
        self.bqm = sb("bqm", [P, 16])
        self.ind = {d: sb(f"ind{d}", [P, P // d]) for d in (16, 32, 64)}
        self.Pb = sb("Pb", [P, 2, 4, S])
        self.PT = sb("PT", [P, 2, 2, BANK])
        self.h = sb("h", [P, TT, D])
        self.hT = sb("hT", [P, KD, BANK])
        self.cT = sb("cT", [P, KD, BANK])
        self.res = sb("res", [P, TT, D])
        self.st = sb("st", [P, TT, 6])
        self.mv = sb("mv", [P, TT, 2])
        self.var = sb("var", [P, TT])
        self.rstd = sb("rstd", [P, TT])
        self.rt = sb("rt", [P, 64])
        self.nm = sb("nm", [P, 16, 4])
        self.sums = sb("sums", [P, 16, 4])
        self.rs = sb("rs", [P, 16, 4])
        self.small = sb("small", [P, 24, TT])
        self.ident = sb("ident", [P, P])
        self.identb = sb("identb", [P, P], BF16)
        self.mask = {m: sb(f"mask_{m}", [P, 2, S], BF16) for m in ("causal", "window")}
        self.before = sb("before", [P, 2, S])
        self.iota = sb("iota", [P, P])
        self.first8 = sb("first8", [P, NE, NE])
        self.upper = sb("upper", [P, P])
        self.ones = sb("ones", [P, P])
        self.starts = sb("starts", [P, NE])
        self.st2 = sb("st2", [P, 5, T // P])
        self.idx = sb("idx", [P, 4, T // P], mybir.dt.uint32)
        self.xb = nc.dram_tensor("xb", (NE * CAP, D), F32, kind="Internal").ap()
        self.yb = nc.dram_tensor("yb", (NE * CAP, D), F32, kind="Internal").ap()
        self.ps = ctx.enter_context(nc.psum_tensor("ps", [P, 8, BANK], F32))
        def sem(name):
            return ctx.enter_context(nc.semaphore(name))

        self.ctx_in = sem("ctx_in")
        self.stats = sem("stats")
        self.root_step = sem("root_step")
        self.gate_exp = sem("gate_exp")
        self.h_ready = sem("h_ready")
        self.res_ready = sem("res_ready")
        self.prod_ready = sem("prod_ready")
        self.copied_v = sem("copied_v")
        self.copied_a = sem("copied_a")
        self.scores_ready = sem("scores_ready")
        self.negmax_ready = sem("negmax_ready")
        self.probs_ready = sem("probs_ready")
        self.pT_ready = sem("pT_ready")
        self.pT_copied_v = sem("pT_copied_v")
        self.pT_copied_a = sem("pT_copied_a")
        self.av_ready = sem("av_ready")
        self.rsum_ready = sem("rsum_ready")
        self.av_normed = sem("av_normed")
        self.out_ready = sem("out_ready")
        self.o_copied = sem("o_copied")
        self.rexp_ready = sem("rexp_ready")
        self.r_ready = sem("r_ready")
        self.x_done = sem("x_done")
        self.chain_v = sem("chain_v")
        self.chain_a = sem("chain_a")
        self.sel_ready = sem("sel_ready")
        self.scattered = sem("scattered")
        self.stored = sem("stored")
        self.loop_sems = (self.ctx_in, self.stored)
        self.loop_count = 28
        self.x_in = sem("x_in")
        self.x_rest = sem("x_rest")
        self.consts = sem("consts")
        self.w_in = [sem(f"w_in{n}") for n in range(LAYERS)]
        self.expert_in = [sem(f"expert_in{n}") for n in range(2 * NE)]
        self.rows_in = [sem(f"rows_in{n}") for n in range(2)]
        self.gathered = [sem(f"gathered{n}") for n in range(T // P)]
        self.zeroed = sem("zeroed")
        self.zero_in = sem("zero_in")
        self.x_out = sem("x_out")

    def clear(self):
        first, last = self.loop_sems[0].num, self.loop_sems[1].num
        assert last - first + 1 == self.loop_count
        self.nc.all_engine_barrier(sems_to_clear=range(first, last + 1))

    def w(self, layer, key, where, rows=P):
        at, n = where[key]
        return self.arena[layer % 2][0:rows, at:at + n]


def constants(k):
    nc = k.nc
    with nc.Block() as block:
        @block.sync
        def _(sp):
            sp.dma_start(k.X[:, 0, :, :], k.dram["x"][:, 0]).then_inc(k.x_in, 16)
            sp.dma_start(k.arena[ORDER[0] % 2][:, 0:WIDTH[ORDER[0]]],
                         k.dram[f"w{ORDER[0]}"]).then_inc(k.w_in[ORDER[0]], 16)
            sp.dma_start(k.X[:, 1:NPAIR, :, :], k.dram["x"][:, 1:NPAIR]).then_inc(k.x_rest, 16)

        @block.vector
        def _(dve):
            dve.wait_ge(k.x_in, 16)
            for part in range(5):
                norm_ahead(k, dve, lambda t: k.X[:, 0, t, :], part)

        @block.gpsimd
        def _(pool):
            nc.gpsimd.memset(k.ident[:], 0.0).then_inc(k.consts, 1)
            nc.gpsimd.memset(k.mask["causal"][:], 0.0).then_inc(k.consts, 1)
            nc.gpsimd.memset(k.before[:], 1.0).then_inc(k.consts, 1)
            nc.gpsimd.iota(k.iota[:], pattern=[[1, P]], base=0, channel_multiplier=0,
                           allow_small_or_imprecise_dtypes=True).then_inc(k.consts, 1)
            nc.gpsimd.memset(k.first8[:], 1.0).then_inc(k.consts, 1)
            nc.gpsimd.memset(k.ones[:], 1.0).then_inc(k.consts, 1)
            nc.gpsimd.iota(k.starts[:], pattern=[[CAP, NE]], base=0, channel_multiplier=0,
                           allow_small_or_imprecise_dtypes=True).then_inc(k.consts, 1)
            nc.gpsimd.memset(k.ind[16][:], 1.0).then_inc(k.consts, 1)
            nc.gpsimd.memset(k.ind[32][:], 1.0).then_inc(k.consts, 1)
            nc.gpsimd.memset(k.ind[64][:], 1.0).then_inc(k.consts, 1)
            pool.wait_ge(k.consts, 10)
            for n, (d, ind) in enumerate(k.ind.items()):
                nc.gpsimd.affine_select(out=ind[:], in_=ind[:], compare_op=ALU.is_ge, fill=0.0, base=0,
                                        pattern=[[-d, P // d]], channel_multiplier=1).then_inc(k.consts, 1)
                pool.wait_ge(k.consts, 11 + 2 * n)
                nc.gpsimd.affine_select(out=ind[:], in_=ind[:], compare_op=ALU.is_ge, fill=0.0, base=d - 1,
                                        pattern=[[d, P // d]], channel_multiplier=-1).then_inc(k.consts, 1)
            nc.gpsimd.affine_select(out=k.first8[:], in_=k.first8[:], compare_op=ALU.is_ge, fill=0.0, base=-1,
                                    pattern=[[1, NE], [-1, NE]], channel_multiplier=0).then_inc(k.consts, 1)
            nc.gpsimd.affine_select(out=k.upper[:], in_=k.ones[:], compare_op=ALU.is_ge, fill=0.0, base=-1,
                                    pattern=[[1, P]], channel_multiplier=-1).then_inc(k.consts, 1)
            nc.gpsimd.affine_select(out=k.ident[:], in_=k.ident[:], compare_op=ALU.not_equal, fill=1.0, base=0,
                                    pattern=[[-1, P]], channel_multiplier=1).then_inc(k.consts, 1)
            nc.gpsimd.affine_select(out=k.mask["causal"][:], in_=k.mask["causal"][:], compare_op=ALU.is_ge,
                                    fill=MASKED, base=0, pattern=[[P, 2], [-1, S]],
                                    channel_multiplier=1).then_inc(k.consts, 1)
            nc.gpsimd.affine_select(out=k.before[:], in_=k.before[:], compare_op=ALU.is_ge, fill=0.0, base=-1,
                                    pattern=[[P, 2], [-1, S]], channel_multiplier=1).then_inc(k.consts, 1)
            pool.wait_ge(k.consts, 21)
            nc.gpsimd.tensor_copy(k.identb[:], k.ident[:]).then_inc(k.consts, 1)
            nc.gpsimd.affine_select(out=k.mask["window"][:], in_=k.mask["causal"][:], compare_op=ALU.is_ge,
                                    fill=MASKED, base=P - 1, pattern=[[-P, 2], [1, S]],
                                    channel_multiplier=-1).then_inc(k.consts, 1)
    k.clear()


def weights(k, layer):
    nc = k.nc
    with nc.Block() as block:
        @block.sync
        def _(sp):
            if layer + 1 in ORDER:
                sp.dma_start(k.arena[(layer + 1) % 2][:, 0:WIDTH[layer + 1]],
                             k.dram[f"w{layer + 1}"]).then_inc(k.w_in[layer + 1], 16)
            if layer + 1 == 8:
                first = sum(MOE2["wc"])
                sp.dma_start(k.arena[(layer + 1) % 2][:, first:first + 2 * FC * D],
                             k.dram["moe2"][0]).then_inc(k.expert_in[0], 16)
            sp.wait_ge(k.w_in[layer], 16)


MAGIC = float(0x5F3759DF)


def inverse_root(k, dve, v, y, t, done=0):
    nc = k.nc
    bits = mybir.dt.uint32
    nc.vector.tensor_scalar(t.bitcast(bits), v.bitcast(bits), 1, None, ALU.logical_shift_right).then_inc(k.root_step, 1)
    dve.wait_ge(k.root_step, done + 1)
    nc.vector.tensor_scalar(y.bitcast(bits), t.bitcast(bits), -1.0, MAGIC, ALU.mult, ALU.add).then_inc(k.root_step, 1)
    for n in range(3):
        dve.wait_ge(k.root_step, done + 3 * n + 2)
        nc.vector.tensor_tensor(t, y, y, ALU.mult).then_inc(k.root_step, 1)
        dve.wait_ge(k.root_step, done + 3 * n + 3)
        nc.vector.scalar_tensor_tensor(out=t, in0=t, scalar=-0.5, in1=v, op0=ALU.mult, op1=ALU.mult
                                       ).then_inc(k.root_step, 1)
        dve.wait_ge(k.root_step, done + 3 * n + 4)
        nc.vector.scalar_tensor_tensor(out=y, in0=t, scalar=1.5, in1=y, op0=ALU.add, op1=ALU.mult
                                       ).then_inc(k.root_step, 1)
    dve.wait_ge(k.root_step, done + 11)


ROOT = 11


def norm_stats(k, dve, src, t):
    k.nc.vector.bn_stats(k.st[:, t, :], src).then_inc(k.stats, 1)


def norm_root(k, dve, done=0, roots=0):
    nc = k.nc
    for t in range(TT):
        dve.wait_ge(k.stats, done + t + 1)
        nc.vector.bn_aggr(k.mv[:, t, :], k.st[:, t, :]).then_inc(k.stats, 1)
    dve.wait_ge(k.stats, done + 2 * TT)
    nc.vector.tensor_scalar(k.var[:], k.mv[:, :, 1], EPS, None, ALU.add).then_inc(k.stats, 1)
    dve.wait_ge(k.stats, done + 2 * TT + 1)
    inverse_root(k, dve, k.var[:], k.rstd[:], k.rt[:, 0:TT], roots)


def norm_apply(k, dve, src, dst, t):
    k.nc.vector.tensor_scalar(dst[:, t, :], src, k.mv[:, t, 0:1], k.rstd[:, t:t + 1],
                              ALU.subtract, ALU.mult).then_inc(k.h_ready, 1)


def norm_ahead(k, dve, src, part, done=0, roots=0):
    if part < 2:
        for t in (2 * part, 2 * part + 1):
            norm_stats(k, dve, src(t), t)
    elif part == 2:
        norm_root(k, dve, done, roots)
    elif part < 5:
        for t in (2 * part - 6, 2 * part - 5):
            norm_apply(k, dve, src(t), k.h, t)


class Prep:

    def __init__(self, L):
        self.steps = []
        if L.selected:
            self.steps += [("gate", 0, "v"), ("selT", 0, "a"), ("hT", 0, "v"), ("hT", 1, "a")]
        if L.normed:
            self.steps += [("qk", t, "v") for t in range(TT)]
            self.steps += [("v", (t, 0, L.NV), "a") for t in range(2 * L.nt)]
            self.steps += [("qkT", c, "av"[c % 2]) for c in range(2 * L.nch)]
        else:
            self.steps += [("q", c, "va"[c % 2]) for c in range(L.nch)]
            self.steps += [("k", c, "a") for c in range(L.nch)]
            self.steps += [("v", (t, c, min(BANK, L.NV)), "v") for t in range(2 * L.nt)
                           for c in range(0, L.NV, BANK)]

    def bank(self, n):
        return (n - len(self.steps)) % 8

    def copied(self, n, engine):
        return sum(1 for s in self.steps[0:n] if s[2] == engine)

    def all(self, kind):
        return max(n for n, s in enumerate(self.steps) if s[0] == kind) + 1


def attention(k, layer):
    nc, L = k.nc, ATTN[layer]
    prep = Prep(L)
    N = len(prep.steps)
    NT = 2 * L.TB
    A = L.at
    wq = k.w(layer, "wq", A).rearrange("p (c n) -> p c n", c=KD)
    wv = k.w(layer, "wv", A, L.kr).rearrange("p (c n) -> p c n", c=KD)
    wo = k.w(layer, "wo", A).rearrange("p (c n) -> p c n", c=L.NC)
    if not L.normed:
        wk = k.w(layer, "wk", A, L.kr).rearrange("p (c n) -> p c n", c=KD)
    kv_in = k.cT if L.ctx else k.hT
    kr = L.kr
    masked = L.mask is not None
    tiles = [(kt, qt) for kt in range(L.nt) for qt in range(L.nt) if not (masked and kt > qt)]
    START = [(a + 1) * L.G + 3 for a in range(2)]
    STEPS = START[1] + 1
    W = k.W

    def seen(x):
        return x[:, 0:len(tiles) * P]

    if L.wide:
        KT = W[:, 8192:9216].rearrange("p (c n) -> p c n", n=BANK)
        V0 = 9216
        VM_V = L.nt * L.H * P // 2
        Vm = W[:, V0:V0 + 2 * L.nt * L.H * P]
        OT = W[:, 17408 if L.nt == 2 else 13312:][:, 0:L.NC * NT].rearrange("p (c n) -> p c n", n=NT)
    elif L.normed:
        VS = W[:, 9216:9216 + TT * L.H * 32].rearrange("p (t c b i x) -> p t c b i x", t=TT, c=L.nch, b=2, i=4)
        KT = W[:, 8192:9216].rearrange("p (c n) -> p c n", n=BANK)
        OT = W[:, 17408:18432].rearrange("p (c n) -> p c n", n=NT)
    else:
        KT = k.KT
        OT = k.O.rearrange("p t n -> p (t n)")[:, 0:L.NC * NT].rearrange("p (c n) -> p c n", n=NT)
    h2 = W[:, 18432:19456].rearrange("p (t d) -> p t d", d=D)
    qkn = W[:, 18432:20480].rearrange("p (t n) -> p t n", t=TT)
    Z, EX, GATE, R1, R2, RANK = (k.small[:, n, :] for n in range(6))
    selT = k.cT[:, 0, :]
    sel = k.cT[:, 1, :]
    scratch = k.res
    move = [W[:, 16384 + b * P:16384 + (b + 1) * P] for b in range(2)]
    mine = [k.small[:, 7, b:b + 1] for b in range(2)]

    def copies(pe, n):
        for sem, engine in ((k.copied_v, "v"), (k.copied_a, "a")):
            if prep.copied(n, engine):
                pe.wait_ge(sem, prep.copied(n, engine))

    def inner_norm(dve, done, roots, rows):
        if rows:
            dve.wait_ge(k.h_ready, rows)
        for t in range(TT):
            norm_stats(k, dve, k.h[:, t, :], t)
        norm_root(k, dve, done, roots)
        for t in range(TT):
            norm_apply(k, dve, k.h[:, t, :], h2, t)

    D_START = [(a + 1) * L.G + 4 for a in range(2)]
    D_STEPS = D_START[1] + 1

    def ended(u):
        return u // L.CS if 0 <= u < L.NS and u % L.CS == L.CS - 1 else None

    def direct_tensor(pe):
        for s in range(D_STEPS):
            if s == 0:
                copies(pe, N)
            if s == L.NS + 3:
                transpose_h(pe, 2 * TT)
            if s < L.NS:
                a, g = divmod(s, L.G)
                if s >= 2:
                    pe.wait_ge(k.probs_ready, 2 * (s - 1))
                for j in range(2):
                    h = 2 * g + j
                    for kt in range(2):
                        o = a * S + kt * P
                        i = nc.tensor.matmul(k.ps[:, 2 * (s % 2) + j, kt * S:(kt + 1) * S], KT[:, h // L.per, o:o + P],
                                             k.QT[:, h, a * S:(a + 1) * S], start=True, stop=True)
                    i.then_inc(k.scores_ready, 1)
            n = ended(s - 3)
            if n is not None:
                pe.wait_ge(k.o_copied, n + 1)
                if n:
                    pe.wait_ge(k.rsum_ready, n)
                for b in range(2):
                    i = nc.tensor.matmul(k.ps[:, 6, 0:S], move[b], k.Pb[:, n % 2, b, :], start=b == 0, stop=b == 1)
                i.then_inc(k.r_ready, 1)
            for a in range(2):
                if s == D_START[a]:
                    pe.wait_ge(k.av_normed, L.nch * (a + 1))
                    if a:
                        pe.wait_ge(k.x_done, a)
                    for q in range(2):
                        for c in range(L.NC):
                            o = a * S + q * P
                            i = nc.tensor.matmul(k.ps[:, 7, q * D:(q + 1) * D], OT[:, c, o:o + P], wo[:, c, :],
                                                 start=c == 0, stop=c == L.NC - 1)
                    i.then_inc(k.out_ready, 1)
            u = s - 1
            if 0 <= u < L.NS:
                a, g = divmod(u, L.G)
                n = u // L.CS
                if u == 0:
                    pe.wait_ge(k.rexp_ready, TT)
                if n >= 2 and u % L.CS == 0:
                    pe.wait_ge(k.o_copied, n - 1)
                for j in range(2):
                    h = 2 * g + j
                    c, b, r = h // L.per, h % L.per // 4, h % 4
                    pe.wait_ge(k.probs_ready, 2 * u + j + 1)
                    for kt in range(2):
                        i = nc.tensor.matmul(k.ps[32 * r:32 * (r + 1), 4 + n % 2, b * S:(b + 1) * S],
                                             VS[:, 2 * a + kt, c, b, r, :], k.PT[:, u % 2, j, kt * S:(kt + 1) * S],
                                             start=kt == 0, stop=kt == 1, skip_group_check=True)
                i.then_inc(k.av_ready, 1)

    def direct_scalar(act):
        for s in range(D_STEPS):
            if s == L.NS + 3:
                copy_hT_a(act, N + 2)
            if s < L.NS:
                if s >= 2:
                    act.wait_ge(k.av_ready, s - 1)
                for j in range(2):
                    act.wait_ge(k.scores_ready, 2 * s + j + 1)
                    nc.scalar.activation(k.PT[:, s % 2, j, :], k.ps[:, 2 * (s % 2) + j, :],
                                         ACT.Exp).then_inc(k.probs_ready, 1)
            n = ended(s - 2)
            if n is not None:
                act.wait_ge(k.av_ready, s - 1)
                if n >= 2:
                    act.wait_ge(k.av_normed, n - 1)
                nc.scalar.activation(k.Pb[:, n % 2, 0:2, :].rearrange("p b n -> p (b n)"), k.ps[:, 4 + n % 2, :],
                                     ACT.Copy).then_inc(k.o_copied, 1)

    def direct_vector(dve):
        chain = 6
        for s in range(D_STEPS):
            if L.NS - 7 <= s < L.NS - 2:
                if s == L.NS - 4:
                    dve.wait_ge(k.res_ready, 1)
                norm_ahead(k, dve, lambda t: k.X[:, (pair + 1) % NPAIR, t, :], s - L.NS + 7, 0, 2 * ROOT)
            n = ended(s - 3)
            if n is not None:
                ob = k.ob[:, n % 2, :]
                rinv = k.rexp[:, n % 2, :, :].rearrange("p q n -> p (q n)")
                dve.wait_ge(k.o_copied, n + 1)
                nc.vector.tensor_scalar(ob, k.Pb[:, n % 2, 0, :], mine[0], None, ALU.mult).then_inc(k.chain_v, 1)
                dve.wait_ge(k.r_ready, n + 1)
                nc.vector.reciprocal(rinv, k.ps[:, 6, 0:S]).then_inc(k.rsum_ready, 1)
                dve.wait_ge(k.chain_v, chain + 2 * n + 1)
                nc.vector.scalar_tensor_tensor(out=ob, in0=k.Pb[:, n % 2, 1, :], scalar=mine[1], in1=ob,
                                               op0=ALU.mult, op1=ALU.add).then_inc(k.chain_v, 1)
                dve.wait_ge(k.chain_v, chain + 2 * n + 2)
                dve.wait_ge(k.rsum_ready, n + 1)
                a, c = divmod(n, L.nch)
                nc.vector.tensor_tensor(OT[:, c, a * S:(a + 1) * S], ob, rinv, ALU.mult).then_inc(k.av_normed, 1)
            if s == L.NS - 2:
                inner_norm(dve, 2 * TT + 1, 3 * ROOT, TT)
            if s == L.NS + 3:
                copy_hT_v(dve, N + 1)
            for a in range(2):
                if s == D_START[a]:
                    dve.wait_ge(k.res_ready, 2)
                    dve.wait_ge(k.out_ready, a + 1)
                    nc.vector.tensor_tensor(
                        k.X[:, pair, 2 * a:2 * a + 2, :], k.ps[:, 7, :].rearrange("p (q d) -> p q d", q=2),
                        k.res[:, 2 * a:2 * a + 2, :], ALU.add).then_inc(k.x_done, 1)

    def transpose_h(pe, rows):
        if rows:
            pe.wait_ge(k.h_ready, rows)
        for c in range(KD):
            for t in range(TT):
                i = nc.tensor.transpose(k.ps[:, c, t * P:(t + 1) * P], (h2 if L.normed else k.h)[:, t, c * P:(c + 1) * P],
                                        k.ident[:])
            i.then_inc(k.prod_ready, 1)

    def copy_hT_v(dve, ready):
        dve.wait_ge(k.prod_ready, ready)
        if L.normed:
            i = nc.vector.tensor_scalar(k.hT[:, 0, :], k.ps[:, 0, :], k.w(layer, "lnw", A)[:, 0:1],
                                        k.w(layer, "lnb", A)[:, 0:1], ALU.mult, ALU.add)
        else:
            i = nc.vector.tensor_copy(k.hT[:, 0, :], k.ps[:, 0, :])
        i.then_inc(k.copied_v, 1)

    def copy_hT_a(act, ready):
        act.wait_ge(k.prod_ready, ready)
        if L.normed:
            i = nc.scalar.activation(k.hT[:, 1, :], k.ps[:, 1, :], ACT.Identity, bias=k.w(layer, "lnb", A)[:, 1:2],
                                     scale=k.w(layer, "lnw", A)[:, 1:2])
        else:
            i = nc.scalar.activation(k.hT[:, 1, :], k.ps[:, 1, :], ACT.Copy)
        i.then_inc(k.copied_a, 1)

    plain = [n for n, a in ATTN.items() if not a.normed and not a.selected]
    first_hT = not L.selected and not (layer in plain and layer - 1 in plain and layer - 1 in ORDER)
    with nc.Block() as block:
        if layer == ORDER[0]:
            @block.sync
            def _(sp):
                sp.wait_ge(k.x_rest, 16)

        if first_hT:
            @block.tensor
            def _(pe):
                transpose_h(pe, TT if L.normed else 0)

            @block.scalar
            def _(act):
                copy_hT_a(act, 2)

        @block.vector
        def _(dve):
            if L.normed:
                inner_norm(dve, 0, 0, 0)
            if first_hT:
                copy_hT_v(dve, 1)
            if L.wide:
                nc.vector.memset(Vm[:, 0:VM_V], 0.0)
            if L.normed:
                dve.wait_ge(k.sel_ready, 3)
                for b in range(2):
                    nc.vector.tensor_reduce(mine[b], move[1 - b], AX.X, ALU.add)
            ind = k.ind[L.dh]
            nc.vector.tensor_scalar(k.hm[:, 0:L.per], ind[:], L.scale, None, ALU.mult).then_inc(k.chain_v, 1)
            dve.wait_ge(k.chain_v, 1)
            if L.qkv_bias and not L.normed:
                for c in range(L.nch):
                    nc.vector.tensor_scalar(k.bqm[:, c * L.per:(c + 1) * L.per], k.hm[:, 0:L.per],
                                            k.w(layer, "bq", A)[:, c:c + 1], None, ALU.mult)

        @block.gpsimd
        def _(pool):
            if L.wide:
                nc.gpsimd.memset(Vm[:, VM_V:], 0.0)
            if L.normed:
                nc.gpsimd.memset(W[:, 16384:16384 + 2 * P], 0.0).then_inc(k.sel_ready, 1)
                pool.wait_ge(k.sel_ready, 1)
                for b in range(2):
                    to = move[b].rearrange("p (i b x) -> p i b x", i=4, b=2)[:, :, b, :]
                    nc.gpsimd.affine_select(out=to, in_=to, compare_op=ALU.not_equal, fill=1.0, base=16 * b - 16,
                                            pattern=[[-32, 4], [-1, 16]], channel_multiplier=1).then_inc(k.sel_ready, 1)
                nc.gpsimd.memset(VS.rearrange("p t c b i x -> p (t c b i x)"), 1.0)
    k.clear()

    with nc.Fori(0, NPAIR) as pair:
        with nc.Block() as block:
            @block.sync
            def _(sp):
                if L.ctx:
                    sp.dma_start(k.cT[0:CR, :, :], k.dram["ctxT"][pair]).then_inc(k.ctx_in, 16)

            @block.gpsimd
            def _(pool):
                src = k.X[:, pair, :, :]
                if L.res_h:
                    nc.gpsimd.tensor_tensor(k.res[:], src, k.h[:], ALU.add).then_inc(k.res_ready, 1)
                    src = k.res[:]
                if L.out_bias:
                    bo = k.w(layer, "bo", A).unsqueeze(1).to_broadcast([P, TT, D])
                    if L.res_h:
                        pool.wait_ge(k.res_ready, 1)
                    nc.gpsimd.tensor_tensor(k.res[:], src, bo, ALU.add).then_inc(k.res_ready, 1)
                if L.normed:
                    for t in range(TT):
                        pool.wait_ge(k.copied_a, t + 1)
                        for b in range(2):
                            v = VS[:, t, :, b, :, 16 * b:16 * (b + 1)]
                            bv = k.w(layer, "bv", A).rearrange("p (c b i d) -> p c b i d", c=L.nch, b=2, i=4)[:, :, b]
                            i = nc.gpsimd.tensor_tensor(v, v, bv, ALU.add)
                        i.then_inc(k.rexp_ready, 1)
                    return
                for n in range(L.NS // L.CS):
                    pool.wait_ge(k.rsum_ready, n + 1)
                    if n >= 2:
                        pool.wait_ge(k.r_ready, n - 1)
                    for q in range(L.nt):
                        rs = k.rs[:, n * L.CS:(n + 1) * L.CS, :].rearrange("p s (j q) -> p (s j) q", j=2)[:, :, q]
                        nc.gpsimd.tensor_copy(
                            k.rexp[:, n % 2, q, :].rearrange("p (h d) -> p h d", d=L.dh),
                            rs.unsqueeze(2).to_broadcast([P, L.per, L.dh])).then_inc(k.rexp_ready, 1)

            @block.scalar
            def _(act):
                if L.selected:
                    act.wait_ge(k.chain_v, TT)
                    nc.scalar.activation(EX, Z, ACT.Exp, scale=-1.0).then_inc(k.gate_exp, 1)
                for n, (kind, c, engine) in enumerate(prep.steps):
                    if kind == "qk":
                        act.wait_ge(k.copied_v, c + 1)
                        nc.scalar.activation(k.Pb[:, c // 2, 2 * (c % 2):2 * (c % 2) + 2, :],
                                             k.PT[:, c // 2, c % 2, :].rearrange("p (a b) -> p a b", a=2),
                                             ACT.Square).then_inc(k.chain_a, 1)
                    if engine != "a":
                        continue
                    src = k.ps[:, prep.bank(n), :]
                    act.wait_ge(k.prod_ready, n + 1)
                    if kind == "hT":
                        i = nc.scalar.activation(k.hT[:, c, 0:NT], src[:, 0:NT], ACT.Copy)
                    elif kind == "selT":
                        i = nc.scalar.activation(selT, src, ACT.Copy)
                    elif kind == "k":
                        if L.qkv_bias:
                            i = nc.scalar.activation(KT[:, c, 0:NT], src[:, 0:NT], ACT.Identity,
                                                     bias=k.w(layer, "bk", A)[:, c:c + 1])
                        else:
                            i = nc.scalar.activation(KT[:, c, 0:NT], src[:, 0:NT], ACT.Copy)
                    elif kind == "v":
                        for b in range(2):
                            cut = src[:, 0:D].rearrange("p (c b i d) -> p c b i d", c=L.nch, b=2, i=4)[:, :, b]
                            i = nc.scalar.activation(VS[:, c[0], :, b, :, 16 * b:16 * (b + 1)], cut, ACT.Copy)
                    elif kind == "qkT" and c >= L.nch:
                        i = nc.scalar.activation(KT[:, c - L.nch, :], src, ACT.Copy)
                    elif kind in ("q", "qkT"):
                        for j in range(L.per):
                            h = c * L.per + j
                            if kind == "q" and L.qkv_bias:
                                i = nc.scalar.activation(k.QT[:, h, 0:NT], src[:, 0:NT], ACT.Identity,
                                                         bias=k.bqm[:, h:h + 1], scale=k.hm[:, j:j + 1])
                            else:
                                i = nc.scalar.activation(k.QT[:, h, 0:NT], src[:, 0:NT], ACT.Copy,
                                                         scale=k.hm[:, j:j + 1])
                    i.then_inc(k.copied_a, 1)
                if L.normed:
                    direct_scalar(act)
                    return
                for s in range(STEPS):
                    if s == L.NS + 2 and not L.selected:
                        copy_hT_a(act, N + 2)
                    if s < L.NS:
                        if s >= 2:
                            act.wait_ge(k.pT_ready, 2 * (s - 1))
                        for j in range(2):
                            act.wait_ge(k.negmax_ready, 2 * s + j + 1)
                            for q in range(L.nt):
                                keys = P * (q + 1) if masked else L.TB
                                m = 2 * j + q
                                nc.scalar.activation(
                                    k.Pb[:, s % 2, m, 0:keys], k.ps[:, 2 * (s % 2) + j, q * S:q * S + keys],
                                    ACT.Exp, bias=k.nm[:, s, m:m + 1],
                                    accum_out=k.sums[:, s, m:m + 1]).then_inc(k.probs_ready, 1)
                    u = s - 1
                    if 0 <= u < L.NS:
                        act.wait_ge(k.pT_ready, 2 * u + 2)
                        if u >= 2:
                            act.wait_ge(k.av_ready, u - 1)
                        nc.scalar.activation(seen(k.PT[:, u % 2, 1, :]), seen(k.ps[:, 5, :]),
                                             ACT.Copy).then_inc(k.pT_copied_a, 1)
                    u = s - 2
                    if 0 <= u < L.NS and u % L.CS == L.CS - 1:
                        n = u // L.CS
                        act.wait_ge(k.av_ready, u + 1)
                        if n >= 2:
                            act.wait_ge(k.av_normed, n - 1)
                        nc.scalar.activation(k.ob[:, n % 2, 0:L.TB], k.ps[:, 6, 0:L.TB], ACT.Copy).then_inc(k.o_copied, 1)

            @block.tensor
            def _(pe):
                for n, (kind, c, engine) in enumerate(prep.steps):
                    out = k.ps[:, prep.bank(n), :]
                    if n >= 8:
                        pe.wait_ge(k.copied_v if prep.steps[n - 8][2] == "v" else k.copied_a,
                                   prep.copied(n - 7, prep.steps[n - 8][2]))
                    if kind == "gate":
                        pe.wait_ge(k.sel_ready, TT)
                        for t in range(TT):
                            i = nc.tensor.transpose(out[:, t * P:(t + 1) * P], k.O[:, t, 0:P], k.ident[:])
                    elif kind == "selT":
                        pe.wait_ge(k.sel_ready, 2 * TT)
                        for t in range(TT):
                            i = nc.tensor.transpose(out[:, t * P:(t + 1) * P], sel[:, t * P:(t + 1) * P], k.ident[:])
                    elif kind == "hT":
                        for a in range(2):
                            for q in range(2):
                                t = 2 * a + q
                                i = nc.tensor.matmul(out[:, a * P:(a + 1) * P], k.h[:, t, c * P:(c + 1) * P],
                                                     sel[:, t * P:(t + 1) * P], start=q == 0, stop=q == 1)
                    elif kind == "qkT":
                        if c == 0:
                            pe.wait_ge(k.sel_ready, TT)
                        for t in range(TT):
                            i = nc.tensor.transpose(out[:, t * P:(t + 1) * P], qkn[:, t, c * P:(c + 1) * P], k.ident[:])
                    else:
                        if L.selected and kind == "q" and c == 0:
                            copies(pe, prep.all("hT"))
                        if kind == "k" and c == 0 and L.ctx:
                            pe.wait_ge(k.ctx_in, 16)
                        for m in range(KD):
                            if kind == "q":
                                i = nc.tensor.matmul(out[:, 0:NT], wq[:, m, c * P:(c + 1) * P], k.hT[:, m, 0:NT],
                                                     start=m == 0, stop=m == KD - 1)
                            elif kind == "k":
                                i = nc.tensor.matmul(out[:, 0:NT], wk[:, m, c * P:(c + 1) * P], kv_in[0:kr, m, 0:NT],
                                                     start=m == 0, stop=m == KD - 1)
                            elif kind == "qk":
                                i = nc.tensor.matmul(out, k.hT[:, m, c * P:(c + 1) * P], wq[:, m, :],
                                                     start=m == 0, stop=m == KD - 1)
                            else:
                                t, c0, w = c
                                i = nc.tensor.matmul(out[:, 0:w], kv_in[0:kr, m, t * P:(t + 1) * P],
                                                     wv[:, m, c0:c0 + w], start=m == 0, stop=m == KD - 1)
                    i.then_inc(k.prod_ready, 1)
                if L.normed:
                    direct_tensor(pe)
                    return
                used = None
                for s in range(STEPS):
                    if s < 2:
                        copies(pe, max(prep.all("k"), N - 6 + 2 * s))
                    if s == 2:
                        copies(pe, N)
                    if s == L.NS + 2 and not L.selected:
                        transpose_h(pe, TT)
                    if s < L.NS:
                        a, g = divmod(s, L.G)
                        if s >= 2:
                            pe.wait_ge(k.probs_ready, L.E * (s - 1))
                        for j in range(2):
                            h = 2 * g + j
                            c = h // L.per
                            bank = k.ps[:, 2 * (s % 2) + j, :]
                            if masked:
                                nc.tensor.matmul(bank, k.identb[:], k.mask[L.mask][:].rearrange("p q n -> p (q n)"),
                                                 start=True, stop=False, skip_group_check=True)
                            for q in range(L.nt):
                                keys = P * (q + 1) if masked else L.TB
                                i = nc.tensor.matmul(
                                    bank[:, q * S:q * S + keys],
                                    k.QT[:, h, a * L.TB + q * P:a * L.TB + (q + 1) * P],
                                    KT[:, c, a * L.TB:a * L.TB + keys],
                                    start=not masked, stop=True, skip_group_check=masked)
                            i.then_inc(k.scores_ready, 1)
                    u = s - 1
                    if u == 0:
                        copies(pe, N - 2)
                    if 0 <= u < L.NS:
                        for j in range(2):
                            pe.wait_ge(k.probs_ready, L.E * u + (j + 1) * L.nt)
                            if u >= 1:
                                pe.wait_ge(k.pT_copied_a if j else k.pT_copied_v, u)
                            for kt, qt in tiles:
                                o = kt * L.TB + qt * P - (P * kt if masked else 0)
                                i = nc.tensor.transpose(k.ps[:, 4 + j, o:o + P],
                                                        k.Pb[:, u % 2, 2 * j + qt, kt * P:(kt + 1) * P], k.ident[:])
                            i.then_inc(k.pT_ready, 1)
                    for a in range(2):
                        if s == START[a]:
                            pe.wait_ge(*used)
                            for q in range(L.nt):
                                for c in range(L.NC):
                                    o = a * L.TB + q * P
                                    i = nc.tensor.matmul(k.ps[:, 7, q * D:(q + 1) * D], OT[:, c, o:o + P], wo[:, c, :],
                                                         start=c == 0, stop=c == L.NC - 1)
                            i.then_inc(k.out_ready, 1)
                            if L.selected:
                                pe.wait_ge(k.sel_ready, 2 * TT + a + 1)
                                for q in range(2):
                                    t = 2 * a + q
                                    i = nc.tensor.matmul(k.ps[:, 7, q * D:(q + 1) * D], selT[:, t * P:(t + 1) * P],
                                                         k.O[:, 2 + a, 0:D], start=True, stop=True)
                                i.then_inc(k.res_ready, 1)
                            used = (k.x_done, a + 1)
                    u = s - 2
                    if 0 <= u < L.NS:
                        a, g = divmod(u, L.G)
                        n, first, last = u // L.CS, u % L.CS == 0, u % L.CS == L.CS - 1
                        if first and n:
                            pe.wait_ge(k.o_copied, n)
                        for j in range(2):
                            h = 2 * g + j
                            pe.wait_ge(k.pT_copied_a if j else k.pT_copied_v, u + 1)
                            for kt in range(L.nt):
                                q0 = P * kt if masked else 0
                                if L.wide:
                                    v = Vm[:, ((a * L.nt + kt) * L.H + h) * P:][:, 0:P]
                                    out = k.ps[:, 6, q0:L.TB]
                                    start, stop = first and j == 0 and kt == 0, last and j == 1 and kt == L.nt - 1
                                else:
                                    v = k.V[:, a * L.nt + kt, h // L.rep * L.dh:(h // L.rep + 1) * L.dh]
                                    r = h % L.per * L.dh
                                    out = k.ps[r:r + L.dh, 6, q0:L.TB]
                                    start, stop = kt == 0, kt == L.nt - 1
                                i = nc.tensor.matmul(out, v, k.PT[:, u % 2, j, kt * L.TB:(kt + 1) * L.TB - q0],
                                                     start=start, stop=stop, skip_group_check=True)
                        i.then_inc(k.av_ready, 1)
                        if last:
                            if used:
                                pe.wait_ge(*used)
                            pe.wait_ge(k.rexp_ready, L.nt * (n + 1))
                            for q in range(L.nt):
                                i = nc.tensor.transpose(k.ps[:, 7, q * P:(q + 1) * P], k.rexp[:, n % 2, q, :], k.ident[:])
                            i.then_inc(k.r_ready, 1)
                            used = (k.av_normed, n + 1)

            @block.vector
            def _(dve):
                if L.selected:
                    for t in range(TT):
                        nc.vector.tensor_tensor_reduce(scratch[:, t, :], k.h[:, t, :], k.w(layer, "wg", A), 1.0, 0.0,
                                                       ALU.mult, ALU.add, Z[:, t:t + 1]).then_inc(k.chain_v, 1)
                    dve.wait_ge(k.gate_exp, 1)
                    nc.vector.tensor_scalar(R1, EX, 1.0, None, ALU.add).then_inc(k.chain_v, 1)
                    dve.wait_ge(k.chain_v, TT + 1)
                    nc.vector.reciprocal(GATE, R1).then_inc(k.chain_v, 1)
                    dve.wait_ge(k.chain_v, TT + 2)
                    for t in range(TT):
                        nc.vector.tensor_copy(k.O[:, t, 0:P], GATE[:, t:t + 1].to_broadcast([P, P])).then_inc(k.sel_ready, 1)
                for n, (kind, c, engine) in enumerate(prep.steps):
                    if engine != "v":
                        continue
                    src = k.ps[:, prep.bank(n), :]
                    dve.wait_ge(k.prod_ready, n + 1)
                    if kind == "gate":
                        for t in range(TT):
                            G = src[:, (t // 2) * S:(t // 2 + 1) * S]
                            nc.vector.tensor_scalar(k.O[:, t, 256:512], G, GATE[:, t:t + 1], None, ALU.is_gt, ALU.add,
                                                    accum_out=R1[:, t:t + 1]).then_inc(k.chain_v, 1)
                            nc.vector.scalar_tensor_tensor(out=k.O[:, t, 512:768], in0=G, scalar=GATE[:, t:t + 1],
                                                           in1=k.before[:, t % 2, :], op0=ALU.is_equal, op1=ALU.mult,
                                                           accum_out=R2[:, t:t + 1]).then_inc(k.chain_v, 1)
                        dve.wait_ge(k.chain_v, 3 * TT + 2)
                        nc.vector.tensor_tensor(RANK, R1, R2, ALU.add).then_inc(k.chain_v, 1)
                        dve.wait_ge(k.chain_v, 3 * TT + 3)
                        for t in range(TT):
                            i = nc.vector.tensor_scalar(sel[:, t * P:(t + 1) * P], k.iota[:], RANK[:, t:t + 1], None,
                                                        ALU.is_equal)
                            i.then_inc(k.sel_ready, 1)
                        nc.vector.tensor_copy(k.small[:, 6, 0:1], src[:, 0:1]).then_inc(k.copied_v, 1)
                        continue
                    if kind == "hT":
                        i = nc.vector.tensor_copy(k.hT[:, c, 0:NT], src[:, 0:NT])
                    elif kind == "qkT" and c >= L.nch:
                        i = nc.vector.tensor_copy(KT[:, c - L.nch, :], src)
                    elif kind in ("q", "qkT"):
                        for j in range(L.per):
                            h = c * L.per + j
                            if kind == "q" and L.qkv_bias:
                                i = nc.vector.tensor_scalar(k.QT[:, h, 0:NT], src[:, 0:NT], k.hm[:, j:j + 1],
                                                            k.bqm[:, h:h + 1], ALU.mult, ALU.add)
                            else:
                                i = nc.vector.tensor_scalar(k.QT[:, h, 0:NT], src[:, 0:NT], k.hm[:, j:j + 1], None,
                                                            ALU.mult)
                    elif kind == "v" and L.wide:
                        t, c0, w = c
                        for m in range(L.nch):
                            o = V0 + (t * L.H + m * L.per) * P
                            to = W[:, o:o + L.per * (P + L.dh)].rearrange("p (i x) -> p i x", x=P + L.dh)[:, :, 0:L.dh]
                            kh = L.per // L.rep
                            to = to.rearrange("p (v r) d -> p v r d", v=kh)
                            wide = [P, kh, L.rep, L.dh]
                            cut = slice(m * kh * L.dh, (m + 1) * kh * L.dh)
                            mine = src[:, cut].rearrange("p (v d) -> p v d", d=L.dh).unsqueeze(2).to_broadcast(wide)
                            if L.qkv_bias:
                                bv = k.w(layer, "bv", A)[:, cut].rearrange("p (v d) -> p v d", d=L.dh)
                                i = nc.vector.tensor_tensor(to, mine, bv.unsqueeze(2).to_broadcast(wide), ALU.add)
                            else:
                                i = nc.vector.tensor_copy(to, mine)
                    elif kind == "v":
                        t, c0, w = c
                        if L.qkv_bias:
                            i = nc.vector.tensor_tensor(k.V[:, t, c0:c0 + w], src[:, 0:w],
                                                        k.w(layer, "bv", A)[:, c0:c0 + w], ALU.add)
                        else:
                            i = nc.vector.tensor_copy(k.V[:, t, c0:c0 + w], src[:, 0:w])
                    elif kind == "qk":
                        i = nc.vector.tensor_tensor(k.PT[:, c // 2, c % 2, :], src, k.w(layer, "bqk", A), ALU.add)
                    i.then_inc(k.copied_v, 1)
                    if kind == "qk":
                        sq = k.Pb[:, c // 2, 2 * (c % 2):2 * (c % 2) + 2, :]
                        ss = (k.sums if c >= 2 else k.nm)[:, 8 * (c % 2):8 * (c % 2) + 8, :].rearrange("p a b -> p (a b)")
                        dve.wait_ge(k.chain_a, c + 1)
                        nc.vector.tensor_reduce(ss, sq.rearrange("p a (j d) -> p (a j) d", d=L.dh), AX.X,
                                                ALU.add).then_inc(k.chain_v, 1)
                    if kind == "qk" and c % 2:
                        m = c // 2
                        flat = (k.sums if m else k.nm)[:].rearrange("p a b -> p (a b)")
                        inv = k.rs[:].rearrange("p a b -> p (a b)")
                        dve.wait_ge(k.chain_v, 3 * m + 2)
                        nc.vector.tensor_scalar(flat, flat, 1e-24, None, ALU.max).then_inc(k.chain_v, 1)
                        dve.wait_ge(k.chain_v, 3 * m + 3)
                        if m:
                            dve.wait_ge(k.sel_ready, 2)
                        inverse_root(k, dve, flat, inv, k.rt[:], ROOT * m)
                        for t in range(2 * m, 2 * m + 2):
                            qk = k.PT[:, t // 2, t % 2, :].rearrange("p (j d) -> p j d", d=L.dh)
                            rn = k.rs[:, 8 * (t % 2):8 * (t % 2) + 8, :].rearrange("p a b -> p (a b)")
                            nc.vector.tensor_tensor(qkn[:, t, :].rearrange("p (j d) -> p j d", d=L.dh), qk,
                                                    rn.unsqueeze(2).to_broadcast([P, 2 * L.H, L.dh]),
                                                    ALU.mult).then_inc(k.sel_ready, 1)
                if L.normed:
                    direct_vector(dve)
                    return
                for s in range(STEPS):
                    if L.NS - 7 <= s < L.NS - 2:
                        if s == L.NS - 4 and L.res_h:
                            dve.wait_ge(k.res_ready, 1)
                        norm_ahead(k, dve, lambda t: k.X[:, (pair + 1) % NPAIR, t, :], s - L.NS + 7)
                    if s == L.NS + 2 and not L.selected:
                        copy_hT_v(dve, N + 1)
                    if s < L.NS:
                        for j in range(2):
                            dve.wait_ge(k.scores_ready, 2 * s + j + 1)
                            src = k.ps[:, 2 * (s % 2) + j, 0:L.nt * L.TB].rearrange("p (q n) -> p q n", q=L.nt)
                            nc.vector.tensor_reduce(k.nm[:, s, 2 * j:2 * j + L.nt], src, AX.X, ALU.max,
                                                    negate=True).then_inc(k.negmax_ready, 1)
                    u = s - 1
                    if 0 <= u < L.NS:
                        dve.wait_ge(k.pT_ready, 2 * u + 1)
                        if u >= 2:
                            dve.wait_ge(k.av_ready, u - 1)
                        nc.vector.tensor_copy(seen(k.PT[:, u % 2, 0, :]), seen(k.ps[:, 4, :])).then_inc(k.pT_copied_v, 1)
                    if 0 <= u < L.NS and u % L.CS == L.CS - 1:
                        n = u // L.CS
                        dve.wait_ge(k.probs_ready, L.E * (u + 1))
                        rv, sm = (x[:, n * L.CS:(n + 1) * L.CS, :].rearrange("p s (j q) -> p (s j) q", j=2)[:, :, 0:L.nt]
                                  for x in (k.rs, k.sums))
                        nc.vector.reciprocal(rv, sm).then_inc(k.rsum_ready, 1)
                    for a in range(2):
                        if s == START[a]:
                            dve.wait_ge(k.out_ready, a + 1)
                            if L.selected:
                                nc.vector.tensor_copy(k.O[:, 2 + a, 0:D], k.ps[:, 7, 0:D]).then_inc(k.sel_ready, 1)
                                dve.wait_ge(k.res_ready, a + 1)
                                for q in range(2):
                                    t = 2 * a + q
                                    i = nc.vector.scalar_tensor_tensor(
                                        out=k.X[:, pair, t, :], in0=k.ps[:, 7, q * D:(q + 1) * D],
                                        scalar=GATE[:, t:t + 1], in1=k.X[:, pair, t, :], op0=ALU.mult, op1=ALU.add)
                            else:
                                dve.wait_ge(k.res_ready, L.res_h + L.out_bias)
                                i = nc.vector.tensor_tensor(
                                    k.X[:, pair, 2 * a:2 * a + 2, :], k.ps[:, 7, :].rearrange("p (q d) -> p q d", q=2),
                                    k.res[:, 2 * a:2 * a + 2, :], ALU.add)
                            i.then_inc(k.x_done, 1)
                    u = s - 2
                    if 0 <= u < L.NS and u % L.CS == L.CS - 1:
                        n = u // L.CS
                        a, c = divmod(n, L.NC)
                        dve.wait_ge(k.o_copied, n + 1)
                        dve.wait_ge(k.r_ready, n + 1)
                        nc.vector.tensor_tensor(OT[:, c, a * L.TB:(a + 1) * L.TB], k.ob[:, n % 2, 0:L.TB],
                                                k.ps[:, 7, 0:L.TB], ALU.mult).then_inc(k.av_normed, 1)
        k.clear()


def mixer(k, layer, out):
    nc = k.nc
    wr, wk, wv = (k.w(layer, n, MIX).rearrange("p (c n) -> p c n", c=KD) for n in ("wr", "wk", "wv"))
    mur, muk = k.w(layer, "mur", MIX), k.w(layer, "muk", MIX)
    XR, XK = k.QT[:, 0:KD, :], k.KT[:, 0:KD, :]
    relu = k.QT[:, KD:2 * KD, :]
    kact = k.KT[:, KD:2 * KD, :]
    ez = k.O[:, :, 0:D]
    r = k.O[:, :, D:2 * D]
    prod = k.O[:, :, 2 * D:3 * D]
    omr, omk = k.small[:, 0, 0:KD], k.small[:, 1, 0:KD]

    def tok(bank):
        return k.ps[:, bank, :].rearrange("p (q d) -> p q d", q=2)

    with nc.Fori(0, NPAIR) as pair:
        with nc.Block() as block:
            @block.scalar
            def _(act):
                act.wait_ge(k.prod_ready, 2)
                nc.scalar.activation(k.hT[:, 1, :], k.ps[:, 1, :], ACT.Copy).then_inc(k.copied_a, 1)
                act.wait_ge(k.copied_v, 1)
                act.wait_ge(k.copied_a, 1)
                for to, mu in ((XR, mur), (XK, muk)):
                    for c in range(KD):
                        nc.scalar.activation(to[:, c, :], k.hT[:, c, :], ACT.Copy,
                                             scale=mu[:, c:c + 1]).then_inc(k.chain_a, 1)
                for b in range(2):
                    act.wait_ge(k.prod_ready, 3 + b)
                    nc.scalar.activation(ez[:, 2 * b:2 * b + 2, :], tok(4 + b), ACT.Exp,
                                         scale=-1.0).then_inc(k.copied_a, 1)
                for c in range(KD):
                    act.wait_ge(k.prod_ready, 5 + c)
                    nc.scalar.activation(relu[:, c, :], k.ps[:, 2 + c, :], ACT.Relu).then_inc(k.chain_a, 1)
                    act.wait_ge(k.chain_a, 2 * KD + 1 + c)
                    nc.scalar.activation(kact[:, c, :], relu[:, c, :], ACT.Square).then_inc(k.copied_a, 1)

            @block.tensor
            def _(pe):
                for c in range(KD):
                    for t in range(TT):
                        i = nc.tensor.transpose(k.ps[:, c, t * P:(t + 1) * P], k.h[:, t, c * P:(c + 1) * P], k.ident[:])
                    i.then_inc(k.prod_ready, 1)
                pe.wait_ge(k.sel_ready, 2)
                for t in range(TT):
                    for m in range(KD):
                        i = nc.tensor.matmul(tok(4 + t // 2)[:, t % 2, :], XR[:, m, t * P:(t + 1) * P], wr[:, m, :],
                                             start=m == 0, stop=m == KD - 1)
                    if t % 2:
                        i.then_inc(k.prod_ready, 1)
                pe.wait_ge(k.sel_ready, 4)
                for c in range(KD):
                    for m in range(KD):
                        i = nc.tensor.matmul(k.ps[:, 2 + c, :], wk[:, m, c * P:(c + 1) * P], XK[:, m, :],
                                             start=m == 0, stop=m == KD - 1)
                    i.then_inc(k.prod_ready, 1)
                pe.wait_ge(k.copied_a, 5)
                for t in range(TT):
                    for m in range(KD):
                        i = nc.tensor.matmul(tok(6 + t // 2)[:, t % 2, :], kact[:, m, t * P:(t + 1) * P], wv[:, m, :],
                                             start=m == 0, stop=m == KD - 1)
                    if t % 2:
                        i.then_inc(k.prod_ready, 1)

            @block.vector
            def _(dve):
                nc.vector.tensor_scalar(omr, mur, -1.0, 1.0, ALU.mult, ALU.add).then_inc(k.chain_v, 1)
                nc.vector.tensor_scalar(omk, muk, -1.0, 1.0, ALU.mult, ALU.add).then_inc(k.chain_v, 1)
                dve.wait_ge(k.prod_ready, 1)
                nc.vector.tensor_copy(k.hT[:, 0, :], k.ps[:, 0, :]).then_inc(k.copied_v, 1)
                dve.wait_ge(k.copied_v, 1)
                dve.wait_ge(k.copied_a, 1)
                n = 0
                for to, om in ((XR, omr), (XK, omk)):
                    for c in range(KD):
                        n += 1
                        dve.wait_ge(k.chain_a, n)
                        x = to[:, c, :].rearrange("p (b s) -> p b s", b=2)[:, :, 1:S]
                        before = k.hT[:, c, :].rearrange("p (b s) -> p b s", b=2)[:, :, 0:S - 1]
                        nc.vector.scalar_tensor_tensor(out=x, in0=before, scalar=om[:, c:c + 1], in1=x, op0=ALU.mult,
                                                       op1=ALU.add).then_inc(k.sel_ready, 1)
                def ahead(*parts):
                    for part in parts:
                        norm_ahead(k, dve, lambda t: k.X[:, (pair + 1) % NPAIR, t, :], part)

                ahead(0, 1, 2)
                for b in range(2):
                    two = slice(2 * b, 2 * b + 2)
                    dve.wait_ge(k.copied_a, 2 + b)
                    nc.vector.tensor_scalar(ez[:, two, :], ez[:, two, :], 1.0, None, ALU.add).then_inc(k.chain_v, 1)
                    dve.wait_ge(k.chain_v, 3 + 2 * b)
                    nc.vector.reciprocal(r[:, two, :], ez[:, two, :]).then_inc(k.chain_v, 1)
                ahead(3, 4)
                for b in range(2):
                    two = slice(2 * b, 2 * b + 2)
                    dve.wait_ge(k.chain_v, 6 + b)
                    dve.wait_ge(k.prod_ready, 7 + b)
                    nc.vector.tensor_tensor(prod[:, two, :], tok(6 + b), r[:, two, :], ALU.mult).then_inc(k.chain_v, 1)
                    dve.wait_ge(k.chain_v, 7 + b)
                    nc.vector.tensor_tensor(k.X[:, pair, two, :], k.X[:, pair, two, :], prod[:, two, :],
                                            ALU.add).then_inc(k.x_done, 1)
        k.clear()


class Route:

    def __init__(self, k, tiles, lg, e, pr, rank):
        self.tiles, self.lg, self.e, self.pr, self.rank = tiles, lg, e, pr, rank
        rs = k.rs[:].rearrange("p a b -> p (a b)")
        self.mx, self.sm, self.ri = (rs[:, n * tiles:(n + 1) * tiles] for n in range(3))
        self.G, self.Q = (k.Pb[:, n, :, :].rearrange("p a b -> p (a b)")[:, 0:tiles * NE * NE].rearrange(
            "p (t e j) -> p t e j", t=tiles, e=NE) for n in range(2))

    STEPS = 9

    def vector(self, k, dve, logits):
        nc = k.nc
        spread = [P, self.tiles, NE]
        wide = [P, self.tiles, NE, NE]
        pr = self.pr
        nc.vector.tensor_reduce(self.mx, logits, AX.X, ALU.max, negate=True).then_inc(k.chain_v, 1)
        dve.wait_ge(k.chain_v, 1)
        nc.vector.tensor_tensor(self.lg, logits, self.mx.unsqueeze(2).to_broadcast(spread), ALU.add).then_inc(k.chain_v, 1)
        dve.wait_ge(k.chain_a, 1)
        nc.vector.tensor_reduce(self.sm, self.e, AX.X, ALU.add).then_inc(k.chain_v, 1)
        dve.wait_ge(k.chain_v, 3)
        nc.vector.reciprocal(self.ri, self.sm).then_inc(k.chain_v, 1)
        dve.wait_ge(k.chain_v, 4)
        nc.vector.tensor_tensor(pr, self.e, self.ri.unsqueeze(2).to_broadcast(spread), ALU.mult).then_inc(k.chain_v, 1)
        dve.wait_ge(k.chain_v, 5)
        other = pr.unsqueeze(2).to_broadcast(wide)
        own = pr.unsqueeze(3).to_broadcast(wide)
        nc.vector.tensor_tensor(self.G, other, own, ALU.is_gt)
        nc.vector.tensor_tensor(self.Q, other, own, ALU.is_equal).then_inc(k.chain_v, 1)
        dve.wait_ge(k.chain_v, 6)
        q = self.Q.rearrange("p t e j -> p t (e j)")
        nc.vector.tensor_tensor(q, q, k.first8[:].rearrange("p e j -> p (e j)").unsqueeze(1).to_broadcast(
            [P, self.tiles, NE * NE]), ALU.mult).then_inc(k.chain_v, 1)
        dve.wait_ge(k.chain_v, 7)
        g = self.G.rearrange("p t e j -> p t (e j)")
        nc.vector.tensor_tensor(g, g, q, ALU.add).then_inc(k.chain_v, 1)
        dve.wait_ge(k.chain_v, 8)
        nc.vector.tensor_reduce(self.rank.rearrange("p t e -> p (t e)"),
                                self.G.rearrange("p t e j -> p (t e) j"), AX.X, ALU.add).then_inc(k.chain_v, 1)
        dve.wait_ge(k.chain_v, 9)

    def scalar(self, k, act):
        act.wait_ge(k.chain_v, 2)
        k.nc.scalar.activation(self.e, self.lg, ACT.Exp).then_inc(k.chain_a, 1)


def composed(k, layer, out):
    nc = k.nc
    at, n = MOE2["wc"]
    wc = k.arena[layer % 2][:, at:at + n].rearrange("p (m n) -> p m n", m=KD)
    wg = k.w(layer, "wg", MOE2).rearrange("p (m e) -> p m e", m=KD)
    NSLOT = 5
    slots = [k.arena[layer % 2][:, at + n:at + n + 2 * FC * D]] + [
        k.W[:, (e - 1) % NSLOT * 2 * FC * D:((e - 1) % NSLOT + 1) * 2 * FC * D] for e in range(1, NE)]
    with nc.Block() as block:
        @block.sync
        def _(sp):
            for e in range(1, NE):
                if e > NSLOT:
                    sp.wait_ge(k.prod_ready, KD * (e - NSLOT + 1))
                sp.dma_start(slots[e], k.dram["moe2"][e]).then_inc(k.expert_in[e], 16)

        @block.tensor
        def _(pe):
            for e in range(NE):
                pe.wait_ge(k.expert_in[e], 16)
                up = slots[e][:, 0:FC * D].rearrange("p (f d) -> p f d", f=FC)
                down = slots[e][:, FC * D:].rearrange("p (f d) -> p f d", f=FC)
                for m in range(KD):
                    if e >= 4:
                        pe.wait_ge(k.copied_a if m else k.copied_v, e - 3)
                    for f in range(FC):
                        i = nc.tensor.matmul(k.ps[:, (KD * e + m) % 8, 0:D], up[:, f, m * P:(m + 1) * P], down[:, f, :],
                                             start=f == 0, stop=f == FC - 1)
                    i.then_inc(k.prod_ready, 1)

        @block.vector
        def _(dve):
            for e in range(NE):
                dve.wait_ge(k.prod_ready, KD * e + 1)
                nc.vector.tensor_copy(wc[:, 0, e * D:(e + 1) * D], k.ps[:, KD * e % 8, 0:D]).then_inc(k.copied_v, 1)

        @block.scalar
        def _(act):
            for e in range(NE):
                act.wait_ge(k.prod_ready, KD * e + 2)
                nc.scalar.activation(wc[:, 1, e * D:(e + 1) * D], k.ps[:, (KD * e + 1) % 8, 0:D],
                                     ACT.Copy).then_inc(k.copied_a, 1)
    k.clear()

    def small(x, n=0):
        return x[:, 8 * n:8 * n + 8, :].rearrange("p a b -> p (a b)").rearrange("p (t e) -> p t e", e=NE)

    route = Route(k, TT, small(k.small), small(k.small, 1), small(k.small, 2), small(k.nm))
    mask = k.sums[:, 0:8, :].rearrange("p a b -> p (a b)").rearrange("p (t e) -> p t e", e=NE)
    with nc.Fori(0, NPAIR) as pair:
        with nc.Block() as block:
            @block.scalar
            def _(act):
                act.wait_ge(k.prod_ready, 2)
                nc.scalar.activation(k.hT[:, 1, :], k.ps[:, 1, :], ACT.Copy).then_inc(k.copied_a, 1)
                route.scalar(k, act)

            @block.tensor
            def _(pe):
                for c in range(KD):
                    for t in range(TT):
                        i = nc.tensor.transpose(k.ps[:, c, t * P:(t + 1) * P], k.h[:, t, c * P:(c + 1) * P], k.ident[:])
                    i.then_inc(k.prod_ready, 1)
                pe.wait_ge(k.copied_v, 1)
                pe.wait_ge(k.copied_a, 1)
                for t in range(TT):
                    for m in range(KD):
                        i = nc.tensor.matmul(k.ps[:, 2, t * NE:(t + 1) * NE], k.hT[:, m, t * P:(t + 1) * P], wg[:, m, :],
                                             start=m == 0, stop=m == KD - 1)
                i.then_inc(k.prod_ready, 1)
                n = 0
                for e in range(0, NE, 2):
                    for t in range(TT):
                        if n >= 5:
                            pe.wait_ge(k.x_done, 2 * (n - 4))
                        for m in range(KD):
                            i = nc.tensor.matmul(k.ps[:, 3 + n % 5, :], k.hT[:, m, t * P:(t + 1) * P],
                                                 wc[:, m, e * D:(e + 2) * D], start=m == 0, stop=m == KD - 1)
                        i.then_inc(k.out_ready, 1)
                        n += 1

            @block.vector
            def _(dve):
                dve.wait_ge(k.prod_ready, 1)
                nc.vector.tensor_copy(k.hT[:, 0, :], k.ps[:, 0, :]).then_inc(k.copied_v, 1)
                dve.wait_ge(k.prod_ready, 3)
                route.vector(k, dve, k.ps[:, 2, 0:TT * NE].rearrange("p (t e) -> p t e", e=NE))
                nc.vector.tensor_scalar(mask, route.rank, 1.5, None, ALU.is_lt).then_inc(k.chain_v, 1)
                for part in range(5):
                    norm_ahead(k, dve, lambda t: k.X[:, (pair + 1) % NPAIR, t, :], part)
                dve.wait_ge(k.chain_v, Route.STEPS + 1)
                n = 0
                for e in range(0, NE, 2):
                    for t in range(TT):
                        dve.wait_ge(k.out_ready, n + 1)
                        for i in range(2):
                            done = 2 * n - 7 if i == 0 else 2 * n + 1
                            if done > 0:
                                dve.wait_ge(k.x_done, done)
                            nc.vector.scalar_tensor_tensor(
                                out=k.X[:, pair, t, :], in0=k.ps[:, 3 + n % 5, i * D:(i + 1) * D],
                                scalar=mask[:, t, e + i:e + i + 1], in1=k.X[:, pair, t, :], op0=ALU.mult,
                                op1=ALU.add).then_inc(k.x_done, 1)
                        n += 1
        k.clear()


def capacity(k, layer, out):
    nc = k.nc
    U32 = mybir.dt.uint32
    NTT = T // P
    xb, yb = k.xb, k.yb
    wr = k.w(layer, "wr", MOE3).rearrange("p (m e) -> p m e", m=KD)
    bias = k.w(layer, "bias", MOE3)
    HB = k.KT[:].rearrange("p c n -> p (c n)").rearrange("p (t d) -> p t d", d=D)
    HP = HB.rearrange("p (g t) d -> p g t d", t=TT)
    flat = k.res[:].rearrange("p t d -> p (t d)")

    def part(n):
        return flat[:, n * NTT * NE:(n + 1) * NTT * NE].rearrange("p (t e) -> p t e", e=NE)

    PR, M1, M2, ALLM, POS, SLOT, TMP, BASE = (part(n) for n in range(8))
    sk = [k.st2[:, n, :] for n in range(2)]
    wk = [k.st2[:, 2 + n, :] for n in range(2)]
    tmp = k.st2[:, 4, :]
    idx = [k.idx[:, n, :] for n in range(4)]
    A0, A1 = k.arena[(layer + 1) % 2], k.arena[layer % 2]
    first = MOE3_WIDTH
    slots = [A0[:, 0:2 * FC * D], A0[:, 2 * FC * D:4 * FC * D], A1[:, first:first + 2 * FC * D],
             k.W[:, 0:4096], k.W[:, 4096:8192], k.W[:, 16384:20480]]
    NSLOT = len(slots)
    zero = k.V[:].rearrange("p c n -> p (c n)")

    with nc.Block() as block:
        @block.vector
        def _(dve):
            nc.vector.memset(zero, 0.0).then_inc(k.zeroed, 1)

        @block.sync
        def _(sp):
            sp.wait_ge(k.zeroed, 1)
            for n in range(2):
                sp.dma_start(xb.rearrange("(p c) d -> p (c d)", p=P)[:, n * 4096:(n + 1) * 4096],
                             zero).then_inc(k.zero_in, 16)
            for e in range(NSLOT):
                sp.dma_start(slots[e], k.dram["moe3"][e]).then_inc(k.expert_in[NE + e], 16)

    LG = POS
    with nc.Fori(0, NPAIR) as pair:
        with nc.Block() as block:

            @block.scalar
            def _(act):
                act.wait_ge(k.prod_ready, 2)
                nc.scalar.activation(k.hT[:, 1, :], k.ps[:, 1, :], ACT.Copy).then_inc(k.copied_a, 1)

            @block.gpsimd
            def _(pool):
                nc.gpsimd.tensor_copy(HP[:, pair, :, :], k.h[:]).then_inc(k.res_ready, 1)
                nc.gpsimd.tensor_tensor(k.X[:, pair, :, :], k.X[:, pair, :, :],
                                        bias.unsqueeze(1).to_broadcast([P, TT, D]), ALU.add).then_inc(k.x_done, 1)

            @block.tensor
            def _(pe):
                for c in range(KD):
                    for t in range(TT):
                        i = nc.tensor.transpose(k.ps[:, c, t * P:(t + 1) * P], k.h[:, t, c * P:(c + 1) * P], k.ident[:])
                    i.then_inc(k.prod_ready, 1)
                pe.wait_ge(k.copied_v, 1)
                pe.wait_ge(k.copied_a, 1)
                for t in range(TT):
                    for m in range(KD):
                        i = nc.tensor.matmul(k.ps[:, 2, t * NE:(t + 1) * NE], k.hT[:, m, t * P:(t + 1) * P], wr[:, m, :],
                                             start=m == 0, stop=m == KD - 1)
                i.then_inc(k.prod_ready, 1)

            @block.vector
            def _(dve):
                dve.wait_ge(k.prod_ready, 1)
                nc.vector.tensor_copy(k.hT[:, 0, :], k.ps[:, 0, :]).then_inc(k.copied_v, 1)
                for part in range(5):
                    if part == 3:
                        dve.wait_ge(k.res_ready, 1)
                        dve.wait_ge(k.prod_ready, 2)
                    norm_ahead(k, dve, lambda t: k.X[:, (pair + 1) % NPAIR, t, :], part)
                dve.wait_ge(k.prod_ready, 3)
                nc.vector.tensor_copy(LG.rearrange("p (g t) e -> p g t e", t=TT)[:, pair, :, :],
                                      k.ps[:, 2, 0:TT * NE].rearrange("p (t e) -> p t e", e=NE)).then_inc(k.chain_v, 1)
        k.clear()

    def one(x):
        return x.rearrange("p t e -> p (t e)")

    route = Route(k, NTT, LG, SLOT, PR, TMP)
    with nc.Block() as block:
        @block.scalar
        def _(act):
            route.scalar(k, act)

        @block.tensor
        def _(pe):
            pe.wait_ge(k.chain_v, Route.STEPS + 3)
            nc.tensor.matmul(k.ps[:, 0, 0:P], k.upper[:], one(ALLM), start=True, stop=True)
            nc.tensor.matmul(k.ps[:, 1, 0:P], k.ones[:], one(ALLM), start=True, stop=True).then_inc(k.prod_ready, 1)

        @block.vector
        def _(dve):
            route.vector(k, dve, LG)
            n = [Route.STEPS]

            def then(i):
                n[0] += 1
                i.then_inc(k.chain_v, 1)
                dve.wait_ge(k.chain_v, n[0])

            then(nc.vector.tensor_scalar(M1, route.rank, 0.0, None, ALU.is_equal))
            then(nc.vector.tensor_scalar(M2, route.rank, 1.0, None, ALU.is_equal))
            then(nc.vector.tensor_tensor(ALLM, M1, M2, ALU.add))
            then(nc.vector.memset(BASE[:, 0, :], 0.0))
            dve.wait_ge(k.prod_ready, 1)
            tot = k.ps[:, 1, 0:P].rearrange("p (t e) -> p t e", e=NE)
            for t in range(1, NTT):
                then(nc.vector.tensor_tensor(BASE[:, t, :], BASE[:, t - 1, :], tot[:, t - 1, :], ALU.add))
            then(nc.vector.tensor_tensor(one(POS), k.ps[:, 0, 0:P], one(BASE), ALU.add))
            then(nc.vector.tensor_scalar(TMP, POS, float(CAP), 4.0 * NE * CAP, ALU.is_ge, ALU.mult))
            then(nc.vector.tensor_tensor(SLOT, POS, TMP, ALU.add))
            then(nc.vector.tensor_tensor(SLOT, SLOT, k.starts[:].unsqueeze(1).to_broadcast([P, NTT, NE]), ALU.add))
            for c, M in enumerate((M1, M2)):
                then(nc.vector.tensor_tensor(TMP, M, SLOT, ALU.mult))
                then(nc.vector.tensor_reduce(sk[c], TMP, AX.X, ALU.add))
                then(nc.vector.tensor_copy(idx[c], sk[c]))
                then(nc.vector.tensor_scalar(tmp, sk[c], NE * CAP - 1.0, None, ALU.min))
                then(nc.vector.tensor_copy(idx[2 + c], tmp))
                then(nc.vector.tensor_tensor(TMP, M, PR, ALU.mult))
                then(nc.vector.tensor_reduce(wk[c], TMP, AX.X, ALU.add))
                then(nc.vector.tensor_scalar(tmp, sk[c], float(NE * CAP), None, ALU.is_lt))
                then(nc.vector.tensor_tensor(wk[c], wk[c], tmp, ALU.mult))
    k.clear()

    xe = [k.Pb[:, n, :, :] for n in range(2)]
    xeT = [k.PT[:, n, :, :] for n in range(2)]
    gT = [k.KT, k.V[:].rearrange("p t (a n) -> p (t a) n", a=2)]
    ysb = [k.h[:], k.cT[:].rearrange("p c (t d) -> p (c t) d", d=D)]
    back = A0[:, 0:2 * NTT * D].rearrange("p (n d) -> p n d", d=D)
    with nc.Block() as block:
        @block.gpsimd
        def _(pool):
            pool.wait_ge(k.zero_in, 32)
            for t in range(NTT):
                for c in range(2):
                    nc.gpsimd.indirect_dma_start(
                        out=xb, out_offset=bass.IndirectOffsetOnAxis(ap=idx[c][:, t:t + 1], axis=0), in_=HB[:, t, :],
                        in_offset=None, bounds_check=NE * CAP - 1, oob_is_err=False).then_inc(k.scattered, 16)
            pool.wait_ge(k.stored, 16 * NE)
            for t in range(NTT):
                for c in range(2):
                    nc.gpsimd.indirect_dma_start(
                        out=back[:, 2 * t + c, :], out_offset=None, in_=yb,
                        in_offset=bass.IndirectOffsetOnAxis(ap=idx[2 + c][:, t:t + 1], axis=0),
                        bounds_check=NE * CAP - 1, oob_is_err=False).then_inc(k.gathered[t], 16)

        @block.sync
        def _(sp):
            sp.wait_ge(k.scattered, 16 * 2 * NTT)
            for e in range(NE):
                if e >= 2:
                    sp.wait_ge(k.prod_ready, KD * (e - 1))
                sp.dma_start(xe[e % 2], xb[e * CAP:(e + 1) * CAP, :].rearrange("(t p) d -> p t d", p=P)
                             ).then_inc(k.rows_in[e % 2], 16)
                if NSLOT <= e + 2 < NE:
                    sp.wait_ge(k.out_ready, 2 * (e + 3 - NSLOT))
                    sp.dma_start(slots[(e + 2) % NSLOT], k.dram["moe3"][e + 2]).then_inc(k.expert_in[NE + e + 2], 16)
                if e >= 1:
                    sp.wait_ge(k.chain_v, 2 * e)
                    sp.dma_start(yb[(e - 1) * CAP:e * CAP, :].rearrange("(t p) d -> p t d", p=P),
                                 ysb[(e - 1) % 2]).then_inc(k.stored, 16)
            sp.wait_ge(k.chain_v, 2 * NE)
            sp.dma_start(yb[(NE - 1) * CAP:NE * CAP, :].rearrange("(t p) d -> p t d", p=P),
                         ysb[(NE - 1) % 2]).then_inc(k.stored, 16)
            for g in range(NPAIR):
                sp.wait_ge(k.x_done, 2 * TT * (g + 1))
                sp.dma_start(out[:, g], k.X[:, g, :, :]).then_inc(k.x_out, 16)
            sp.wait_ge(k.x_out, 16 * NPAIR)

        @block.tensor
        def _(pe):
            for e in range(NE):
                w = slots[e % NSLOT]
                w1 = w[:, 0:KD * F].rearrange("p (m f) -> p m f", m=KD)
                w2 = w[:, KD * F:].rearrange("p (f d) -> p f d", f=FC)
                pe.wait_ge(k.rows_in[e % 2], 16 * (e // 2 + 1))
                if e >= 1:
                    pe.wait_ge(k.copied_v, KD * e)
                for c in range(KD):
                    for t in range(TT):
                        i = nc.tensor.transpose(k.ps[:, c, t * P:(t + 1) * P], xe[e % 2][:, t, c * P:(c + 1) * P],
                                                k.ident[:])
                    i.then_inc(k.prod_ready, 1)
                pe.wait_ge(k.copied_v, KD * (e + 1))
                pe.wait_ge(k.expert_in[NE + e], 16)
                for f in range(FC):
                    n = e * FC + f
                    if n >= 4:
                        pe.wait_ge(k.copied_a, n - 3)
                    for m in range(KD):
                        i = nc.tensor.matmul(k.ps[:, 2 + n % 4, :], w1[:, m, f * P:(f + 1) * P], xeT[e % 2][:, m, :],
                                             start=m == 0, stop=m == KD - 1)
                    i.then_inc(k.scores_ready, 1)
                pe.wait_ge(k.copied_a, FC * (e + 1))
                for b in range(2):
                    if e >= 1:
                        pe.wait_ge(k.chain_v, 2 * e + b - 1)
                    for q in range(2):
                        t = 2 * b + q
                        for f in range(FC):
                            i = nc.tensor.matmul(k.ps[:, 6 + b, q * D:(q + 1) * D], gT[e % 2][:, f, t * P:(t + 1) * P],
                                                 w2[:, f, :], start=f == 0, stop=f == FC - 1)
                    i.then_inc(k.out_ready, 1)

        @block.scalar
        def _(act):
            for e in range(NE):
                if e >= 2:
                    act.wait_ge(k.out_ready, 2 * (e - 1))
                for f in range(FC):
                    n = e * FC + f
                    act.wait_ge(k.scores_ready, n + 1)
                    nc.scalar.activation(gT[e % 2][:, f, :], k.ps[:, 2 + n % 4, :], ACT.Gelu_apprx_tanh
                                         ).then_inc(k.copied_a, 1)

        @block.vector
        def _(dve):
            for e in range(NE):
                for c in range(KD):
                    dve.wait_ge(k.prod_ready, KD * e + c + 1)
                    nc.vector.tensor_copy(xeT[e % 2][:, c, :], k.ps[:, c, :]).then_inc(k.copied_v, 1)
                if e >= 2:
                    dve.wait_ge(k.stored, 16 * (e - 1))
                for b in range(2):
                    dve.wait_ge(k.out_ready, 2 * e + b + 1)
                    nc.vector.tensor_copy(ysb[e % 2][:, 2 * b:2 * b + 2, :],
                                          k.ps[:, 6 + b, :].rearrange("p (q d) -> p q d", q=2)).then_inc(k.chain_v, 1)
            X = k.X[:].rearrange("p g t d -> p (g t) d")
            for t in range(NTT):
                dve.wait_ge(k.gathered[t], 32)
                for c in range(2):
                    if c:
                        dve.wait_ge(k.x_done, 2 * t + 1)
                    nc.vector.scalar_tensor_tensor(out=X[:, t, :], in0=back[:, 2 * t + c, :], scalar=wk[c][:, t:t + 1],
                                                   in1=X[:, t, :], op0=ALU.mult, op1=ALU.add).then_inc(k.x_done, 1)
    k.clear()


OTHER = {2: mixer, 8: composed, 11: capacity}
ORDER = list(range(LAYERS))


def program(nc, dram, out):
    with ExitStack() as ctx:
        k = Core(nc, ctx, dram)
        constants(k)
        for n in ORDER:
            weights(k, n)
            if n in ATTN:
                attention(k, n)
            else:
                OTHER[n](k, n, out)


def _rows(w, r=P):
    c = w.shape[0] // r
    w = w.reshape(c, r, -1).transpose(1, 0, 2).reshape(r, -1)
    full = np.zeros((P, w.shape[1]), np.float32)
    full[0:r] = w
    return full


def _copies(w, L):
    w = w.reshape(-1, L.kvh, 1, L.dh)
    return np.broadcast_to(w, (w.shape[0], L.kvh, L.rep, L.dh)).reshape(w.shape[0], L.inner)


def _cols(b):
    return np.ascontiguousarray(b.reshape(-1, P).T)


def _spread(b):
    return np.broadcast_to(b.reshape(1, -1), (P, b.size))


def _pack_attn(L, a):
    n = L.name + "_"
    parts = []
    if L.normed:
        w, b = a[n + "qkv_w"].T, a[n + "qkv_b"]
        wo = a[n + "out_w"].T.reshape(L.nch, 2, 4, L.dh, D).transpose(0, 2, 1, 3, 4).reshape(D, D)
        parts = [_rows(w[:, 0:2 * D]), _rows(w[:, 2 * D:]), _rows(wo), _spread(b[0:2 * D]),
                 _spread(b[2 * D:]), _spread(a[n + "out_b"]), _cols(a[n + "ln_w"]), _cols(a[n + "ln_b"])]
        return np.concatenate(parts, axis=1)
    if L.name == "L2_attn":
        w, b = a["L2_attn_W_qkv"], a["L2_attn_b_qkv"]
        wq, wk, wv, wo = w[:, 0:D], w[:, D:2 * D], w[:, 2 * D:], a["L2_attn_W_proj"]
        bq, bk, bv, bo = b[0:D], b[D:2 * D], b[2 * D:], a["L2_attn_b_proj"]
    else:
        wq, wk, wv, wo = (a[n + x] for x in ("Wq", "Wk", "Wv", "Wo"))
        if L.name == "L0_xattn":
            wq, wk, wv, wo = wq.T, wk.T, wv.T, wo.T
        if L.qkv_bias:
            bq, bk, bv = (a[n + x] for x in ("bq", "bk", "bv"))
        if L.out_bias:
            bo = a[n + "bo"]
    parts = [_rows(wq), _rows(_copies(wk, L), L.kr),
             _rows(wv, L.kr), _rows(wo)]
    if L.qkv_bias:
        parts += [_cols(bq), _cols(_copies(bk, L)), _spread(bv)]
    if L.out_bias:
        parts += [_spread(bo)]
    if L.selected:
        parts += [_spread(a[n + "Wg"])]
    return np.concatenate(parts, axis=1)


def _layout(a):
    out = {"x": a["x"].reshape(NPAIR, TT, P, D).transpose(2, 0, 1, 3),
           "ctxT": a["ctx_768"].reshape(NPAIR, 2 * S, KD, CR).transpose(0, 3, 2, 1)}
    for n, L in ATTN.items():
        out[f"w{n}"] = _pack_attn(L, a)
    out["w2"] = np.concatenate([_rows(a["L0_ffn_W_r"].T), _rows(a["L0_ffn_W_k"].T), _rows(a["L0_ffn_W_v"].T),
                                _cols(a["L0_ffn_mu_r"]), _cols(a["L0_ffn_mu_k"])], axis=1)
    out["w8"] = _rows(a["L2_ffn_gate_w"].T)
    out["moe2"] = np.stack([np.concatenate([_rows(a["L2_ffn_w_up"][e].T), _rows(a["L2_ffn_w_down"][e])], axis=1)
                            for e in range(NE)])
    out["w11"] = np.concatenate([_rows(a["L3_ffn_w_router"]), _spread(a["L3_ffn_bias"])], axis=1)
    out["moe3"] = np.stack([np.concatenate([_rows(a["L3_ffn_w1"][e]), _rows(a["L3_ffn_w2"][e])], axis=1)
                            for e in range(NE)])
    return {n: np.ascontiguousarray(v) for n, v in out.items()}


def kernel(**inputs):
    import concourse.bacc as bacc
    from concourse.bass_utils import run_bass_kernel_spmd

    arrays = _layout({n: np.asarray(v) for n, v in inputs.items()})
    nc = bacc.Bacc("TRN2", target_bir_lowering=False, num_devices=1)
    dram = {n: nc.dram_tensor(n, v.shape, mybir.dt.from_np(v.dtype), kind="ExternalInput").ap()
            for n, v in arrays.items()}
    out = nc.dram_tensor("out", (P, NPAIR, TT, D), F32, kind="ExternalOutput").ap()
    program(nc, dram, out)
    r = run_bass_kernel_spmd(nc, [arrays], core_ids=[0])
    return np.ascontiguousarray(r.results[0]["out"].transpose(1, 2, 0, 3)).reshape(B, S, D)
```
